# Optimizing a Trainium2 kernel written in Bass

```python
import numpy as np
import jax
import jax.numpy as jnp

def _softmax(x, axis=-1):
    return jax.nn.softmax(x, axis=axis)

def _gelu(x):
    return jax.nn.gelu(x, approximate=True)

def _silu(x):
    return jax.nn.silu(x)

def _sigmoid(x):
    return jax.nn.sigmoid(x)

def _layernorm(x, axis=-1, eps=1e-05):
    m = jnp.mean(x, axis=axis, keepdims=True)
    v = jnp.var(x, axis=axis, keepdims=True)
    return (x - m) / jnp.sqrt(v + eps)

def _scatter_add(tgt, idx, src, axis=0):
    return tgt.at[idx].add(src)

def _segment_sum(src, seg, n):
    return jax.ops.segment_sum(src, seg, n)
kernel_name = 'mk_hybrid_d1_jaxref_r4_32e7fc'

def setup_inputs(seed: int=0):
    np.random.seed(seed)
    _w = jnp.asarray

    def _L0_attn_a_setup():
        import jax, jax.numpy as jnp
        import numpy as np
        B, S, D = (2, 512, 512)
        H, DH = (16, 128)
        key = jax.random.key(seed)
        k1, k2, k3 = jax.random.split(key, 3)
        x = jax.random.normal(k1, (B, S, D), dtype=jnp.float32)
        w_in = jax.random.normal(k2, (3 * H * DH, D), dtype=jnp.float32) * (1.0 / np.sqrt(D))
        w_out = jax.random.normal(k3, (D, H * DH), dtype=jnp.float32) * (1.0 / np.sqrt(H * DH))
        return {'x': x, 'w_in': w_in, 'w_out': w_out}
    _L0_attn_a_in = _L0_attn_a_setup()

    def _L0_attn_b_setup():
        import jax, jax.numpy as jnp
        import numpy as np
        B, S, D = (2, 512, 512)
        H = 16
        Q_LORA, KV_LORA = (384, 128)
        ROPE_DIM, NOPE_DIM, V_DIM = (64, 64, 128)
        Q_HEAD_DIM = NOPE_DIM + ROPE_DIM
        ROPE_THETA, ROPE_RATIO = (10000.0, 1.0)

        def _rope_tables(seq_len):
            half = ROPE_DIM // 2
            inv_freq = ROPE_RATIO / ROPE_THETA ** (jnp.arange(half, dtype=jnp.float32) * 2.0 / ROPE_DIM)
            freqs = jnp.arange(seq_len, dtype=jnp.float32)[:, None] * inv_freq[None, :]
            return (jnp.cos(freqs), jnp.sin(freqs))

        def _apply_rope(x, cos, sin):
            x_even = x[..., 0::2]
            x_odd = x[..., 1::2]
            r_even = x_even * cos - x_odd * sin
            r_odd = x_odd * cos + x_even * sin
            return jnp.stack([r_even, r_odd], axis=-1).reshape(x.shape)
        key = jax.random.key(seed)
        ks = jax.random.split(key, 6)
        std = 0.02
        return {'hidden_states': jax.random.normal(ks[0], (B, S, D), jnp.float32), 'Wqa': jax.random.normal(ks[1], (D, Q_LORA), jnp.float32) * std, 'Wqb': jax.random.normal(ks[2], (Q_LORA, H * Q_HEAD_DIM), jnp.float32) * std, 'Wkva': jax.random.normal(ks[3], (D, KV_LORA + ROPE_DIM), jnp.float32) * std, 'Wkvb': jax.random.normal(ks[4], (KV_LORA, H * (NOPE_DIM + V_DIM)), jnp.float32) * std, 'Wo': jax.random.normal(ks[5], (H * V_DIM, D), jnp.float32) * std}
    _L0_attn_b_in = _L0_attn_b_setup()

    def _L0_ffn_setup():
        import jax, jax.numpy as jnp
        import numpy as np
        K = 2

        def gelu(v):
            return jax.nn.gelu(v, approximate=False)
        key = jax.random.key(seed)
        ks = jax.random.split(key, 10)
        B, S, D, H, E = (4, 512, 512, 256, 8)
        SH = 2 * H
        u = lambda k_, shape, b: jax.random.uniform(k_, shape, jnp.float32, -b, b)
        return {'x': jax.random.normal(ks[0], (B, S, D), jnp.float32), 'gate_w': u(ks[1], (D, E), 1.0 / D), 'w1': u(ks[2], (E, D, H), 1.0 / D), 'b1': u(ks[3], (E, H), 1.0 / np.sqrt(D)), 'w2': u(ks[4], (E, H, D), 1.0 / H), 'b2': u(ks[5], (E, D), 1.0 / np.sqrt(H)), 'shared_w1': u(ks[6], (D, SH), 1.0 / D), 'shared_b1': u(ks[7], (SH,), 1.0 / np.sqrt(D)), 'shared_w2': u(ks[8], (SH, D), 1.0 / SH), 'shared_b2': u(ks[9], (D,), 1.0 / np.sqrt(SH))}
    _L0_ffn_in = _L0_ffn_setup()
    _d = {'L0_attn_a_x': _L0_attn_a_in['x'], 'L0_attn_a_w_in': _L0_attn_a_in['w_in'], 'L0_attn_a_w_out': _L0_attn_a_in['w_out'], 'L0_attn_b_Wqa': _L0_attn_b_in['Wqa'], 'L0_attn_b_Wqb': _L0_attn_b_in['Wqb'], 'L0_attn_b_Wkva': _L0_attn_b_in['Wkva'], 'L0_attn_b_Wkvb': _L0_attn_b_in['Wkvb'], 'L0_attn_b_Wo': _L0_attn_b_in['Wo'], 'L0_ffn_gate_w': _L0_ffn_in['gate_w'], 'L0_ffn_w1': _L0_ffn_in['w1'], 'L0_ffn_b1': _L0_ffn_in['b1'], 'L0_ffn_w2': _L0_ffn_in['w2'], 'L0_ffn_b2': _L0_ffn_in['b2'], 'L0_ffn_shared_w1': _L0_ffn_in['shared_w1'], 'L0_ffn_shared_b1': _L0_ffn_in['shared_b1'], 'L0_ffn_shared_w2': _L0_ffn_in['shared_w2'], 'L0_ffn_shared_b2': _L0_ffn_in['shared_b2']}
    _x0 = _d['L0_attn_a_x']
    _d['L0_attn_a_x'] = jax.random.normal(jax.random.fold_in(jax.random.key(seed), 1), (4, 512, 512), dtype=_x0.dtype)
    del _x0
    return _d

def reference(L0_attn_a_x, L0_attn_a_w_in, L0_attn_a_w_out, L0_attn_b_Wqa, L0_attn_b_Wqb, L0_attn_b_Wkva, L0_attn_b_Wkvb, L0_attn_b_Wo, L0_ffn_gate_w, L0_ffn_w1, L0_ffn_b1, L0_ffn_w2, L0_ffn_b2, L0_ffn_shared_w1, L0_ffn_shared_b1, L0_ffn_shared_w2, L0_ffn_shared_b2):

    def _L0_attn_a_ref(x, w_in, w_out):
        import jax, jax.numpy as jnp
        import numpy as np
        B, S, D = (2, 512, 512)
        H, DH = (16, 128)
        b, s, _ = x.shape
        projected = jnp.einsum('bsd,ed->bse', x, w_in)
        projected = projected.reshape(b, s, H, 3 * DH)
        q, k, v = jnp.split(projected, 3, axis=-1)
        scores = jnp.einsum('bqhd,bkhd->bhqk', q, k) * (1.0 / np.sqrt(DH))
        causal_mask = jnp.tril(jnp.ones((s, s), dtype=bool))
        scores = jnp.where(causal_mask, scores, jnp.float32(-jnp.inf))
        attn = jax.nn.softmax(scores, axis=-1)
        out = jnp.einsum('bhqk,bkhd->bqhd', attn, v)
        out = out.reshape(b, s, H * DH)
        return jnp.einsum('bse,de->bsd', out, w_out)

    def _L0_attn_b_ref(hidden_states, Wqa, Wqb, Wkva, Wkvb, Wo):
        import jax, jax.numpy as jnp
        import numpy as np
        B, S, D = (2, 512, 512)
        H = 16
        Q_LORA, KV_LORA = (384, 128)
        ROPE_DIM, NOPE_DIM, V_DIM = (64, 64, 128)
        Q_HEAD_DIM = NOPE_DIM + ROPE_DIM
        ROPE_THETA, ROPE_RATIO = (10000.0, 1.0)

        def _rope_tables(seq_len):
            half = ROPE_DIM // 2
            inv_freq = ROPE_RATIO / ROPE_THETA ** (jnp.arange(half, dtype=jnp.float32) * 2.0 / ROPE_DIM)
            freqs = jnp.arange(seq_len, dtype=jnp.float32)[:, None] * inv_freq[None, :]
            return (jnp.cos(freqs), jnp.sin(freqs))

        def _apply_rope(x, cos, sin):
            x_even = x[..., 0::2]
            x_odd = x[..., 1::2]
            r_even = x_even * cos - x_odd * sin
            r_odd = x_odd * cos + x_even * sin
            return jnp.stack([r_even, r_odd], axis=-1).reshape(x.shape)
        b, s, _ = hidden_states.shape
        scale = Q_HEAD_DIM ** (-0.5)
        q_latent = hidden_states @ Wqa
        q = (q_latent @ Wqb).reshape(b, s, H, Q_HEAD_DIM)
        q = jnp.transpose(q, (0, 2, 1, 3))
        q_nope, q_pe = (q[..., :NOPE_DIM], q[..., NOPE_DIM:])
        kv_comp = hidden_states @ Wkva
        c_kv, k_pe = (kv_comp[..., :KV_LORA], kv_comp[..., KV_LORA:])
        cos, sin = _rope_tables(s)
        q_pe = _apply_rope(q_pe, cos, sin)
        k_pe = _apply_rope(k_pe, cos, sin)
        kv = (c_kv @ Wkvb).reshape(b, s, H, NOPE_DIM + V_DIM)
        kv = jnp.transpose(kv, (0, 2, 1, 3))
        k_nope, v = (kv[..., :NOPE_DIM], kv[..., NOPE_DIM:])
        k_pe_b = jnp.broadcast_to(k_pe[:, None], (b, H, s, ROPE_DIM))
        q_full = jnp.concatenate([q_nope, q_pe], axis=-1)
        k_full = jnp.concatenate([k_nope, k_pe_b], axis=-1)
        scores = jnp.einsum('bhqd,bhkd->bhqk', q_full, k_full) * scale
        causal = jnp.tril(jnp.ones((s, s), dtype=bool))
        scores = jnp.where(causal[None, None], scores, jnp.finfo(scores.dtype).min)
        probs = jax.nn.softmax(scores, axis=-1)
        attn = jnp.einsum('bhqk,bhkd->bhqd', probs, v)
        out = jnp.transpose(attn, (0, 2, 1, 3)).reshape(b, s, H * V_DIM)
        return out @ Wo

    def _L0_ffn_ref(x, gate_w, w1, b1, w2, b2, shared_w1, shared_b1, shared_w2, shared_b2):
        import jax, jax.numpy as jnp
        import numpy as np
        K = 2

        def gelu(v):
            return jax.nn.gelu(v, approximate=False)
        B, S, D = x.shape
        E = gate_w.shape[1]
        xf = x.reshape(-1, D)
        logits = xf @ gate_w
        top_logits, top_idx = jax.lax.top_k(logits, K)
        top_gates = jax.nn.softmax(top_logits, axis=-1)
        gates = jnp.sum(jax.nn.one_hot(top_idx, E, dtype=xf.dtype) * top_gates[..., None], axis=1)
        h = gelu(jnp.einsum('nd,edh->neh', xf, w1) + b1)
        out_e = jnp.einsum('neh,ehd->ned', h, w2) + b2
        routed = jnp.einsum('ne,ned->nd', gates, out_e)
        shared = gelu(xf @ shared_w1 + shared_b1) @ shared_w2 + shared_b2
        return (routed + shared).reshape(B, S, D)
    x = L0_attn_a_x
    x = x + _L0_attn_a_ref(_layernorm(x, axis=-1), L0_attn_a_w_in, L0_attn_a_w_out)
    x = x + _L0_ffn_ref(_layernorm(x, axis=-1), L0_ffn_gate_w, L0_ffn_w1, L0_ffn_b1, L0_ffn_w2, L0_ffn_b2, L0_ffn_shared_w1, L0_ffn_shared_b1, L0_ffn_shared_w2, L0_ffn_shared_b2)
    x = x + _L0_attn_b_ref(_layernorm(x, axis=-1), L0_attn_b_Wqa, L0_attn_b_Wqb, L0_attn_b_Wkva, L0_attn_b_Wkvb, L0_attn_b_Wo)
    x = x + _L0_ffn_ref(_layernorm(x, axis=-1), L0_ffn_gate_w, L0_ffn_w1, L0_ffn_b1, L0_ffn_w2, L0_ffn_b2, L0_ffn_shared_w1, L0_ffn_shared_b1, L0_ffn_shared_w2, L0_ffn_shared_b2)
    return x

_drawn_inputs = setup_inputs


def setup_inputs(seed=0):
    import zlib

    import numpy as np

    out = dict(_drawn_inputs(seed))
    spreads = {}
    factors = {'L0_attn_b_Wqa': 8.0,
     'L0_attn_b_Wqb': 8.0,
     'L0_attn_b_Wkva': 3.727,
     'L0_attn_b_Wkvb': 3.785,
     'L0_attn_b_Wo': 3.716,
     'L0_ffn_w1': 8.0,
     'L0_ffn_b1': 8.0,
     'L0_ffn_w2': 8.0,
     'L0_ffn_shared_w1': 8.0,
     'L0_ffn_shared_b1': 8.0,
     'L0_ffn_shared_w2': 8.0}
    for name, (base, spread) in spreads.items():
        noise = np.random.default_rng([zlib.crc32(name.encode()), seed]).standard_normal(out[name].shape)
        drawn = base * np.exp(spread * noise) if base else spread * noise
        out[name] = jnp.asarray(drawn.astype(out[name].dtype))
    for name, factor in factors.items():
        out[name] = (out[name] * factor).astype(out[name].dtype)
    return out
```

```python
from contextlib import ExitStack

import numpy as np
import concourse.bass as bass
from concourse import mybir

F32 = mybir.dt.float32
F32R = mybir.dt.float32r
ALU = mybir.AluOpType
ACT = mybir.ActivationFunctionType
AX = mybir.AxisListType

P = 128
D = 512
KD = D // P
B = 4
S = 512
NT = S // P
H = 16
DH = 128
HALF = 64
QUARTER = 32
KQ = 3
E = 8
NE = E + 2
HF = 256
KH = HF // P
SCALE = float(DH) ** -0.5
EPS = 1e-5
BIG = 1.0e30
FLT_MAX = 3.0e38
HI, LO = 0, 1

PT_AT = [0, 512, 1152, 1024]
PT_MOV = [(0, 0, 512), (512, 128, 384), (1152, 256, 256), (896, 256, 256)]
PT_ZERO = 896
PT_COLS = 1408
S_AT = [0, 128, 384, 768]
S_COLS = 1280


def product(nc, out, hi, lo, mov_hi, mov_lo, first, last):
    nc.tensor.matmul(out, hi, mov_hi, start=first, stop=False)
    nc.tensor.matmul(out, hi, mov_lo, start=False, stop=False)
    return nc.tensor.matmul(out, lo, mov_hi, start=False, stop=last)



def constants(nc, pool, m):
    nc.gpsimd.memset(m.ident[:, :], 0.0).then_inc(m.const_set, 1)
    nc.gpsimd.memset(m.mask[:, :], 0.0).then_inc(m.const_set, 1)
    nc.gpsimd.memset(m.pt_hi[:, PT_ZERO:PT_ZERO + P].bitcast(F32), 0.0).then_inc(m.const_set, 1)
    nc.gpsimd.memset(m.pt_lo[:, PT_ZERO:PT_ZERO + P].bitcast(F32), 0.0).then_inc(m.const_set, 1)
    for e in range(E):
        nc.gpsimd.memset(m.ramp[:, :, e:e + 1], float(E - e)).then_inc(m.const_set, 1)
    nc.gpsimd.memset(m.gates[:, :, E:NE], 1.0).then_inc(m.const_set, 1)
    pool.wait_ge(m.const_set, 2)
    nc.gpsimd.affine_select(out=m.ident[:, :], in_=m.ident[:, :], compare_op=ALU.not_equal, fill=1.0,
                            base=0, pattern=[[-1, P]], channel_multiplier=1).then_inc(m.const_set, 1)
    tri = m.mask[:, S - P:S]
    nc.gpsimd.affine_select(out=tri, in_=tri, compare_op=ALU.is_ge, fill=-BIG,
                            base=0, pattern=[[-1, P]], channel_multiplier=1).then_inc(m.const_set, 1)


CONSTS = 4 + E + 1 + 2



def norm_vector(nc, dve, m, n, r, start):
    for b in range(B):
        start(dve, b)
        c = B * r + b
        for t in range(NT):
            nc.vector.bn_stats(m.stats[:, t, :], m.x[:, b * NT + t, :]).then_inc(n.stats_done, 1)
        for t in range(NT):
            dve.wait_ge(n.stats_done, c * NT + t + 1)
            nc.vector.bn_aggr(m.moments[:, t, :], m.stats[:, t, :]).then_inc(n.moments_done, 1)
        dve.wait_ge(n.moments_done, NT * (c + 1))
        nc.vector.tensor_scalar_add(m.var[:, :], m.moments[:, :, 1], EPS).then_inc(n.var_done, 1)
        dve.wait_ge(n.root_done, c + 1)
        nc.vector.reciprocal(m.rstd0[:, :], m.root[:, :]).then_inc(n.newton, 1)
        dve.wait_ge(n.newton, 5 * c + 1)
        nc.vector.tensor_tensor(m.newt[:, 0, :], m.rstd0[:, :], m.rstd0[:, :], ALU.mult).then_inc(n.newton, 1)
        dve.wait_ge(n.newton, 5 * c + 2)
        nc.vector.tensor_tensor(m.newt[:, 1, :], m.newt[:, 0, :], m.var[:, :], ALU.mult).then_inc(n.newton, 1)
        dve.wait_ge(n.newton, 5 * c + 3)
        nc.vector.tensor_scalar(m.newt[:, 2, :], m.newt[:, 1, :], -0.5, 1.5, ALU.mult, ALU.add).then_inc(n.newton, 1)
        dve.wait_ge(n.newton, 5 * c + 4)
        nc.vector.tensor_tensor(m.rstd[:, :], m.rstd0[:, :], m.newt[:, 2, :], ALU.mult).then_inc(n.newton, 1)
        dve.wait_ge(n.newton, 5 * c + 5)

        def normalise(t):
            i = b * NT + t
            if c * NT + t >= 2:
                dve.wait_ge(n.turned, c * NT + t - 1)
            nc.vector.tensor_scalar(m.xn[:, t % 2, :], m.x[:, i, :], m.moments[:, t, 0:1],
                                    m.rstd[:, t:t + 1], ALU.subtract, ALU.mult).then_inc(n.normed, 1)

        normalise(0)
        for t in range(NT):
            if t + 1 < NT:
                normalise(t + 1)
            i = b * NT + t
            dve.wait_ge(n.xt_hi, c * NT + t + 1)
            at = (slice(None), b, slice(None), slice(t * P, t * P + P))
            nc.vector.tensor_tensor(m.xT[LO][at], m.bank[6 + i % 2][:, :].rearrange("p (k n) -> p k n", k=KD),
                                    m.xT[HI][at].bitcast(F32), ALU.subtract).then_inc(n.xt_lo, 1)


def norm_scalar(nc, act, m, n, r):
    for b in range(B):
        act.wait_ge(n.var_done, B * r + b + 1)
        nc.scalar.activation(m.root[:, :], m.var[:, :], ACT.Sqrt).then_inc(n.root_done, 1)
        for t in range(NT):
            i = b * NT + t
            act.wait_ge(n.turned, B * NT * r + i + 1)
            nc.scalar.activation(m.xT[HI][:, b, :, t * P:t * P + P],
                                 m.bank[6 + i % 2][:, :].rearrange("p (k n) -> p k n", k=KD),
                                 ACT.Copy).then_inc(n.xt_hi, 1)


def norm_tensor(nc, pe, m, n, r):
    for i in range(B * NT):
        done = B * NT * r + i
        pe.wait_ge(n.normed, done + 1)
        if done >= 2:
            pe.wait_ge(n.xt_lo, done - 1)
        for k in range(KD):
            last = nc.tensor.transpose(m.bank[6 + i % 2][:, k * P:k * P + P],
                                       m.xn[:, i % 2, k * P:k * P + P], m.ident[:, :])
        last.then_inc(n.turned, 1)
    pe.wait_ge(n.xt_lo, B * NT * (r + 1))



def scores_of(m, t):
    n = max(256, (t + 1) * P)
    return m.bank[max(t - 1, 0)][:, (256 if t == 1 else 0):(256 if t == 1 else 0) + n], n


def attend_tensor(nc, pe, m, a, mla):
    parts = 2 if mla else 3

    def keys(b):
        return (m.xT[HI][:, b, KQ, :], m.xT[LO][:, b, KQ, :]) if mla else (m.k[HI][:, :], m.k[LO][:, :])

    def scores(u, b):
        pe.wait_ge(a.q_lo, u + 1)
        pe.wait_ge(a.k_lo, u + 1)
        k_hi, k_lo = keys(b)
        for t in range(NT):
            out, n = scores_of(m, t)
            at = slice(t * P, t * P + P)
            product(nc, out, m.q[HI][:, at], m.q[LO][:, at], k_hi[:, 0:n], k_lo[:, 0:n],
                    True, True).then_inc(a.scores_done, 1)

    def turn(u):
        pe.wait_ge(a.probs_ready, NT * (u + 1))
        for group in ((0,), (1,), (3, 2)):
            col = 0
            for j in group:
                for t in range(j, NT):
                    last = nc.tensor.transpose(m.bank[min(j, 2)][:, col:col + P],
                                               m.s[:, S_AT[t] + j * P:S_AT[t] + j * P + P], m.ident[:, :])
                    col += P
            last.then_inc(a.pt_done, 1)

    def times_v(u):
        pe.wait_ge(a.pt_lo, 3 * (u + 1))
        pe.wait_ge(a.v_lo, u + 1)
        for j in range(NT):
            src, q0, n = PT_MOV[j]
            at = slice(j * DH, j * DH + DH)
            last = product(nc, m.bank[5][:, q0:q0 + n], m.v[HI][:, at], m.v[LO][:, at],
                           m.pt_hi[:, src:src + n], m.pt_lo[:, src:src + n], j == 0, j == NT - 1)
        last.then_inc(a.av_done, 1)

    def output(v, slot, tiles):
        if tiles[0] == 0:
            pe.wait_ge(a.o_lo, v + 1)
        for t in tiles:
            ge(pe, a.y_added, NT * v + t - 1)
            at = slice(t * P, t * P + P)
            product(nc, m.bank[6 + t % 2][:, :], m.o[HI][:, at], m.o[LO][:, at],
                    m.wo[HI][:, slot, :], m.wo[LO][:, slot, :], True, True).then_inc(a.y_done, 1)

    def project_q(s, h, b):
        if b == 0:
            pe.wait_ge(a.w_lo, parts * h + 1)
        ge(pe, a.v_lo if mla else a.vt_copied, s)
        kn = KQ if mla else KD
        for k in range(kn):
            at = slice(k * DH, k * DH + DH)
            last = product(nc, m.bank[3][:, :], m.w[HI][:, at], m.w[LO][:, at],
                           m.xT[HI][:, b, k, :], m.xT[LO][:, b, k, :], k == 0, k == kn - 1)
        last.then_inc(a.proj_done, 1)

    def project_k(s, h, b):
        if b == 0:
            pe.wait_ge(a.w_lo, parts * h + 2)
        ge(pe, a.k_lo if mla else a.v_lo, s)
        if mla:
            last = product(nc, m.bank[4][0:HALF, :], m.w[HI][:, 512:512 + HALF], m.w[LO][:, 512:512 + HALF],
                           m.ckv[HI][:, b, :], m.ckv[LO][:, b, :], True, True)
        else:
            for k in range(KD):
                at = slice(512 + k * DH, 512 + k * DH + DH)
                last = product(nc, m.bank[4][:, :], m.w[HI][:, at], m.w[LO][:, at],
                               m.xT[HI][:, b, k, :], m.xT[LO][:, b, k, :], k == 0, k == KD - 1)
        last.then_inc(a.proj_done, 1)

    def project_v(s, h, b):
        if mla:
            if b == 0:
                pe.wait_ge(a.wv_copied, h + 1)
            pe.wait_ge(a.nope_out, s + 1)
            pe.wait_ge(a.rope_out, s + 1)
            for t in range(NT):
                last = nc.tensor.matmul(m.bank[3][:, t * DH:t * DH + DH], m.ckv32[:, b, t * P:t * P + P],
                                        m.wv32[:, :], start=True, stop=True)
        else:
            if b == 0:
                pe.wait_ge(a.w_lo, parts * h + 3)
            pe.wait_ge(a.q_lo, s + 1)
            for k in range(KD):
                at = slice(1024 + k * DH, 1024 + k * DH + DH)
                last = product(nc, m.bank[3][:, :], m.w[HI][:, at], m.w[LO][:, at],
                               m.xT[HI][:, b, k, :], m.xT[LO][:, b, k, :], k == 0, k == KD - 1)
        last.then_inc(a.proj_done, 1)

    def turn_v(s):
        pe.wait_ge(a.vt_copied, s + 1)
        pe.wait_ge(a.k_lo, s + 1)
        for t in range(NT):
            last = nc.tensor.transpose(m.bank[4][:, t * DH:t * DH + DH], m.vt[:, t * P:t * P + P], m.ident[:, :])
        last.then_inc(a.v_turned, 1)

    def step(h, b, n1, n2, new=True):
        s = 4 * h + b
        u, v = s - 1, s - 2
        bu, slot = (b - 1) % B, (h if b >= 2 else h - 1) % 2
        if n1:
            scores(u, bu)
        if n2:
            if b == 2:
                pe.wait_ge(a.wo_lo, h + 1)
            output(v, slot, (0, 1))
        if new:
            project_q(s, h, b)
        if n1:
            turn(u)
        if new:
            project_k(s, h, b)
            project_v(s, h, b)
        if n1:
            times_v(u)
        if n2:
            output(v, slot, (2, 3))
        if new and not mla:
            turn_v(s)

    for b in range(B):
        step(0, b, b >= 1, b >= 2)
    with pe.Fori(1, H) as h:
        for b in range(B):
            step(h, b, True, True)
    step(H, 0, True, True, new=False)
    step(H, 1, False, True, new=False)


def attend_scalar(nc, act, m, a, mla):
    def split_w(h, part, wait=True):
        act.wait_ge(a.w_loaded, 16 * h + 16)
        if wait:
            act.wait_ge(a.proj_done, 12 * h)
        if mla:
            if part == 2:
                nc.scalar.activation(m.wv32[:, :], m.w_raw[:, 448:576], ACT.Copy).then_inc(a.wv_copied, 1)
                return
            src, dst = ((0, 384), (384, 448))[part], ((0, 384), (512, 576))[part]
        else:
            src = dst = (512 * part, 512 * part + 512)
        nc.scalar.activation(m.w[HI][:, dst[0]:dst[1]], m.w_raw[:, src[0]:src[1]], ACT.Copy).then_inc(a.w_hi, 1)

    def split_last(h, wait=True):
        act.wait_ge(a.wo_loaded, 16 * h + 16)
        if wait:
            act.wait_ge(a.y_done, 16 * h - 8)
        split_w(h, 2, wait)
        nc.scalar.activation(m.wo[HI][:, one(h % 2), :], m.wo_raw[:, 0:D].rearrange("p (a n) -> p a n", a=1), ACT.Copy).then_inc(a.wo_hi, 1)

    def exps(u, b):
        for t in range(NT):
            act.wait_ge(a.masked, NT * u + t + 1)
            at = m.s[:, S_AT[t]:S_AT[t] + (t + 1) * P]
            nc.scalar.activation(at, at, ACT.Exp, bias=m.top[:, b, t:t + 1], scale=-1.0,
                                 accum_out=m.rowsum[:, b, t:t + 1]).then_inc(a.probs_ready, 1)

    def probs_hi(u):
        for g, (dst, n, src) in enumerate(((0, 512, 0), (512, 384, 1), (1024, 384, 2))):
            act.wait_ge(a.pt_done, 3 * u + g + 1)
            nc.scalar.activation(m.pt_hi[:, dst:dst + n], m.bank[src][:, 0:n], ACT.Copy).then_inc(a.pt_hi, 1)

    def step(h, b, n1, new=True):
        s = 4 * h + b
        u, bu = s - 1, (b - 1) % B
        fresh = new and b == 0
        later = n1
        if fresh:
            split_w(h, 0, later)
        if n1:
            exps(u, bu)
        if fresh:
            split_w(h, 1, later)
            split_last(h, later)
        if new:
            act.wait_ge(a.proj_done, 3 * s + 1)
            if mla:
                nc.scalar.activation(m.qf[0:HALF, :], m.bank[3][0:HALF, :], ACT.Copy).then_inc(a.nope_out, 1)
            else:
                nc.scalar.activation(m.q[HI][:, :], m.bank[3][:, :], ACT.Copy).then_inc(a.q_hi, 1)
        if n1:
            probs_hi(u)
        if new:
            act.wait_ge(a.proj_done, 3 * s + 2)
            if mla:
                nc.scalar.activation(m.xT[HI][0:HALF, b, KQ, :], m.bank[4][0:HALF, :], ACT.Copy).then_inc(a.k_hi, 1)
                act.wait_ge(a.nope_out, s + 1)
                act.wait_ge(a.rope_added, s + 1)
                nc.scalar.activation(m.q[HI][:, :], m.qf[:, :], ACT.Copy).then_inc(a.q_hi, 1)
            else:
                nc.scalar.activation(m.k[HI][:, :], m.bank[4][:, :], ACT.Copy).then_inc(a.k_hi, 1)
                act.wait_ge(a.proj_done, 3 * s + 3)
                nc.scalar.activation(m.vt[:, :], m.bank[3][:, :], ACT.Copy).then_inc(a.vt_copied, 1)
        if new and mla:
            act.wait_ge(a.proj_done, 3 * s + 3)
            ge(act, a.av_done, s)
            nc.scalar.activation(m.v[HI][:, :], m.bank[3][:, :], ACT.Copy).then_inc(a.v_hi, 1)
        if n1:
            act.wait_ge(a.av_done, u + 1)
            ge(act, a.y_done, 4 * u)
            nc.scalar.activation(m.o[HI][:, :], m.bank[5][:, :], ACT.Copy).then_inc(a.o_hi, 1)
        if new and not mla:
            act.wait_ge(a.v_turned, s + 1)
            nc.scalar.activation(m.v[HI][:, :], m.bank[4][:, :], ACT.Copy).then_inc(a.v_hi, 1)

    for b in range(B):
        step(0, b, b >= 1)
    with act.Fori(1, H) as h:
        for b in range(B):
            step(h, b, True)
    step(H, 0, True, new=False)


def attend_vector(nc, dve, m, a, mla):
    def mask_and_max(u, b):
        for t in range(NT):
            out, _ = scores_of(m, t)
            n = (t + 1) * P
            nc.vector.tensor_tensor_reduce(
                out=m.s[:, S_AT[t]:S_AT[t] + n], in0=out[:, 0:n], in1=m.mask[:, S - n:S], scale=-SCALE,
                scalar=FLT_MAX, op0=ALU.add, op1=ALU.min, accum_out=m.top[:, b, t:t + 1]).then_inc(a.masked, 1)

    def add_output(v, b, tiles):
        for t in tiles:
            dve.wait_ge(a.y_done, NT * v + t + 1)
            xt = m.x[:, b * NT + t, :]
            nc.vector.scalar_tensor_tensor(out=xt, in0=m.bank[6 + t % 2][:, :], scalar=m.inv[:, b, t:t + 1],
                                           in1=xt, op0=ALU.mult, op1=ALU.add).then_inc(a.y_added, 1)

    def probs_lo(u):
        for g, (dst, n, src) in enumerate(((0, 512, 0), (512, 384, 1), (1024, 384, 2))):
            dve.wait_ge(a.pt_hi, 3 * u + g + 1)
            nc.vector.tensor_tensor(m.pt_lo[:, dst:dst + n], m.bank[src][:, 0:n],
                                    m.pt_hi[:, dst:dst + n].bitcast(F32), ALU.subtract).then_inc(a.pt_lo, 1)

    def rest(out, bank, hi, done):
        return nc.vector.tensor_tensor(out, bank, hi.bitcast(F32), ALU.subtract).then_inc(done, 1)

    def step(h, b, n1, n2, new=True):
        s = 4 * h + b
        u, v, bu, bv = s - 1, s - 2, (b - 1) % B, (b - 2) % B
        if n1:
            dve.wait_ge(a.scores_done, NT * (u + 1))
        if n2:
            nc.vector.reciprocal(m.inv[:, bv, :], m.rowsum[:, bv, :]).then_inc(a.inverted, 1)
        if n1:
            mask_and_max(u, bu)
        if n2:
            dve.wait_ge(a.inverted, v + 1)
            add_output(v, bv, (0, 1))
        if new:
            if mla:
                dve.wait_ge(a.proj_done, 3 * s + 1)
                rotate(nc, m, m.bank[3]).then_inc(a.rope_out, 1)
            else:
                dve.wait_ge(a.q_hi, s + 1)
                rest(m.q[LO][:, :], m.bank[3][:, :], m.q[HI][:, :], a.q_lo)
        if n1:
            probs_lo(u)
        if new:
            dve.wait_ge(a.k_hi, s + 1)
            if mla:
                rest(m.xT[LO][0:HALF, b, KQ, :], m.bank[4][0:HALF, :], m.xT[HI][0:HALF, b, KQ, :], a.k_lo)
                dve.wait_ge(a.v_hi, s + 1)
                rest(m.v[LO][:, :], m.bank[3][:, :], m.v[HI][:, :], a.v_lo)
            else:
                rest(m.k[LO][:, :], m.bank[4][:, :], m.k[HI][:, :], a.k_lo)
        if n2:
            add_output(v, bv, (2, 3))
        if n1:
            dve.wait_ge(a.o_hi, u + 1)
            rest(m.o[LO][:, :], m.bank[5][:, :], m.o[HI][:, :], a.o_lo)
        if new and not mla:
            dve.wait_ge(a.v_hi, s + 1)
            rest(m.v[LO][:, :], m.bank[4][:, :], m.v[HI][:, :], a.v_lo)

    for b in range(B):
        step(0, b, b >= 1, b >= 2)
    with dve.Fori(1, H) as h:
        for b in range(B):
            step(h, b, True, True)
    step(H, 0, True, True, new=False)
    step(H, 1, False, True, new=False)


def attend_gpsimd(nc, pool, m, a, mla):
    parts = 2 if mla else 3

    def rest_w(h, part):
        pool.wait_ge(a.w_hi, parts * h + part + 1)
        if mla:
            src, dst = ((0, 384), (384, 448))[part], ((0, 384), (512, 576))[part]
        else:
            src = dst = (512 * part, 512 * part + 512)
        at = slice(dst[0], dst[1])
        nc.gpsimd.tensor_tensor(m.w[LO][:, at], m.w_raw[:, src[0]:src[1]], m.w[HI][:, at].bitcast(F32),
                                ALU.subtract).then_inc(a.w_lo, 1)

    def rest_wo(h):
        pool.wait_ge(a.wo_hi, h + 1)
        at = one(h % 2)
        nc.gpsimd.tensor_tensor(m.wo[LO][:, at, :], m.wo_raw[:, 0:D].rearrange("p (a n) -> p a n", a=1),
                                m.wo[HI][:, at, :].bitcast(F32), ALU.subtract).then_inc(a.wo_lo, 1)

    def head(h):
        for b in range(B):
            s = 4 * h + b
            if b == 0:
                rest_w(h, 0)
                rest_w(h, 1)
                if not mla:
                    rest_w(h, 2)
                    rest_wo(h)
            if mla:
                pool.wait_ge(a.rope_out, s + 1)
                ge(pool, a.q_lo, s)
                if b == 0:
                    pool.wait_ge(a.w_lo, parts * (h + 1))
                if b == 1:
                    pool.wait_ge(a.wo_lo, h + 1)
                nc.gpsimd.tensor_tensor(m.qf[HALF:P, :], m.ra[HALF:P, :], m.rb[HALF:P, :],
                                        ALU.add).then_inc(a.rope_added, 1)
                pool.wait_ge(a.q_hi, s + 1)
                nc.gpsimd.tensor_tensor(m.q[LO][:, :], m.qf[:, :], m.q[HI][:, :].bitcast(F32),
                                        ALU.subtract).then_inc(a.q_lo, 1)
                if b == 0:
                    rest_wo(h)

    head(0)
    with pool.Fori(1, H) as h:
        head(h)


def attend_sync(nc, sp, m, a, mla, w_dram, wo_dram):
    def head(h, first):
        if not first:
            sp.wait_ge(a.w_lo, (2 if mla else 3) * h)
            if mla:
                sp.wait_ge(a.wv_copied, h)
            sp.wait_ge(a.wo_lo, h)
        sp.dma_start(m.w_raw[:, 0:w_dram.shape[2]], w_dram[one(h), :, :].rearrange("h p n -> p (h n)")).then_inc(a.w_loaded, 16)
        sp.dma_start(m.wo_raw[:, 0:D], wo_dram[one(h), :, :].rearrange("h p n -> p (h n)")).then_inc(a.wo_loaded, 16)

    head(0, True)
    with sp.Fori(1, H) as h:
        head(h, False)


def one(i):
    return slice(i, i + 1) if isinstance(i, int) else bass.ds(i, 1)


def ge(eng, sem, value):
    if not isinstance(value, int) or value > 0:
        eng.wait_ge(sem, value)


def rotate(nc, m, bank):
    e, o = HALF, HALF + QUARTER
    nc.vector.tensor_tensor(m.ra[e:P, :], bank[e:P, :], m.rope[e:P, 0, :], ALU.mult)
    nc.vector.tensor_tensor(m.rb[e:o, :], bank[o:P, :], m.rope[o:P, 1, :], ALU.mult)
    return nc.vector.tensor_tensor(m.rb[o:P, :], bank[e:o, :], m.rope[e:o, 1, :], ALU.mult)



def latent_tensor(nc, pe, m, l):
    pe.wait_ge(l.w_lo, 2)
    for b in range(B):
        for c in range(KQ + 2):
            if b:
                if c <= KQ:
                    pe.wait_ge(l.lo, (KQ + 1) * (b - 1) + c + 1)
                else:
                    pe.wait_ge(l.rope_out, b)
            for k in range(KD):
                at = slice(k * 384 + c * P, k * 384 + c * P + P) if c < KQ else \
                    slice(k * 192 + HALF * (c - KQ), k * 192 + HALF * (c - KQ) + P)
                w = m.w if c < KQ else m.wo1
                last = product(nc, m.bank[c][:, :], w[HI][:, at], w[LO][:, at],
                               m.xT[HI][:, b, k, :], m.xT[LO][:, b, k, :], k == 0, k == KD - 1)
            last.then_inc(l.done, 1)
    pe.wait_ge(l.lo, (KQ + 1) * B)
    pe.wait_ge(l.rope_lo, B)


def latent_scalar(nc, act, m, l):
    act.wait_ge(l.w_loaded, 32)
    nc.scalar.activation(m.w[HI][:, :], m.w_raw[:, :], ACT.Copy).then_inc(l.w_hi, 1)
    nc.scalar.activation(m.wo1[HI][:, 0:768], m.wo_raw[:, 0:768], ACT.Copy).then_inc(l.w_hi, 1)
    for b in range(B):
        act.wait_ge(l.done, (KQ + 2) * (b + 1))
        for c in range(KQ + 1):
            out = m.xT[HI][:, b, c, :] if c < KQ else m.ckv[HI][:, b, :]
            nc.scalar.activation(out, m.bank[c][:, :], ACT.Copy).then_inc(l.hi, 1)
        nc.scalar.activation(m.ckv32[:, b, :], m.bank[KQ][:, :], ACT.Copy).then_inc(l.ckv_out, 1)
        act.wait_ge(l.rope_added, b + 1)
        nc.scalar.activation(m.xT[HI][HALF:P, b, KQ, :], m.qf[HALF:P, :], ACT.Copy).then_inc(l.rope_hi, 1)


def latent_vector(nc, dve, m, l):
    for b in range(B):
        dve.wait_ge(l.done, (KQ + 2) * (b + 1))
        ge(dve, l.rope_added, b)
        rotate(nc, m, m.bank[KQ + 1]).then_inc(l.rope_out, 1)
        for c in range(KQ + 1):
            if c < KQ:
                dve.wait_ge(l.hi, (KQ + 1) * b + c + 1)
            else:
                dve.wait_ge(l.ckv_out, b + 1)
            lo, hi = (m.xT[LO][:, b, c, :], m.xT[HI][:, b, c, :]) if c < KQ else (m.ckv[LO][:, b, :], m.ckv[HI][:, b, :])
            nc.vector.tensor_tensor(lo, m.bank[c][:, :], hi.bitcast(F32), ALU.subtract).then_inc(l.lo, 1)


def latent_gpsimd(nc, pool, m, l):
    for p, (lo, hi, raw, n) in enumerate(((m.w[LO], m.w[HI], m.w_raw, 1536), (m.wo1[LO], m.wo1[HI], m.wo_raw, 768))):
        pool.wait_ge(l.w_hi, p + 1)
        nc.gpsimd.tensor_tensor(lo[:, 0:n], raw[:, 0:n], hi[:, 0:n].bitcast(F32), ALU.subtract).then_inc(l.w_lo, 1)
    for b in range(B):
        pool.wait_ge(l.rope_out, b + 1)
        if b:
            pool.wait_ge(l.rope_lo, b)
        else:
            pool.wait_ge(l.w_lo, 2)
        nc.gpsimd.tensor_tensor(m.qf[HALF:P, :], m.ra[HALF:P, :], m.rb[HALF:P, :], ALU.add).then_inc(l.rope_added, 1)
        pool.wait_ge(l.rope_hi, b + 1)
        nc.gpsimd.tensor_tensor(m.xT[LO][HALF:P, b, KQ, :], m.qf[HALF:P, :],
                                m.xT[HI][HALF:P, b, KQ, :].bitcast(F32), ALU.subtract).then_inc(l.rope_lo, 1)
    pool.wait_ge(l.rope_lo, B)



def gate_tensor(nc, pe, m, g):
    for b in range(B):
        if b >= 2:
            pe.wait_ge(g.lt_out, b - 1)
        for k in range(KD):
            last = product(nc, m.bank[b % 2][0:E, :], m.gw[HI][:, k, :], m.gw[LO][:, k, :],
                           m.xT[HI][:, b, k, :], m.xT[LO][:, b, k, :], k == 0, k == KD - 1)
        last.then_inc(g.lt_done, 1)
    for b in range(B):
        pe.wait_ge(g.lt_out, b + 1)
        for t in range(NT):
            i = b * NT + t
            last = nc.tensor.transpose(m.bank[2][:, i * E:i * E + E], m.lt[:, b, t * P:t * P + P], m.ident[0:E, 0:E])
    last.then_inc(g.logits_done, 1)
    pe.wait_ge(g.gates_done, 1)
    for b in range(B):
        if b >= 2:
            pe.wait_ge(g.gt_out, b - 1)
        for t in range(NT):
            last = nc.tensor.transpose(m.bank[3 + b % 2][0:E + 1, t * P:t * P + P], m.gates[:, b * NT + t, 0:E + 1], m.ident[:, :])
        last.then_inc(g.gt_done, 1)
    for i in range(B * NT):
        if i % NT == 0:
            pe.wait_ge(g.gt_out, i // NT + 1)
        if i >= 2:
            pe.wait_ge(g.bias_added, i - 1)
        nc.tensor.matmul(m.bank[5 + i % 2][:, :],  
                         m.gt[:, i // NT, (i % NT) * P:(i % NT) * P + P], m.b2[:, :], start=True, stop=True).then_inc(g.bias_done, 1)
    pe.wait_ge(g.bias_added, B * NT)


def gate_scalar(nc, act, m, g):
    for b in range(B):
        act.wait_ge(g.lt_done, b + 1)
        nc.scalar.activation(m.lt[:, b, :], m.bank[b % 2][0:E, :], ACT.Copy).then_inc(g.lt_out, 1)
    act.wait_ge(g.gap_done, 1)
    nc.scalar.activation(m.gap_exp[:, :], m.gap[:, :], ACT.Exp).then_inc(g.exp_done, 1)
    for b in range(B):
        act.wait_ge(g.gt_done, b + 1)
        nc.scalar.activation(m.gt[:, b, :], m.bank[3 + b % 2][0:E + 1, :], ACT.Copy).then_inc(g.gt_out, 1)


def gate_vector(nc, dve, m, g):
    count = [0]

    def then(op):
        count[0] += 1
        op.then_inc(g.chain, 1)
        dve.wait_ge(g.chain, count[0])

    def wide(x):
        return x[:, :].rearrange("p (n a) -> p n a", a=1).to_broadcast([P, B * NT, E])

    def first_of_largest(src, top, pick):
        then(nc.vector.tensor_reduce(top[:, :], src, axis=AX.X, op=ALU.max))
        then(nc.vector.tensor_tensor(pick[:, :, :], src, wide(top), ALU.is_equal))
        then(nc.vector.tensor_tensor(pick[:, :, :], pick[:, :, :], m.ramp[:, :, :], ALU.mult))
        then(nc.vector.tensor_reduce(m.rank[:, :], pick[:, :, :], axis=AX.X, op=ALU.max))
        then(nc.vector.tensor_tensor(pick[:, :, :], pick[:, :, :], wide(m.rank), ALU.is_equal))

    dve.wait_ge(g.logits_done, 1)
    then(nc.vector.tensor_copy(m.logits[:, :, :], m.bank[2][:, 0:B * NT * E].rearrange("p (n e) -> p n e", e=E)))
    first_of_largest(m.logits[:, :, :], m.top1, m.pick1)
    then(nc.vector.scalar_tensor_tensor(out=m.logits[:, :, :], in0=m.pick1[:, :, :], scalar=-FLT_MAX,
                                        in1=m.logits[:, :, :], op0=ALU.mult, op1=ALU.add))
    first_of_largest(m.logits[:, :, :], m.top2, m.pick2)
    nc.vector.tensor_tensor(m.gap[:, :], m.top2[:, :], m.top1[:, :], ALU.subtract).then_inc(g.gap_done, 1)
    dve.wait_ge(g.exp_done, 1)
    then(nc.vector.tensor_scalar_add(m.gap[:, :], m.gap_exp[:, :], 1.0))
    then(nc.vector.reciprocal(m.top1[:, :], m.gap[:, :]))
    then(nc.vector.tensor_tensor(m.top2[:, :], m.top1[:, :], m.gap_exp[:, :], ALU.mult))
    then(nc.vector.tensor_tensor(m.pick1[:, :, :], m.pick1[:, :, :], wide(m.top1), ALU.mult))
    then(nc.vector.tensor_tensor(m.pick2[:, :, :], m.pick2[:, :, :], wide(m.top2), ALU.mult))
    nc.vector.tensor_tensor(m.gates[:, :, 0:E], m.pick1[:, :, :], m.pick2[:, :, :], ALU.add).then_inc(g.gates_done, 1)
    for i in range(B * NT):
        dve.wait_ge(g.bias_done, i + 1)
        nc.vector.tensor_tensor(m.x[:, i, :], m.bank[5 + i % 2][:, :], m.x[:, i, :], ALU.add).then_inc(g.bias_added, 1)



def expert_tensor(nc, pe, m, f):
    def up(s, e, b):
        if b == 0:
            pe.wait_ge(f.w1_lo, e + 1)
        for j in range(KH):
            ge(pe, f.gelu_done, KH * s - KH + j + 1)
            for k in range(KD):
                at = slice(k * HF + j * P, k * HF + j * P + P)
                last = product(nc, m.bank[j][:, :], m.w[HI][:, at], m.w[LO][:, at],
                               m.xT[HI][:, b, k, :], m.xT[LO][:, b, k, :], k == 0, k == KD - 1)
            last.then_inc(f.up_done, 1)

    def down(u, half):
        pe.wait_ge(f.h_lo, KH * (u + 1))
        for t in range(NT):
            ge(pe, f.y_added, NT * u - NT + t + 1)
            for k in range(KH):
                at = slice(t * P, t * P + P)
                last = product(nc, m.bank[2 + t][:, :], m.h[HI][:, half, k, at], m.h[LO][:, half, k, at],
                               m.wo[HI][:, k, :], m.wo[LO][:, k, :], k == 0, k == KH - 1)
            last.then_inc(f.y_done, 1)

    def step(e, b, n1):
        s = B * e + b
        up(s, e, b)
        if n1:
            if b == 1:
                pe.wait_ge(f.w2_lo, e + 1)
            down(s - 1, (b - 1) % 2)

    for b in range(B):
        step(0, b, b >= 1)
    with pe.Fori(1, NE) as e:
        for b in range(B):
            step(e, b, True)
    down(B * NE - 1, 1)


def expert_scalar(nc, act, m, f):
    def step(e, b, n1):
        s = B * e + b
        if b == 0:
            act.wait_ge(f.w1_loaded, 16 * e + 16)
            if n1:
                act.wait_ge(f.up_done, KH * s)
            nc.scalar.activation(m.w[HI][:, 0:KD * HF], m.w_raw[:, 0:KD * HF], ACT.Copy).then_inc(f.w1_hi, 1)
            nc.scalar.activation(m.bias[:, :], m.b1[:, one(e), :], ACT.Copy).then_inc(f.bias_set, 1)
        for j in range(KH):
            act.wait_ge(f.up_done, KH * s + j + 1)
            ge(act, f.h_lo, KH * s - KH + j + 1)
            act.wait_ge(f.bias_set, e + 1)
            nc.scalar.activation(m.hid[:, j, :], m.bank[j][:, :], ACT.Gelu, bias=m.bias[:, j:j + 1]).then_inc(f.gelu_done, 1)
            act.wait_ge(f.gelu_done, KH * s + j + 1)
            if j == 0 and not (isinstance(e, int) and s < 2):
                act.wait_ge(f.y_done, NT * (s - 1))
            nc.scalar.activation(m.h[HI][:, b % 2, j, :], m.hid[:, j, :], ACT.Copy).then_inc(f.h_hi, 1)
        if b == 0:
            act.wait_ge(f.w2_loaded, 16 * e + 16)
            if n1:
                act.wait_ge(f.y_done, NT * s)
            nc.scalar.activation(m.wo[HI][:, :, :], m.wo_raw[:, :].rearrange("p (k n) -> p k n", k=KH), ACT.Copy).then_inc(f.w2_hi, 1)

    for b in range(B):
        step(0, b, False)
    with act.Fori(1, NE) as e:
        for b in range(B):
            step(e, b, True)


def expert_vector(nc, dve, m, f):
    def add(u, b, e):
        for t in range(NT):
            dve.wait_ge(f.y_done, NT * u + t + 1)
            xt = m.x[:, b * NT + t, :]
            nc.vector.scalar_tensor_tensor(out=xt, in0=m.bank[2 + t][:, :], scalar=m.gates[:, b * NT + t, one(e)],
                                           in1=xt, op0=ALU.mult, op1=ALU.add).then_inc(f.y_added, 1)

    def step(e, b, n1):
        s = B * e + b
        for j in range(KH):
            dve.wait_ge(f.h_hi, KH * s + j + 1)
            nc.vector.tensor_tensor(m.h[LO][:, b % 2, j, :], m.hid[:, j, :], m.h[HI][:, b % 2, j, :].bitcast(F32),
                                    ALU.subtract).then_inc(f.h_lo, 1)
        if n1:
            add(s - 1, (b - 1) % B, e if b else e - 1)

    for b in range(B):
        step(0, b, b >= 1)
    with dve.Fori(1, NE) as e:
        for b in range(B):
            step(e, b, True)
    add(B * NE - 1, B - 1, NE - 1)


def expert_gpsimd(nc, pool, m, f):
    def expert(e):
        n = KD * HF
        pool.wait_ge(f.w1_hi, e + 1)
        nc.gpsimd.tensor_tensor(m.w[LO][:, 0:n], m.w_raw[:, 0:n], m.w[HI][:, 0:n].bitcast(F32),
                                ALU.subtract).then_inc(f.w1_lo, 1)
        pool.wait_ge(f.w2_hi, e + 1)
        nc.gpsimd.tensor_tensor(m.wo[LO][:, :, :], m.wo_raw[:, :].rearrange("p (k n) -> p k n", k=KH),
                                m.wo[HI][:, :, :].bitcast(F32), ALU.subtract).then_inc(f.w2_lo, 1)

    expert(0)
    with pool.Fori(1, NE) as e:
        expert(e)


def expert_sync(nc, sp, m, f, w1, w2):
    def expert(e, first):
        if not first:
            sp.wait_ge(f.w1_lo, e)
        sp.dma_start(m.w_raw[:, 0:KD * HF], w1[one(e), :, :].rearrange("e p n -> p (e n)")).then_inc(f.w1_loaded, 16)
        if not first:
            sp.wait_ge(f.w2_lo, e)
        sp.dma_start(m.wo_raw[:, :], w2[one(e), :, :].rearrange("e p n -> p (e n)")).then_inc(f.w2_loaded, 16)

    expert(0, True)
    with sp.Fori(1, NE) as e:
        expert(e, False)




class NormSems:
    def __init__(self, sem):
        self.stats_done = sem("stats_done")
        self.moments_done = sem("moments_done")
        self.var_done = sem("var_done")
        self.root_done = sem("root_done")
        self.newton = sem("newton")
        self.normed = sem("normed")
        self.turned = sem("turned")
        self.xt_hi = sem("xt_hi")
        self.xt_lo = sem("xt_lo")


class AttendSems:
    def __init__(self, sem, mla):
        self.w_loaded = sem("w_loaded")
        self.wo_loaded = sem("wo_loaded")
        self.w_hi = sem("w_hi")
        self.w_lo = sem("w_lo")
        self.wo_hi = sem("wo_hi")
        self.wo_lo = sem("wo_lo")
        self.proj_done = sem("proj_done")
        self.q_hi = sem("q_hi")
        self.q_lo = sem("q_lo")
        self.k_hi = sem("k_hi")
        self.k_lo = sem("k_lo")
        self.v_hi = sem("v_hi")
        self.v_lo = sem("v_lo")
        self.scores_done = sem("scores_done")
        self.masked = sem("masked")
        self.probs_ready = sem("probs_ready")
        self.inverted = sem("inverted")
        self.pt_done = sem("pt_done")
        self.pt_hi = sem("pt_hi")
        self.pt_lo = sem("pt_lo")
        self.av_done = sem("av_done")
        self.o_hi = sem("o_hi")
        self.o_lo = sem("o_lo")
        self.y_done = sem("y_done")
        self.y_added = sem("y_added")
        if mla:
            self.wv_copied = sem("wv_copied")
            self.nope_out = sem("nope_out")
            self.rope_out = sem("rope_out")
            self.rope_added = sem("rope_added")
        else:
            self.vt_copied = sem("vt_copied")
            self.v_turned = sem("v_turned")


class LatentSems:
    def __init__(self, sem):
        self.w_loaded = sem("w_loaded")
        self.w_hi = sem("w_hi")
        self.w_lo = sem("w_lo")
        self.done = sem("done")
        self.hi = sem("hi")
        self.lo = sem("lo")
        self.ckv_out = sem("ckv_out")
        self.rope_out = sem("rope_out")
        self.rope_added = sem("rope_added")
        self.rope_hi = sem("rope_hi")
        self.rope_lo = sem("rope_lo")


class GateSems:
    def __init__(self, sem):
        self.lt_done = sem("lt_done")
        self.lt_out = sem("lt_out")
        self.logits_done = sem("logits_done")
        self.chain = sem("chain")
        self.gap_done = sem("gap_done")
        self.exp_done = sem("exp_done")
        self.gates_done = sem("gates_done")
        self.gt_done = sem("gt_done")
        self.gt_out = sem("gt_out")
        self.bias_done = sem("bias_done")
        self.bias_added = sem("bias_added")


class ExpertSems:
    def __init__(self, sem):
        self.w1_loaded = sem("w1_loaded")
        self.w2_loaded = sem("w2_loaded")
        self.w1_hi = sem("w1_hi")
        self.w1_lo = sem("w1_lo")
        self.w2_hi = sem("w2_hi")
        self.w2_lo = sem("w2_lo")
        self.bias_set = sem("bias_set")
        self.up_done = sem("up_done")
        self.gelu_done = sem("gelu_done")
        self.h_hi = sem("h_hi")
        self.h_lo = sem("h_lo")
        self.y_done = sem("y_done")
        self.y_added = sem("y_added")


class Buffers:
    pass


def program(nc, x_in, wa, woa, wqa, wkva, wb, wob, rope, gate, w1, b1, w2, b2, out):
    with ExitStack() as ctx:
        def sb(name, shape, dt=F32):
            return ctx.enter_context(nc.sbuf_tensor(name, shape, dt))

        def pair(name, shape):
            return [sb(name + "_hi", shape, F32R), sb(name + "_lo", shape, F32R)]

        def named(prefix):
            return lambda name: ctx.enter_context(nc.semaphore(f"{prefix}_{name}"))

        m = Buffers()
        m.x = sb("x", [P, B * NT, D])
        m.xT = pair("xT", [P, B, KD, S])
        m.ident = sb("ident", [P, P])
        m.mask = sb("mask", [P, S])
        m.w_raw = sb("w_raw", [P, 1536])
        m.w = pair("w", [P, 1536])
        m.wo_raw = sb("wo_raw", [P, 2 * D])
        m.wo = pair("wo", [P, 2, D])
        m.wo1 = [w[:, :, :].rearrange("p a n -> p (a n)") for w in m.wo]
        m.wv32 = sb("wv32", [P, DH])
        m.hq = pair("hq", [P, 2, KH, S])
        m.h = m.hq
        m.q = [t[:, 0, 0, :] for t in m.hq]
        m.k = [t[:, 0, 1, :] for t in m.hq]
        m.v = [t[:, 1, 0, :] for t in m.hq]
        m.o = [t[:, 1, 1, :] for t in m.hq]
        m.s = sb("s", [P, S_COLS])
        m.hid = m.s[:, 0:KH * S].rearrange("p (k n) -> p k n", k=KH)
        m.xn = m.s[:, 0:2 * D].rearrange("p (k n) -> p k n", k=2)
        m.pt_hi = sb("pt_hi", [P, PT_COLS], F32R)
        m.pt_lo = sb("pt_lo", [P, PT_COLS], F32R)
        m.top = sb("top", [P, B, NT])
        m.rowsum = sb("rowsum", [P, B, NT])
        m.inv = sb("inv", [P, B, NT])
        m.stats = sb("stats", [P, NT, 6])
        m.moments = sb("moments", [P, NT, 2])
        m.var, m.root, m.rstd0, m.rstd = (sb(n, [P, NT]) for n in ("var", "root", "rstd0", "rstd"))
        m.newt = sb("newt", [P, 3, NT])
        m.ckv = pair("ckv", [P, B, S])
        m.ckv32 = sb("ckv32", [P, B, S])
        m.rope = sb("rope", [P, 2, S])
        m.qf, m.ra, m.rb = (sb(n, [P, S]) for n in ("qf", "ra", "rb"))
        m.vt = m.qf
        m.gw_raw = sb("gw_raw", [P, KD, E])
        m.gw = pair("gw", [P, KD, E])
        m.b1 = sb("b1", [P, NE, KH])
        m.bias = sb("bias", [P, KH])
        m.b2 = sb("b2", [E + 1, D])
        m.lt = m.ckv32[0:E, :, :]
        m.gt = m.ckv32[0:E + 1, :, :]
        m.gates = sb("gates", [P, B * NT, NE])
        m.ramp, m.logits, m.pick1, m.pick2 = (sb(n, [P, B * NT, E]) for n in ("ramp", "logits", "pick1", "pick2"))
        m.top1, m.top2, m.rank, m.gap, m.gap_exp = (sb(n, [P, B * NT]) for n in ("top1", "top2", "rank", "gap", "gap_exp"))
        m.bank = [ctx.enter_context(nc.psum_tensor(f"bank{i}", [P, 512], F32)) for i in range(8)]

        m.const_set = ctx.enter_context(nc.semaphore("const_set"))
        x_loaded = [ctx.enter_context(nc.semaphore(f"x_loaded{b}")) for b in range(B)]
        small_loaded, gw_split, stored = (ctx.enter_context(nc.semaphore(n)) for n in ("small_loaded", "gw_split", "stored"))
        SMALL = 16 * 5
        n = NormSems(named("norm"))
        a1, a2 = AttendSems(named("attn"), False), AttendSems(named("mla"), True)
        lat = LatentSems(named("latent"))
        g = [GateSems(named(f"gate{i}")) for i in range(2)]
        f = [ExpertSems(named(f"expert{i}")) for i in range(2)]
        A_END, F_END = NT * B * H, NT * B * NE

        block = ctx.enter_context(nc.Block())

        @block.sync
        def _(sp):
            for b in range(B):
                sp.dma_start(m.x[:, b * NT:(b + 1) * NT, :],
                             x_in[b, :, :].rearrange("(t p) d -> p t d", p=P)).then_inc(x_loaded[b], 16)
            sp.dma_start(m.gw_raw[:, :, :], gate).then_inc(small_loaded, 16)
            sp.dma_start(m.b1[:, :, :], b1).then_inc(small_loaded, 16)
            sp.dma_start(m.b2[:, :], b2).then_inc(small_loaded, 16)
            sp.dma_start(m.rope[HALF:P, 0, :], rope[0, :, :]).then_inc(small_loaded, 16)
            sp.dma_start(m.rope[HALF:P, 1, :], rope[1, :, :]).then_inc(small_loaded, 16)
            attend_sync(nc, sp, m, a1, False, wa, woa)
            sp.wait_ge(a1.y_added, A_END)
            expert_sync(nc, sp, m, f[0], w1, w2)
            sp.wait_ge(f[0].y_added, F_END)
            sp.dma_start(m.w_raw[:, :], wqa).then_inc(lat.w_loaded, 16)
            sp.dma_start(m.wo_raw[:, 0:768], wkva).then_inc(lat.w_loaded, 16)
            sp.wait_ge(lat.w_lo, 2)
            attend_sync(nc, sp, m, a2, True, wb, wob)
            sp.wait_ge(a2.y_added, A_END)
            expert_sync(nc, sp, m, f[1], w1, w2)
            for b in range(B):
                sp.wait_ge(f[1].y_added, F_END - NT * (B - 1 - b))
                sp.dma_start(out[b, :, :].rearrange("(t p) d -> p t d", p=P),
                             m.x[:, b * NT:(b + 1) * NT, :]).then_inc(stored, 16)
            sp.wait_ge(stored, 16 * B)

        @block.gpsimd
        def _(pool):
            constants(nc, pool, m)
            pool.wait_ge(gw_split, 1)
            nc.gpsimd.tensor_tensor(m.gw[LO][:, :, :], m.gw_raw[:, :, :], m.gw[HI][:, :, :].bitcast(F32),
                                    ALU.subtract).then_inc(gw_split, 1)
            attend_gpsimd(nc, pool, m, a1, False)
            pool.wait_ge(a1.y_added, A_END)
            expert_gpsimd(nc, pool, m, f[0])
            pool.wait_ge(f[0].y_added, F_END)
            latent_gpsimd(nc, pool, m, lat)
            attend_gpsimd(nc, pool, m, a2, True)
            pool.wait_ge(a2.y_added, A_END)
            expert_gpsimd(nc, pool, m, f[1])

        @block.scalar
        def _(act):
            act.wait_ge(small_loaded, SMALL)
            nc.scalar.activation(m.gw[HI][:, :, :], m.gw_raw[:, :, :], ACT.Copy).then_inc(gw_split, 1)
            norm_scalar(nc, act, m, n, 0)
            attend_scalar(nc, act, m, a1, False)
            act.wait_ge(a1.y_added, A_END)
            norm_scalar(nc, act, m, n, 1)
            gate_scalar(nc, act, m, g[0])
            expert_scalar(nc, act, m, f[0])
            act.wait_ge(f[0].y_added, F_END)
            norm_scalar(nc, act, m, n, 2)
            latent_scalar(nc, act, m, lat)
            attend_scalar(nc, act, m, a2, True)
            act.wait_ge(a2.y_added, A_END)
            norm_scalar(nc, act, m, n, 3)
            gate_scalar(nc, act, m, g[1])
            expert_scalar(nc, act, m, f[1])

        @block.vector
        def _(dve):
            dve.wait_ge(m.const_set, CONSTS)
            dve.wait_ge(small_loaded, SMALL)
            norm_vector(nc, dve, m, n, 0, lambda e, b: e.wait_ge(x_loaded[b], 16))
            attend_vector(nc, dve, m, a1, False)
            dve.wait_ge(a1.y_added, A_END)
            norm_vector(nc, dve, m, n, 1, lambda e, b: None)
            gate_vector(nc, dve, m, g[0])
            expert_vector(nc, dve, m, f[0])
            dve.wait_ge(f[0].y_added, F_END)
            norm_vector(nc, dve, m, n, 2, lambda e, b: None)
            latent_vector(nc, dve, m, lat)
            attend_vector(nc, dve, m, a2, True)
            dve.wait_ge(a2.y_added, A_END)
            norm_vector(nc, dve, m, n, 3, lambda e, b: None)
            gate_vector(nc, dve, m, g[1])
            expert_vector(nc, dve, m, f[1])

        @block.tensor
        def _(pe):
            pe.wait_ge(m.const_set, CONSTS)
            pe.wait_ge(gw_split, 2)
            norm_tensor(nc, pe, m, n, 0)
            attend_tensor(nc, pe, m, a1, False)
            pe.wait_ge(a1.y_added, A_END)
            norm_tensor(nc, pe, m, n, 1)
            gate_tensor(nc, pe, m, g[0])
            expert_tensor(nc, pe, m, f[0])
            pe.wait_ge(f[0].y_added, F_END)
            norm_tensor(nc, pe, m, n, 2)
            latent_tensor(nc, pe, m, lat)
            attend_tensor(nc, pe, m, a2, True)
            pe.wait_ge(a2.y_added, A_END)
            norm_tensor(nc, pe, m, n, 3)
            gate_tensor(nc, pe, m, g[1])
            expert_tensor(nc, pe, m, f[1])


def kernel(**inputs):
    import concourse.bacc as bacc
    from concourse.bass_utils import run_bass_kernel_spmd

    def arr(name):
        return np.asarray(inputs[name])

    def tiles(w, cols):
        return w.reshape(-1, P, cols).transpose(1, 0, 2)

    c = np.ascontiguousarray
    w_in = arr("L0_attn_a_w_in").reshape(H, 3, DH, KD, P).transpose(0, 4, 1, 3, 2).reshape(H, P, 3 * KD * DH)
    wo_a = arr("L0_attn_a_w_out").T.reshape(H, DH, D)
    turned = np.concatenate([np.arange(0, HALF, 2), np.arange(1, HALF, 2)])
    order = np.concatenate([np.arange(HALF), HALF + turned])
    wqb = arr("L0_attn_b_Wqb").reshape(KQ, P, H, DH)[:, :, :, order].transpose(2, 1, 0, 3).reshape(H, P, KQ * DH)
    wkvb = arr("L0_attn_b_Wkvb").reshape(P, H, HALF + DH).transpose(1, 0, 2)
    wb = np.concatenate([wqb, wkvb], axis=2)
    wkva = arr("L0_attn_b_Wkva")[:, np.concatenate([np.arange(P), P + turned])]
    wob = arr("L0_attn_b_Wo").reshape(H, DH, D)
    sw1, sb1, sw2 = arr("L0_ffn_shared_w1"), arr("L0_ffn_shared_b1"), arr("L0_ffn_shared_w2")
    w1 = np.concatenate([arr("L0_ffn_w1"), sw1.reshape(D, 2, HF).transpose(1, 0, 2)])
    w1 = w1.reshape(NE, KD, P, HF).transpose(0, 2, 1, 3).reshape(NE, P, KD * HF)
    b1 = np.concatenate([arr("L0_ffn_b1"), sb1.reshape(2, HF)]).reshape(NE, KH, P).transpose(2, 0, 1)
    w2 = np.concatenate([arr("L0_ffn_w2"), sw2.reshape(2, HF, D)])
    w2 = w2.reshape(NE, KH, P, D).transpose(0, 2, 1, 3).reshape(NE, P, KH * D)
    b2 = np.concatenate([arr("L0_ffn_b2"), arr("L0_ffn_shared_b2")[None]])
    inv_freq = (1.0 / np.float32(10000.0) ** (np.arange(QUARTER, dtype=np.float32) * np.float32(2.0 / HALF))).astype(np.float32)
    freqs = inv_freq[:, None] * np.arange(S, dtype=np.float32)[None, :]
    rope = np.stack([np.concatenate([np.cos(freqs), np.cos(freqs)]), np.concatenate([np.sin(freqs), -np.sin(freqs)])]).astype(np.float32)
    arrays = {
        "x_in": c(arr("L0_attn_a_x")), "wa": c(w_in), "woa": c(wo_a),
        "wqa": c(tiles(arr("L0_attn_b_Wqa"), 384).reshape(P, -1)), "wkva": c(tiles(wkva, 192).reshape(P, -1)),
        "wb": c(wb), "wob": c(wob), "rope": c(rope), "gate": c(tiles(arr("L0_ffn_gate_w"), E)),
        "w1": c(w1), "b1": c(b1), "w2": c(w2), "b2": c(b2),
    }
    nc = bacc.Bacc("TRN2", target_bir_lowering=False, num_devices=1)
    args = [nc.dram_tensor("dram_" + k, v.shape, mybir.dt.from_np(v.dtype), kind="ExternalInput").ap() for k, v in arrays.items()]
    args.append(nc.dram_tensor("dram_out", (B, S, D), F32, kind="ExternalOutput").ap())
    program(nc, *args)
    r = run_bass_kernel_spmd(nc, [{"dram_" + k: v for k, v in arrays.items()}], core_ids=[0])
    return r.results[0]["dram_out"]
```

```python
from contextlib import ExitStack

import numpy as np
import concourse.bass as bass
from concourse import mybir

F32 = mybir.dt.float32
F32R = mybir.dt.float32r
ALU = mybir.AluOpType
ACT = mybir.ActivationFunctionType
AX = mybir.AxisListType

P = 128
D = 512
KD = D // P
B = 4
S = 512
NT = S // P
H = 16
DH = 128
HALF = 64
QUARTER = 32
KQ = 3
E = 8
NE = E + 2
HF = 256
KH = HF // P
SCALE = float(DH) ** -0.5
EPS = 1e-5
BIG = 1.0e30
FLT_MAX = 3.0e38
HI, LO = 0, 1

PT_AT = [0, 512, 1152, 1024]
PT_MOV = [(0, 0, 512), (512, 128, 384), (1152, 256, 256), (896, 256, 256)]
PT_ZERO = 896
PT_COLS = 1408
S_AT = [0, 128, 384, 768]
S_COLS = 1280


def product(nc, out, hi, lo, mov_hi, mov_lo, first, last):
    nc.tensor.matmul(out, hi, mov_hi, start=first, stop=False)
    nc.tensor.matmul(out, hi, mov_lo, start=False, stop=False)
    return nc.tensor.matmul(out, lo, mov_hi, start=False, stop=last)



def constants(nc, pool, m):
    nc.gpsimd.memset(m.ident[:, :], 0.0).then_inc(m.const_set, 1)
    nc.gpsimd.memset(m.mask[:, :], 0.0).then_inc(m.const_set, 1)
    nc.gpsimd.memset(m.pt_hi[:, PT_ZERO:PT_ZERO + P].bitcast(F32), 0.0).then_inc(m.const_set, 1)
    nc.gpsimd.memset(m.pt_lo[:, PT_ZERO:PT_ZERO + P].bitcast(F32), 0.0).then_inc(m.const_set, 1)
    for e in range(E):
        nc.gpsimd.memset(m.ramp[:, :, e:e + 1], float(E - e)).then_inc(m.const_set, 1)
    nc.gpsimd.memset(m.gates[:, :, 0:2], 1.0).then_inc(m.const_set, 1)
    nc.gpsimd.memset(m.packed[:, :, :].bitcast(F32), 0.0).then_inc(m.const_set, 1)
    pool.wait_ge(m.const_set, 2)
    nc.gpsimd.affine_select(out=m.ident[:, :], in_=m.ident[:, :], compare_op=ALU.not_equal, fill=1.0,
                            base=0, pattern=[[-1, P]], channel_multiplier=1).then_inc(m.const_set, 1)
    tri = m.mask[:, S - P:S]
    nc.gpsimd.affine_select(out=tri, in_=tri, compare_op=ALU.is_ge, fill=-BIG,
                            base=0, pattern=[[-1, P]], channel_multiplier=1).then_inc(m.const_set, 1)


CONSTS = 4 + E + 2 + 2




def norm_bank(m, r, t):
    return m.bank[(6 if r == 0 else 3) + t % 2]


def norm_stats_vector(nc, dve, m, n, r, b, tile_loaded=None):
    c = B * r + b
    for t in range(NT):
        if tile_loaded:
            dve.wait_ge(tile_loaded[t], 16)
        nc.vector.bn_stats(m.stats[:, b, t, :], m.x[:, b * NT + t, :]).then_inc(n.stats_done, 1)
    for t in range(NT):
        dve.wait_ge(n.stats_done, c * NT + t + 1)
        nc.vector.bn_aggr(m.moments[:, b, t, :], m.stats[:, b, t, :]).then_inc(n.moments_done, 1)
    dve.wait_ge(n.moments_done, NT * (c + 1))
    nc.vector.tensor_scalar_add(m.var[:, b, :], m.moments[:, b, :, 1], EPS).then_inc(n.var_done, 1)


    square, product_, factor = (m.newt[:, b, i, :] for i in range(3))
    dve.wait_ge(n.root_done, c + 1)
    nc.vector.reciprocal(m.rstd0[:, b, :], m.root[:, b, :]).then_inc(n.newton, 1)
    dve.wait_ge(n.newton, 5 * c + 1)
    nc.vector.tensor_tensor(square, m.rstd0[:, b, :], m.rstd0[:, b, :], ALU.mult).then_inc(n.newton, 1)
    dve.wait_ge(n.newton, 5 * c + 2)
    nc.vector.tensor_tensor(product_, square, m.var[:, b, :], ALU.mult).then_inc(n.newton, 1)
    dve.wait_ge(n.newton, 5 * c + 3)
    nc.vector.tensor_scalar(factor, product_, -0.5, 1.5, ALU.mult, ALU.add).then_inc(n.newton, 1)
    dve.wait_ge(n.newton, 5 * c + 4)
    nc.vector.tensor_tensor(m.rstd[:, b, :], m.rstd0[:, b, :], factor, ALU.mult).then_inc(n.newton, 1)
    dve.wait_ge(n.newton, 5 * c + 5)


def normalise(nc, dve, m, n, r, b, t):
    done = NT * (B * r + b) + t
    if done >= 2:
        dve.wait_ge(n.turned, done - 1)
    nc.vector.tensor_scalar(m.xn[:, t % 2, :], m.x[:, b * NT + t, :], m.moments[:, b, t, 0:1],
                            m.rstd[:, b, t:t + 1], ALU.subtract, ALU.mult).then_inc(n.normed, 1)


def norm_start_vector(nc, dve, m, n, r, b):
    normalise(nc, dve, m, n, r, b, 0)
    normalise(nc, dve, m, n, r, b, 1)


def norm_tile_vector(nc, dve, m, n, r, b, t):
    if t + 2 < NT:
        normalise(nc, dve, m, n, r, b, t + 2)
    dve.wait_ge(n.xt_hi, NT * (B * r + b) + t + 1)
    at = (slice(None), b, slice(None), slice(t * P, t * P + P))
    nc.vector.tensor_tensor(m.xT[LO][at], norm_bank(m, r, t)[:, :].rearrange("p (k n) -> p k n", k=KD),
                            m.xT[HI][at].bitcast(F32), ALU.subtract).then_inc(n.xt_lo, 1)


def norm_root_scalar(nc, act, m, n, r, b):
    act.wait_ge(n.var_done, B * r + b + 1)
    nc.scalar.activation(m.root[:, b, :], m.var[:, b, :], ACT.Sqrt).then_inc(n.root_done, 1)


def norm_tile_scalar(nc, act, m, n, r, b, t):
    act.wait_ge(n.turned, NT * (B * r + b) + t + 1)
    nc.scalar.activation(m.xT[HI][:, b, :, t * P:t * P + P],
                         norm_bank(m, r, t)[:, :].rearrange("p (k n) -> p k n", k=KD),
                         ACT.Copy).then_inc(n.xt_hi, 1)


def norm_tile_tensor(nc, pe, m, n, r, b, t):
    done = NT * (B * r + b) + t
    pe.wait_ge(n.normed, done + 1)
    if done >= 2:
        pe.wait_ge(n.xt_lo, done - 1)
    for k in range(KD):
        last = nc.tensor.transpose(norm_bank(m, r, t)[:, k * P:k * P + P],
                                   m.xn[:, t % 2, k * P:k * P + P], m.ident[:, :])
    last.then_inc(n.turned, 1)


OPEN = -1


def nothing(*_):
    pass



def scores_of(m, t):
    n = max(256, (t + 1) * P)
    return m.bank[max(t - 1, 0)][:, (256 if t == 1 else 0):(256 if t == 1 else 0) + n], n


def attend_tensor(nc, pe, m, a, mla, input_ready, first=nothing, after=nothing):
    parts = 3

    def keys(b):
        return (m.xT[HI][:, b, KQ, :], m.xT[LO][:, b, KQ, :]) if mla else (m.k[HI][:, :], m.k[LO][:, :])

    def scores(u, b):
        pe.wait_ge(a.q_lo, u + 1)
        pe.wait_ge(a.k_lo, u + 1)
        k_hi, k_lo = keys(b)
        for t in range(NT):
            out, n = scores_of(m, t)
            at = slice(t * P, t * P + P)
            product(nc, out, m.q[HI][:, at], m.q[LO][:, at], k_hi[:, 0:n], k_lo[:, 0:n],
                    True, True).then_inc(a.scores_done, 1)

    def turn(u):
        pe.wait_ge(a.probs_ready, NT * (u + 1))
        for group in ((0,), (1,), (3, 2)):
            col = 0
            for j in group:
                for t in range(j, NT):
                    last = nc.tensor.transpose(m.bank[min(j, 2)][:, col:col + P],
                                               m.s[:, S_AT[t] + j * P:S_AT[t] + j * P + P], m.ident[:, :])
                    col += P
            last.then_inc(a.pt_done, 1)

    def times_v(u):
        pe.wait_ge(a.v_lo, u + 1)
        for j in range(NT):
            if j < 3:
                pe.wait_ge(a.pt_lo, 3 * u + j + 1)
            src, q0, n = PT_MOV[j]
            at = slice(j * DH, j * DH + DH)
            last = product(nc, m.bank[5][:, q0:q0 + n], m.v[HI][:, at], m.v[LO][:, at],
                           m.pt_hi[:, src:src + n], m.pt_lo[:, src:src + n], j == 0, j == NT - 1)
        last.then_inc(a.av_done, 1)

    def output(v, slot, tiles):
        if tiles[0] == 0:
            pe.wait_ge(a.o_lo, v + 1)
        for t in tiles:
            ge(pe, a.y_added, NT * v + t - 1)
            at = slice(t * P, t * P + P)
            product(nc, m.bank[6 + t % 2][:, :], m.o[HI][:, at], m.o[LO][:, at],
                    m.wo[HI][:, slot, :], m.wo[LO][:, slot, :], True, True).then_inc(a.y_done, 1)

    def project_q(s, h, b):
        if b == 0:
            pe.wait_ge(a.w_lo, parts * h + 1)
        if mla:
            ge(pe, a.nope_out, s)
            ge(pe, a.rope_out, s)
            if b == 1:
                pe.wait_ge(a.wo_lo, h + 1)
        else:
            ge(pe, a.vt_copied, s)
        kn = KQ if mla else KD
        for k in range(kn):
            at = slice(k * DH, k * DH + DH)
            last = product(nc, m.bank[3][:, :], m.w[HI][:, at], m.w[LO][:, at],
                           m.xT[HI][:, b, k, :], m.xT[LO][:, b, k, :], k == 0, k == kn - 1)
        last.then_inc(a.proj_done, 1)

    def project_k(s, h, b):
        if b == 0:
            pe.wait_ge(a.w_lo, parts * h + 2)
        ge(pe, a.k_lo if mla else a.v_lo, s)
        if mla:
            last = product(nc, m.bank[4][0:HALF, :], m.w[HI][:, 512:512 + HALF], m.w[LO][:, 512:512 + HALF],
                           m.ckv[HI][:, b, :], m.ckv[LO][:, b, :], True, True)
        else:
            for k in range(KD):
                at = slice(512 + k * DH, 512 + k * DH + DH)
                last = product(nc, m.bank[4][:, :], m.w[HI][:, at], m.w[LO][:, at],
                               m.xT[HI][:, b, k, :], m.xT[LO][:, b, k, :], k == 0, k == KD - 1)
        last.then_inc(a.proj_done, 1)

    def project_v(s, h, b):
        if b == 0:
            pe.wait_ge(a.w_lo, parts * h + 3)
        pe.wait_ge(a.q_lo, s + 1)
        for k in range(KD):
            at = slice(1024 + k * DH, 1024 + k * DH + DH)
            last = product(nc, m.bank[3][:, :], m.w[HI][:, at], m.w[LO][:, at],
                           m.xT[HI][:, b, k, :], m.xT[LO][:, b, k, :], k == 0, k == KD - 1)
        last.then_inc(a.proj_done, 1)

    def combine(s, h):
        pe.wait_ge(a.w_lo, parts * h + 3)
        pe.wait_ge(a.nope_out, s + 1)
        pe.wait_ge(a.rope_out, s + 1)
        product(nc, m.bank[3][:, :], m.w[HI][:, 576:576 + DH], m.w[LO][:, 576:576 + DH],
                m.w[HI][:, 1024:1536], m.w[LO][:, 1024:1536], True, True).then_inc(a.combined, 1)

    def turn_v(s):
        pe.wait_ge(a.vt_copied, s + 1)
        pe.wait_ge(a.k_lo, s + 1)
        for t in range(NT):
            last = nc.tensor.transpose(m.bank[4][:, t * DH:t * DH + DH], m.vt[:, t * P:t * P + P], m.ident[:, :])
        last.then_inc(a.v_turned, 1)

    def step(h, b, n1, n2, new=True, hook=nothing):
        s = 4 * h + b
        u, v = s - 1, s - 2
        bu, slot = (b - 1) % B, (h if b >= 2 else h - 1) % 2
        if mla and isinstance(h, int) and h == 0:
            input_ready(b)
        if n1:
            scores(u, bu)
        if not mla and isinstance(h, int) and h == 0:
            input_ready(b)
        if new and mla:
            project_q(s, h, b)
        if n2:
            if b == 2:
                pe.wait_ge(a.wo_lo, h + 1)
            output(v, slot, (0, 1))
        if new and not mla:
            project_q(s, h, b)
        hook(b, 0)
        if n1:
            turn(u)
        if new:
            project_k(s, h, b)
            hook(b, 1)
            if not mla:
                project_v(s, h, b)
                hook(b, 2)
            elif b == 0:
                combine(s, h)
        if n2 and mla:
            output(v, slot, (2, 3))
        if n1:
            times_v(u)
        if n2 and not mla:
            output(v, slot, (2, 3))
        if new and not mla:
            turn_v(s)
        hook(b, 3)

    for b in range(B):
        step(0, b, b >= 1, b >= 2, hook=first)
    with pe.Fori(1, H - 1) as h:
        for b in range(B):
            step(h, b, True, True)
    for b in range(B):
        step(H - 1, b, True, True)
    after(0)
    step(H, 0, True, True, new=False)
    after(1)
    step(H, 1, False, True, new=False)


def split_weights(nc, act, m, a, mla, h, part, again, free=nothing):
    parts, proj = weight_parts(mla), a.projections
    if part == 0:
        act.wait_ge(a.w_loaded, 16 * h + 16)
        if again:
            act.wait_ge(a.proj_done, proj * B * h - (1 if mla else 0))
        else:
            free(0)
    if mla and part == 1 and again:
        act.wait_ge(a.proj_done, proj * B * h)
    src, dst = parts[part]
    if mla and part == 2:
        act.wait_ge(a.wo_loaded, 16 * h + 16)
        if again:
            act.wait_ge(a.combined, h)
        nc.scalar.activation(m.w[HI][:, dst[0]:dst[1]], m.wo_raw[:, 0:D], ACT.Copy).then_inc(a.w_hi, 1)
    else:
        nc.scalar.activation(m.w[HI][:, dst[0]:dst[1]], m.w_raw[:, src[0]:src[1]], ACT.Copy).then_inc(a.w_hi, 1)


def attend_scalar(nc, act, m, a, mla, free, first=nothing, mid=nothing, after=nothing):
    parts = weight_parts(mla)
    proj = 2 if mla else 3

    def split_w(h, part, again):
        split_weights(nc, act, m, a, mla, h, part, again, free)

    def split_last(h, again):
        if not mla:
            act.wait_ge(a.wo_loaded, 16 * h + 16)
            if again:
                act.wait_ge(a.y_done, 16 * h - 8)
            else:
                free(1)
        split_w(h, 2, again)
        if not mla:
            nc.scalar.activation(m.wo[HI][:, one(h % 2), :], m.wo_raw[:, 0:D].rearrange("p (a n) -> p a n", a=1),
                                 ACT.Copy).then_inc(a.wo_hi, 1)

    def exps(u, b):
        for t in range(NT):
            act.wait_ge(a.masked, NT * u + t + 1)
            at = m.s[:, S_AT[t]:S_AT[t] + (t + 1) * P]
            nc.scalar.activation(at, at, ACT.Exp, bias=m.top[:, b, t:t + 1], scale=-1.0,
                                 accum_out=m.rowsum[:, b, t:t + 1]).then_inc(a.probs_ready, 1)

    def probs_hi(u):
        for g, (dst, n, src) in enumerate(((0, 512, 0), (512, 384, 1), (1024, 384, 2))):
            act.wait_ge(a.pt_done, 3 * u + g + 1)
            nc.scalar.activation(m.pt_hi[:, dst:dst + n], m.bank[src][:, 0:n], ACT.Copy).then_inc(a.pt_hi, 1)

    def step(h, b, n1, new=True, mid=None, hook=nothing):
        s = 4 * h + b
        u, bu = s - 1, (b - 1) % B
        fresh = new and b == 0 and not mla
        ahead = mla and new and b == B - 1 and not last_head(h)
        if fresh:
            split_w(h, 0, n1)
        if n1:
            exps(u, bu)
        if fresh:
            split_w(h, 1, n1)
            split_last(h, n1)
        hook(b, OPEN)
        if new:
            act.wait_ge(a.proj_done, proj * s + 1)
            if mla:
                nc.scalar.activation(m.qf[0:HALF, :], m.bank[3][0:HALF, :], ACT.Copy).then_inc(a.nope_out, 1)
                if ahead:
                    split_w(h + 1, 0, True)
            else:
                nc.scalar.activation(m.q[HI][:, :], m.bank[3][:, :], ACT.Copy).then_inc(a.q_hi, 1)
        hook(b, 0)
        if n1:
            probs_hi(u)
        if new:
            act.wait_ge(a.proj_done, proj * s + 2)
            if mla:
                nc.scalar.activation(m.xT[HI][0:HALF, b, KQ, :], m.bank[4][0:HALF, :], ACT.Copy).then_inc(a.k_hi, 1)
                if b == 0:
                    act.wait_ge(a.combined, h + 1)
                    if n1:
                        act.wait_ge(a.y_done, 16 * h - 8)
                    else:
                        free(1)
                act.wait_ge(a.nope_out, s + 1)
                act.wait_ge(a.rope_added, s + 1)
                nc.scalar.activation(m.q[HI][:, :], m.qf[:, :], ACT.Copy).then_inc(a.q_hi, 1)
                if b == 0:
                    nc.scalar.activation(m.wo[HI][:, one(h % 2), :], m.bank[3][:, :].rearrange("p (a n) -> p a n", a=1),
                                         ACT.Copy).then_inc(a.wo_hi, 1)
                if ahead:
                    split_w(h + 1, 1, True)
                    split_w(h + 1, 2, True)
                if mid:
                    mid()
            else:
                nc.scalar.activation(m.k[HI][:, :], m.bank[4][:, :], ACT.Copy).then_inc(a.k_hi, 1)
                hook(b, 1)
                if mid:
                    mid()
                act.wait_ge(a.proj_done, proj * s + 3)
                nc.scalar.activation(m.vt[:, :], m.bank[3][:, :], ACT.Copy).then_inc(a.vt_copied, 1)
                hook(b, 2)
        if n1:
            act.wait_ge(a.av_done, u + 1)
            ge(act, a.y_done, 4 * u)
            nc.scalar.activation(m.o[HI][:, :], m.bank[5][:, :], ACT.Copy).then_inc(a.o_hi, 1)
        if mid and not new:
            mid()
        if new and mla:
            nc.scalar.activation(m.v[HI][:, :], m.ctok[:, b, :], ACT.Copy).then_inc(a.v_hi, 1)
        if new and not mla:
            act.wait_ge(a.v_turned, s + 1)
            nc.scalar.activation(m.v[HI][:, :], m.bank[4][:, :], ACT.Copy).then_inc(a.v_hi, 1)
        hook(b, 3)

    for b in range(B):
        step(0, b, b >= 1, hook=first)
    with act.Fori(1, H - 1) as h:
        for b in range(B):
            step(h, b, True)
    for b in range(B):
        step(H - 1, b, True, mid=(lambda: mid(0)) if b == B - 1 else None)
    after(0)
    step(H, 0, True, new=False, mid=lambda: mid(1))
    after(1)


def attend_vector(nc, dve, m, a, mla, first=nothing, mid=nothing, after=nothing):
    proj = 2 if mla else 3

    def mask_and_max(u, b):
        for t in range(NT):
            out, _ = scores_of(m, t)
            n = (t + 1) * P
            nc.vector.tensor_tensor_reduce(
                out=m.s[:, S_AT[t]:S_AT[t] + n], in0=out[:, 0:n], in1=m.mask[:, S - n:S], scale=-SCALE,
                scalar=FLT_MAX, op0=ALU.add, op1=ALU.min, accum_out=m.top[:, b, t:t + 1]).then_inc(a.masked, 1)

    def add_output(v, b, tiles):
        for t in tiles:
            dve.wait_ge(a.y_done, NT * v + t + 1)
            xt = m.x[:, b * NT + t, :]
            nc.vector.scalar_tensor_tensor(out=xt, in0=m.bank[6 + t % 2][:, :], scalar=m.inv[:, b, t:t + 1],
                                           in1=xt, op0=ALU.mult, op1=ALU.add).then_inc(a.y_added, 1)

    def probs_lo(u):
        for g, (dst, n, src) in enumerate(((0, 512, 0), (512, 384, 1), (1024, 384, 2))):
            dve.wait_ge(a.pt_hi, 3 * u + g + 1)
            nc.vector.tensor_tensor(m.pt_lo[:, dst:dst + n], m.bank[src][:, 0:n],
                                    m.pt_hi[:, dst:dst + n].bitcast(F32), ALU.subtract).then_inc(a.pt_lo, 1)

    def rest(out, bank, hi, done):
        return nc.vector.tensor_tensor(out, bank, hi.bitcast(F32), ALU.subtract).then_inc(done, 1)

    def step(h, b, n1, n2, new=True, mid=None, hook=nothing):
        s = 4 * h + b
        u, v, bu, bv = s - 1, s - 2, (b - 1) % B, (b - 2) % B
        if n1:
            dve.wait_ge(a.scores_done, NT * (u + 1))
        if n2:
            nc.vector.reciprocal(m.inv[:, bv, :], m.rowsum[:, bv, :]).then_inc(a.inverted, 1)
        if n1:
            mask_and_max(u, bu)
        if new and mla:
            dve.wait_ge(a.proj_done, proj * s + 1)
            ge(dve, a.rope_added, s)
            rotate(nc, m, m.bank[3]).then_inc(a.rope_out, 1)
        if n2:
            dve.wait_ge(a.inverted, v + 1)
            add_output(v, bv, (0, 1))
        hook(b, OPEN)
        if new and not mla:
            dve.wait_ge(a.q_hi, s + 1)
            rest(m.q[LO][:, :], m.bank[3][:, :], m.q[HI][:, :], a.q_lo)
        hook(b, 0)
        if n1:
            probs_lo(u)
        if new:
            dve.wait_ge(a.k_hi, s + 1)
            if mla:
                rest(m.xT[LO][0:HALF, b, KQ, :], m.bank[4][0:HALF, :], m.xT[HI][0:HALF, b, KQ, :], a.k_lo)
                if b == 0:
                    dve.wait_ge(a.wo_hi, h + 1)
                    flat = m.bank[3][:, :].rearrange("p (a n) -> p a n", a=1)
                    rest(m.wo[LO][:, one(h % 2), :], flat, m.wo[HI][:, one(h % 2), :], a.wo_lo)
            else:
                rest(m.k[LO][:, :], m.bank[4][:, :], m.k[HI][:, :], a.k_lo)
            hook(b, 1)
            if mid:
                mid()
            hook(b, 2)
        if n2:
            add_output(v, bv, (2, 3))
        if n1:
            dve.wait_ge(a.o_hi, u + 1)
            rest(m.o[LO][:, :], m.bank[5][:, :], m.o[HI][:, :], a.o_lo)
        if mid and not new:
            mid()
        if new and not mla:
            dve.wait_ge(a.v_hi, s + 1)
            rest(m.v[LO][:, :], m.bank[4][:, :], m.v[HI][:, :], a.v_lo)
        hook(b, 3)

    for b in range(B):
        step(0, b, b >= 1, b >= 2, hook=first)
    with dve.Fori(1, H - 1) as h:
        for b in range(B):
            step(h, b, True, True)
    for b in range(B):
        step(H - 1, b, True, True, mid=(lambda: mid(0)) if b == B - 1 else None)
    after(0)
    step(H, 0, True, True, new=False, mid=lambda: mid(1))
    after(1)
    step(H, 1, False, True, new=False)


def weight_parts(mla):
    if mla:
        return ((0, 384), (0, 384)), ((384, 576), (512, 704)), ((0, 512), (1024, 1536))
    return tuple(((512 * i, 512 * i + 512),) * 2 for i in range(3))


def rest_weights(nc, pool, m, a, mla, h, part):
    pool.wait_ge(a.w_hi, 3 * h + part + 1)
    src, dst = weight_parts(mla)[part]
    at = slice(dst[0], dst[1])
    raw = m.wo_raw if mla and part == 2 else m.w_raw
    nc.gpsimd.tensor_tensor(m.w[LO][:, at], raw[:, src[0]:src[1]], m.w[HI][:, at].bitcast(F32),
                            ALU.subtract).then_inc(a.w_lo, 1)


def attend_gpsimd(nc, pool, m, a, mla):
    def rest_w(h, part):
        rest_weights(nc, pool, m, a, mla, h, part)

    def rest_wo(h):
        pool.wait_ge(a.wo_hi, h + 1)
        at = one(h % 2)
        nc.gpsimd.tensor_tensor(m.wo[LO][:, at, :], m.wo_raw[:, 0:D].rearrange("p (a n) -> p a n", a=1),
                                m.wo[HI][:, at, :].bitcast(F32), ALU.subtract).then_inc(a.wo_lo, 1)

    def head(h):
        if not mla:
            for part in range(3):
                rest_w(h, part)
            rest_wo(h)
            return
        for b in range(B):
            s = 4 * h + b
            pool.wait_ge(a.rope_out, s + 1)
            ge(pool, a.q_lo, s)
            ge(pool, a.v_lo, s)
            if b == 0:
                pool.wait_ge(a.w_lo, 3 * (h + 1))
            nc.gpsimd.tensor_tensor(m.qf[HALF:P, :], m.ra[HALF:P, :], m.rb[HALF:P, :],
                                    ALU.add).then_inc(a.rope_added, 1)
            ahead = b == B - 1 and not last_head(h)
            if ahead:
                pool.wait_ge(a.rope_added, s + 1)
                rest_w(h + 1, 0)
            pool.wait_ge(a.q_hi, s + 1)
            nc.gpsimd.tensor_tensor(m.q[LO][:, :], m.qf[:, :], m.q[HI][:, :].bitcast(F32),
                                    ALU.subtract).then_inc(a.q_lo, 1)
            if ahead:
                rest_w(h + 1, 1)
                rest_w(h + 1, 2)
            pool.wait_ge(a.v_hi, s + 1)
            nc.gpsimd.tensor_tensor(m.v[LO][:, :], m.ctok[:, b, :], m.v[HI][:, :].bitcast(F32),
                                    ALU.subtract).then_inc(a.v_lo, 1)

    head(0)
    with pool.Fori(1, H - 1 if mla else H) as h:
        head(h)
    if mla:
        head(H - 1)


def load_head(sp, m, a, w_dram, wo_dram, h):
    sp.dma_start(m.w_raw[:, 0:w_dram.shape[2]], w_dram[one(h), :, :].rearrange("h p n -> p (h n)")).then_inc(a.w_loaded, 16)
    sp.dma_start(m.wo_raw[:, 0:D], wo_dram[one(h), :, :].rearrange("h p n -> p (h n)")).then_inc(a.wo_loaded, 16)


def attend_sync(nc, sp, m, a, mla, w_dram, wo_dram):
    with sp.Fori(1, H) as h:
        sp.wait_ge(a.w_lo, 3 * h)
        if not mla:
            sp.wait_ge(a.wo_lo, h)
        load_head(sp, m, a, w_dram, wo_dram, h)


def last_head(h):
    return isinstance(h, int) and h == H - 1


def one(i):
    return slice(i, i + 1) if isinstance(i, int) else bass.ds(i, 1)


def ge(eng, sem, value):
    if not isinstance(value, int) or value > 0:
        eng.wait_ge(sem, value)


def rotate(nc, m, bank):
    e, o = HALF, HALF + QUARTER
    nc.vector.tensor_tensor(m.ra[e:P, :], bank[e:P, :], m.rope[e:P, 0, :], ALU.mult)
    nc.vector.tensor_tensor(m.rb[e:o, :], bank[o:P, :], m.rope[o:P, 1, :], ALU.mult)
    return nc.vector.tensor_tensor(m.rb[o:P, :], bank[e:o, :], m.rope[e:o, 1, :], ALU.mult)



LATENT_BANK = [0, 1, 2, 5, 6]


def latent_tensor(nc, pe, m, l, f, input_ready, first):
    for b in range(B):
        input_ready(b)
        for c in range(KQ + 2):
            if b == 0 and c == 0:
                pe.wait_ge(l.w_lo, 1)
            if b == 0 and c == KQ - 1:
                pe.wait_ge(f.y_added, NT * B * NE)
            if b == 0 and c == KQ:
                pe.wait_ge(l.w_lo, 2)
            if b:
                if c <= KQ:
                    pe.wait_ge(l.lo, (KQ + 1) * (b - 1) + c + 1)
                else:
                    pe.wait_ge(l.rope_out, b)
            for k in range(KD):
                at = slice(k * 384 + c * P, k * 384 + c * P + P) if c < KQ else \
                    slice(k * 192 + HALF * (c - KQ), k * 192 + HALF * (c - KQ) + P)
                w = m.w if c < KQ else m.wo1
                last = product(nc, m.bank[LATENT_BANK[c]][:, :], w[HI][:, at], w[LO][:, at],
                               m.xT[HI][:, b, k, :], m.xT[LO][:, b, k, :], k == 0, k == KD - 1)
            last.then_inc(l.done, 1)
            if 0 < c <= KQ:
                first(b, c - 1)
        pe.wait_ge(l.ckv_out, b + 1)
        ge(pe, l.tok_out, b)
        for t in range(NT):
            last = nc.tensor.transpose(m.bank[7][:, t * P:t * P + P], m.ckv32[:, t * P:t * P + P], m.ident[:, :])
        last.then_inc(l.tok_done, 1)
        first(b, NT - 1)


def latent_scalar(nc, act, m, l, f, first, then):
    act.wait_ge(l.w_loaded, 16)
    act.wait_ge(f.up_done, KH * B * NE)
    nc.scalar.activation(m.w[HI][:, :], m.w_raw[:, :], ACT.Copy).then_inc(l.w_hi, 1)
    act.wait_ge(l.wkva_loaded, 16)
    act.wait_ge(f.y_done, NT * B * NE)
    nc.scalar.activation(m.wo1[HI][:, 0:768], m.wo_raw[:, 0:768], ACT.Copy).then_inc(l.w_hi, 1)
    for b in range(B):
        for i in range(OPEN, NT - 1):
            first(b, i)
        act.wait_ge(l.done, (KQ + 2) * b + KQ + 1)
        nc.scalar.activation(m.ckv32[:, :], m.bank[5][:, :], ACT.Copy).then_inc(l.ckv_out, 1)
        act.wait_ge(l.done, (KQ + 2) * (b + 1))
        if b == B - 1:
            then()
        for c in range(KQ + 1):
            out = m.xT[HI][:, b, c, :] if c < KQ else m.ckv[HI][:, b, :]
            nc.scalar.activation(out, m.bank[LATENT_BANK[c]][:, :], ACT.Copy).then_inc(l.hi, 1)
        act.wait_ge(l.tok_done, b + 1)
        nc.scalar.activation(m.ctok[:, b, :], m.bank[7][:, :], ACT.Copy).then_inc(l.tok_out, 1)
        act.wait_ge(l.rope_added, b + 1)
        nc.scalar.activation(m.xT[HI][HALF:P, b, KQ, :], m.qf[HALF:P, :], ACT.Copy).then_inc(l.rope_hi, 1)
        first(b, NT - 1)


def latent_vector(nc, dve, m, l, first):
    def rotary(b):
        dve.wait_ge(l.done, (KQ + 2) * (b + 1))
        ge(dve, l.rope_added, b)
        rotate(nc, m, m.bank[6]).then_inc(l.rope_out, 1)

    for b in range(B):
        for i in range(OPEN, NT - 1):
            first(b, i)
        if b == B - 1:
            rotary(b)
        for c in range(KQ + 1):
            dve.wait_ge(l.hi, (KQ + 1) * b + c + 1)
            lo, hi = (m.xT[LO][:, b, c, :], m.xT[HI][:, b, c, :]) if c < KQ else (m.ckv[LO][:, b, :], m.ckv[HI][:, b, :])
            nc.vector.tensor_tensor(lo, m.bank[LATENT_BANK[c]][:, :], hi.bitcast(F32), ALU.subtract).then_inc(l.lo, 1)
        if b < B - 1:
            rotary(b)
        first(b, NT - 1)


def latent_gpsimd(nc, pool, m, l, a, then):
    for p, (lo, hi, raw, n) in enumerate(((m.w[LO], m.w[HI], m.w_raw, 1536), (m.wo1[LO], m.wo1[HI], m.wo_raw, 768))):
        pool.wait_ge(l.w_hi, p + 1)
        nc.gpsimd.tensor_tensor(lo[:, 0:n], raw[:, 0:n], hi[:, 0:n].bitcast(F32), ALU.subtract).then_inc(l.w_lo, 1)
    for b in range(B):
        if b == B - 1:
            pool.wait_ge(l.rope_lo, b)
            then()
        pool.wait_ge(l.rope_out, b + 1)
        if b:
            pool.wait_ge(l.rope_lo, b)
        else:
            pool.wait_ge(l.w_lo, 2)
        if b == B - 1:
            pool.wait_ge(a.w_lo, 3)
        nc.gpsimd.tensor_tensor(m.qf[HALF:P, :], m.ra[HALF:P, :], m.rb[HALF:P, :], ALU.add).then_inc(l.rope_added, 1)
        pool.wait_ge(l.rope_hi, b + 1)
        nc.gpsimd.tensor_tensor(m.xT[LO][HALF:P, b, KQ, :], m.qf[HALF:P, :],
                                m.xT[HI][HALF:P, b, KQ, :].bitcast(F32), ALU.subtract).then_inc(l.rope_lo, 1)
    pool.wait_ge(l.rope_lo, B)



CHAIN = 23
GAP = 14
GROUP = 32
BIAS_ROWS = 3 * GROUP


def gate_vector(nc, dve, m, g, b):
    count = [CHAIN * b]

    def then(op):
        count[0] += 1
        op.then_inc(g.chain, 1)
        dve.wait_ge(g.chain, count[0])

    def wide(x):
        return x[:, :].rearrange("p (n a) -> p n a", a=1).to_broadcast([P, NT, E])

    def first_of_largest(top, pick):
        then(nc.vector.tensor_reduce(top[:, :], m.logits[:, :, :], axis=AX.X, op=ALU.max))
        then(nc.vector.tensor_tensor(pick[:, :, :], m.logits[:, :, :], wide(top), ALU.is_equal))
        then(nc.vector.tensor_tensor(pick[:, :, :], pick[:, :, :], m.ramp[:, :, :], ALU.mult))
        then(nc.vector.tensor_reduce(m.rank[:, :], pick[:, :, :], axis=AX.X, op=ALU.max))
        then(nc.vector.tensor_tensor(pick[:, :, :], pick[:, :, :], wide(m.rank), ALU.is_equal))

    dve.wait_ge(g.logits_done, b + 1)
    halves = m.bank[4][:, 0:NT * 2 * E].rearrange("p (n e) -> p n e", e=2 * E)
    then(nc.vector.tensor_copy(m.pick1[:, :, :], halves[:, :, 0:E]))
    then(nc.vector.tensor_tensor(m.logits[:, :, :], m.pick1[:, :, :], halves[:, :, E:2 * E], ALU.add))
    first_of_largest(m.top1, m.pick1)
    then(nc.vector.scalar_tensor_tensor(out=m.logits[:, :, :], in0=m.pick1[:, :, :], scalar=-FLT_MAX,
                                        in1=m.logits[:, :, :], op0=ALU.mult, op1=ALU.add))
    first_of_largest(m.top2, m.pick2)
    then(nc.vector.tensor_tensor(m.gap[:, :], m.top2[:, :], m.top1[:, :], ALU.subtract))
    dve.wait_ge(g.exp_done, b + 1)
    then(nc.vector.tensor_scalar_add(m.gap[:, :], m.gap_exp[:, :], 1.0))
    then(nc.vector.reciprocal(m.top1[:, :], m.gap[:, :]))
    then(nc.vector.tensor_tensor(m.top2[:, :], m.top1[:, :], m.gap_exp[:, :], ALU.mult))
    then(nc.vector.tensor_tensor(m.pick1[:, :, :], m.pick1[:, :, :], wide(m.top1), ALU.mult))
    then(nc.vector.tensor_tensor(m.pick2[:, :, :], m.pick2[:, :, :], wide(m.top2), ALU.mult))
    then(nc.vector.tensor_tensor(m.gates[:, b * NT:(b + 1) * NT, 2:NE], m.pick1[:, :, :], m.pick2[:, :, :], ALU.add))
    gates = m.gates[:, b * NT:(b + 1) * NT, 1:NE]
    hi, again, lo = (m.packed[:, :, i * GROUP:i * GROUP + E + 1] for i in range(3))
    ge(dve, g.gt_done, b)
    nc.vector.tensor_copy(again, gates).then_inc(g.chain, 1)
    count[0] += 1
    then(nc.vector.tensor_copy(hi, gates))
    then(nc.vector.tensor_tensor(lo, gates, hi.bitcast(F32), ALU.subtract))
    assert count[0] == CHAIN * (b + 1)



Y_BANK = [2, 5, 6, 7]
W1_PARTS = [slice(0, KD * HF // 2), slice(KD * HF // 2, KD * HF)]


def expert_tensor(nc, pe, m, f, g, input_ready, first=nothing, after=nothing):
    def up(s, e, b, hook=nothing):
        for j in range(KH):
            ge(pe, f.gelu_done, KH * s - KH + j + 1)
            for k in range(KD):
                if b == 0 and j == 0 and k % (KD // 2) == 0:
                    pe.wait_ge(f.w1_lo, 2 * e + 1 + k // (KD // 2))
                at = slice(k * HF + j * P, k * HF + j * P + P)
                last = product(nc, m.bank[j][:, :], m.w[HI][:, at], m.w[LO][:, at],
                               m.xT[HI][:, b, k, :], m.xT[LO][:, b, k, :], k == 0, k == KD - 1)
            last.then_inc(f.up_done, 1)
            hook(j)

    def down(u, half, hook=nothing, biases=None):
        pe.wait_ge(f.h_lo, KH * (u + 1))
        if biases is not None:
            pe.wait_ge(g.gt_out, biases + 1)
        for t in range(NT):
            ge(pe, f.y_added, NT * u - NT + t + 1)
            for k in range(KH):
                at = slice(t * P, t * P + P)
                last = product(nc, m.bank[Y_BANK[t]][:, :], m.h[HI][:, half, k, at], m.h[LO][:, half, k, at],
                               m.wo[HI][:, k, :], m.wo[LO][:, k, :], k == 0, k == KH - 1 and biases is None)
            if biases is not None:
                last = nc.tensor.matmul(m.bank[Y_BANK[t]][:, :], m.gt[:, t * P:t * P + P], m.b2[:, :],
                                        start=False, stop=True)
            last.then_inc(f.y_done, 1)
            hook(t)

    def logits(b):
        if b == 0:
            pe.wait_ge(m.gw_split, 2)
            pe.wait_ge(m.b2_split, 2)
        ge(pe, g.lt_out, b)
        for k in range(KD):
            for part in (HI, LO):
                last = nc.tensor.matmul(m.bank[3][0:2 * E, :], m.gw[:, k, :], m.xT[part][:, b, k, :],
                                        start=k == 0 and part == HI, stop=k == KD - 1 and part == LO)
        last.then_inc(g.lt_done, 1)

    def turn_logits(b):
        pe.wait_ge(g.lt_out, b + 1)
        ge(pe, g.gt_out, b)
        for t in range(NT):
            last = nc.tensor.transpose(m.bank[4][:, t * 2 * E:t * 2 * E + 2 * E], m.lt[:, t * P:t * P + P],
                                       m.ident[0:2 * E, 0:2 * E])
        last.then_inc(g.logits_done, 1)

    def turn_gates(b):
        pe.wait_ge(g.chain, CHAIN * (b + 1))
        for t in range(NT):
            last = nc.tensor.transpose(m.bank[4][0:BIAS_ROWS, t * P:t * P + P], m.packed[:, t, :].bitcast(F32),
                                       m.ident[:, :])
        last.then_inc(g.gt_done, 1)

    def step(e, b, biases=None):
        s = B * e + b
        up(s, e, b, hook=lambda j: turn_gates(biases) if biases is not None and j == 0 else None)
        if b == 1:
            pe.wait_ge(f.w2_lo, e + 1)
        down(s - 1, (b - 1) % 2, biases=biases)

    for b in range(B):
        input_ready(b)
        up(b, 0, b, hook=lambda j: first(b, j))
        if b:
            if b == 1:
                pe.wait_ge(f.w2_lo, 1)
            down(b - 1, (b - 1) % 2, hook=lambda t: first(b, 2 + t // 2) if t % 2 else None)
        else:
            first(b, 2)
            first(b, 3)
    for b in range(B):
        s = B + b
        logits(b)
        up(s, 1, b, hook=lambda j: turn_gates(b - 1) if b and j == 0 else None)
        turn_logits(b)
        if b == 1:
            pe.wait_ge(f.w2_lo, 2)
        down(s - 1, (b - 1) % 2, biases=b - 1 if b else None)
    for b in range(B):
        step(2, b, biases=None if b else B - 1)
    with pe.Fori(3, NE - 1) as e:
        for b in range(B):
            step(e, b)
    for b in range(B):
        step(NE - 1, b)
        if b >= 2:
            after(b - 2)
    down(B * NE - 1, 1)


def split_w1(nc, act, m, f, e):
    act.wait_ge(f.w1_loaded, 16 * e + 16)
    for at in W1_PARTS:
        nc.scalar.activation(m.w[HI][:, at], m.w_raw[:, at], ACT.Copy).then_inc(f.w1_hi, 1)
    nc.scalar.activation(m.bias[:, :], m.b1[:, one(e), :], ACT.Copy).then_inc(f.bias_set, 1)


def expert_scalar(nc, act, m, f, g, a, first=nothing, mid=nothing, after=nothing):
    def step(e, b, n1, logits=False, gates=None, hook=nothing):
        s = B * e + b
        hook(b, OPEN)
        if b == 0 and n1:
            act.wait_ge(f.up_done, KH * s)
            split_w1(nc, act, m, f, e)
        if logits:
            act.wait_ge(g.lt_done, b + 1)
            nc.scalar.activation(m.lt[:, :], m.bank[3][0:2 * E, :], ACT.Copy).then_inc(g.lt_out, 1)
        act.wait_ge(f.bias_set, e + 1)
        for j in range(KH):
            act.wait_ge(f.up_done, KH * s + j + 1)
            ge(act, f.h_lo, KH * s - KH + j + 1)
            nc.scalar.activation(m.hid[:, j, :], m.bank[j][:, :], ACT.Gelu,
                                 bias=m.bias[:, j:j + 1]).then_inc(f.gelu_done, 1)
            act.wait_ge(f.gelu_done, KH * s + j + 1)
            if j == 0 and not (isinstance(e, int) and s < 2):
                act.wait_ge(f.y_done, NT * (s - 1))
            nc.scalar.activation(m.h[HI][:, b % 2, j, :], m.hid[:, j, :], ACT.Copy).then_inc(f.h_hi, 1)
            if j == 0 and gates is not None:
                act.wait_ge(g.gt_done, gates + 1)
                nc.scalar.activation(m.gt[:, :], m.bank[4][0:BIAS_ROWS, :], ACT.Copy).then_inc(g.gt_out, 1)
            hook(b, j)
        hook(b, 2)
        hook(b, 3)
        if b == 0:
            act.wait_ge(f.w2_loaded, 16 * e + 16)
            if n1:
                act.wait_ge(f.y_done, NT * s)
            else:
                act.wait_ge(a.y_done, NT * B * H)
            nc.scalar.activation(m.wo[HI][:, :, :], m.wo_raw[:, :].rearrange("p (k n) -> p k n", k=KH), ACT.Copy).then_inc(f.w2_hi, 1)
        if logits:
            act.wait_ge(g.chain, CHAIN * b + GAP)
            nc.scalar.activation(m.gap_exp[:, :], m.gap[:, :], ACT.Exp).then_inc(g.exp_done, 1)

    for b in range(B):
        step(0, b, False, hook=first)
    for b in range(B):
        step(1, b, True, logits=True, gates=b - 1 if b else None)
    for b in range(B):
        step(2, b, True, gates=None if b else B - 1)
    with act.Fori(3, NE - 1) as e:
        for b in range(B):
            step(e, b, True)
    for b in range(B):
        step(NE - 1, b, True, hook=lambda b, i: mid(b - 2) if b >= 2 and i == OPEN else None)
        if b >= 2:
            after(b - 2)


def expert_vector(nc, dve, m, f, g, first=nothing, mid=nothing, after=nothing):
    def add(u, b, e, tiles=range(NT)):
        for t in tiles:
            dve.wait_ge(f.y_done, NT * u + t + 1)
            xt = m.x[:, b * NT + t, :]
            nc.vector.scalar_tensor_tensor(out=xt, in0=m.bank[Y_BANK[t]][:, :], scalar=m.gates[:, b * NT + t, one(e)],
                                           in1=xt, op0=ALU.mult, op1=ALU.add).then_inc(f.y_added, 1)

    def step(e, b, n1, gates=False, hook=nothing):
        s = B * e + b
        hook(b, OPEN)
        for j in range(KH):
            dve.wait_ge(f.h_hi, KH * s + j + 1)
            nc.vector.tensor_tensor(m.h[LO][:, b % 2, j, :], m.hid[:, j, :], m.h[HI][:, b % 2, j, :].bitcast(F32),
                                    ALU.subtract).then_inc(f.h_lo, 1)
            hook(b, j)
        if gates:
            gate_vector(nc, dve, m, g, b)
        if n1:
            add(s - 1, (b - 1) % B, e if b else e - 1, (0, 1))
        hook(b, 2)
        if n1:
            add(s - 1, (b - 1) % B, e if b else e - 1, (2, 3))
        hook(b, 3)

    for b in range(B):
        step(0, b, b >= 1, hook=first)
    for b in range(B):
        step(1, b, True, gates=True)
    with dve.Fori(2, NE - 1) as e:
        for b in range(B):
            step(e, b, True)
    def last_hook(b, i):
        if b >= 2 and i == OPEN:
            dve.wait_ge(f.y_added, NT * (B * (NE - 1) + b - 1))
            mid(b - 2)

    for b in range(B):
        step(NE - 1, b, True, hook=last_hook)
        if b >= 2:
            after(b - 2)
    add(B * NE - 1, B - 1, NE - 1)


def expert_gpsimd(nc, pool, m, f):
    def expert(e):
        for part, at in enumerate(W1_PARTS):
            pool.wait_ge(f.w1_hi, 2 * e + part + 1)
            nc.gpsimd.tensor_tensor(m.w[LO][:, at], m.w_raw[:, at], m.w[HI][:, at].bitcast(F32),
                                    ALU.subtract).then_inc(f.w1_lo, 1)
        pool.wait_ge(f.w2_hi, e + 1)
        nc.gpsimd.tensor_tensor(m.wo[LO][:, :, :], m.wo_raw[:, :].rearrange("p (k n) -> p k n", k=KH),
                                m.wo[HI][:, :, :].bitcast(F32), ALU.subtract).then_inc(f.w2_lo, 1)

    expert(0)
    with pool.Fori(1, NE) as e:
        expert(e)


def expert_sync(nc, sp, m, f, a, w1, w2):
    def expert(e, first):
        if first:
            sp.wait_ge(a.w_lo, 3 * H)
            sp.wait_ge(a.wo_lo, H)
        else:
            sp.wait_ge(f.w1_lo, 2 * e)
        sp.dma_start(m.w_raw[:, 0:KD * HF], w1[one(e), :, :].rearrange("e p n -> p (e n)")).then_inc(f.w1_loaded, 16)
        if not first:
            sp.wait_ge(f.w2_lo, e)
        sp.dma_start(m.wo_raw[:, :], w2[one(e), :, :].rearrange("e p n -> p (e n)")).then_inc(f.w2_loaded, 16)

    expert(0, True)
    with sp.Fori(1, NE) as e:
        expert(e, False)




class NormSems:
    def __init__(self, sem):
        self.stats_done = sem("stats_done")
        self.moments_done = sem("moments_done")
        self.var_done = sem("var_done")
        self.root_done = sem("root_done")
        self.newton = sem("newton")
        self.normed = sem("normed")
        self.turned = sem("turned")
        self.xt_hi = sem("xt_hi")
        self.xt_lo = sem("xt_lo")


class AttendSems:
    def __init__(self, sem, mla):
        self.w_loaded = sem("w_loaded")
        self.wo_loaded = sem("wo_loaded")
        self.w_hi = sem("w_hi")
        self.w_lo = sem("w_lo")
        self.wo_hi = sem("wo_hi")
        self.wo_lo = sem("wo_lo")
        self.proj_done = sem("proj_done")
        self.q_hi = sem("q_hi")
        self.q_lo = sem("q_lo")
        self.k_hi = sem("k_hi")
        self.k_lo = sem("k_lo")
        self.v_hi = sem("v_hi")
        self.v_lo = sem("v_lo")
        self.scores_done = sem("scores_done")
        self.masked = sem("masked")
        self.probs_ready = sem("probs_ready")
        self.inverted = sem("inverted")
        self.pt_done = sem("pt_done")
        self.pt_hi = sem("pt_hi")
        self.pt_lo = sem("pt_lo")
        self.av_done = sem("av_done")
        self.o_hi = sem("o_hi")
        self.o_lo = sem("o_lo")
        self.y_done = sem("y_done")
        self.y_added = sem("y_added")
        self.projections = 2 if mla else 3
        if mla:
            self.combined = sem("combined")
            self.nope_out = sem("nope_out")
            self.rope_out = sem("rope_out")
            self.rope_added = sem("rope_added")
        else:
            self.vt_copied = sem("vt_copied")
            self.v_turned = sem("v_turned")


class LatentSems:
    def __init__(self, sem):
        self.w_loaded = sem("w_loaded")
        self.w_hi = sem("w_hi")
        self.w_lo = sem("w_lo")
        self.done = sem("done")
        self.hi = sem("hi")
        self.lo = sem("lo")
        self.wkva_loaded = sem("wkva_loaded")
        self.ckv_out = sem("ckv_out")
        self.tok_done = sem("tok_done")
        self.tok_out = sem("tok_out")
        self.rope_out = sem("rope_out")
        self.rope_added = sem("rope_added")
        self.rope_hi = sem("rope_hi")
        self.rope_lo = sem("rope_lo")


class GateSems:
    def __init__(self, sem):
        self.lt_done = sem("lt_done")
        self.lt_out = sem("lt_out")
        self.logits_done = sem("logits_done")
        self.chain = sem("chain")
        self.exp_done = sem("exp_done")
        self.gt_done = sem("gt_done")
        self.gt_out = sem("gt_out")


class ExpertSems:
    def __init__(self, sem):
        self.w1_loaded = sem("w1_loaded")
        self.w2_loaded = sem("w2_loaded")
        self.w1_hi = sem("w1_hi")
        self.w1_lo = sem("w1_lo")
        self.w2_hi = sem("w2_hi")
        self.w2_lo = sem("w2_lo")
        self.bias_set = sem("bias_set")
        self.up_done = sem("up_done")
        self.gelu_done = sem("gelu_done")
        self.h_hi = sem("h_hi")
        self.h_lo = sem("h_lo")
        self.y_done = sem("y_done")
        self.y_added = sem("y_added")


class Buffers:
    pass


def program(nc, x_in, wa, woa, wqa, wkva, wb, wob, rope, gate, w1, b1, w2, b2, out):
    with ExitStack() as ctx:
        def sb(name, shape, dt=F32):
            return ctx.enter_context(nc.sbuf_tensor(name, shape, dt))

        def pair(name, shape):
            return [sb(name + "_hi", shape, F32R), sb(name + "_lo", shape, F32R)]

        def named(prefix):
            return lambda name: ctx.enter_context(nc.semaphore(f"{prefix}_{name}"))

        m = Buffers()
        m.x = sb("x", [P, B * NT, D])
        m.xT = pair("xT", [P, B, KD, S])
        m.ident = sb("ident", [P, P])
        m.mask = sb("mask", [P, S])
        m.w_raw = sb("w_raw", [P, 1536])
        m.w = pair("w", [P, 1536])
        m.wo_raw = sb("wo_raw", [P, 2 * D])
        m.wo = pair("wo", [P, 2, D])
        m.wo1 = [w[:, :, :].rearrange("p a n -> p (a n)") for w in m.wo]
        m.hq = pair("hq", [P, 2, KH, S])
        m.h = m.hq
        m.q = [t[:, 0, 0, :] for t in m.hq]
        m.k = [t[:, 0, 1, :] for t in m.hq]
        m.v = [t[:, 1, 0, :] for t in m.hq]
        m.o = [t[:, 1, 1, :] for t in m.hq]
        m.s = sb("s", [P, S_COLS])
        m.hid = m.s[:, 0:KH * S].rearrange("p (k n) -> p k n", k=KH)
        m.xn = sb("xn", [P, 2, D])
        m.pt_hi = sb("pt_hi", [P, PT_COLS], F32R)
        m.pt_lo = sb("pt_lo", [P, PT_COLS], F32R)
        m.top = sb("top", [P, B, NT])
        m.rowsum = sb("rowsum", [P, B, NT])
        m.inv = sb("inv", [P, B, NT])
        m.stats = sb("stats", [P, B, NT, 6])
        m.moments = sb("moments", [P, B, NT, 2])
        m.var, m.root, m.rstd0, m.rstd = (sb(n, [P, B, NT]) for n in ("var", "root", "rstd0", "rstd"))
        m.newt = sb("newt", [P, B, 3, NT])
        m.ckv = pair("ckv", [P, B, S])
        m.ckv32 = m.s[:, 0:S]
        m.ctok = sb("ctok", [P, B, S])
        m.rope = sb("rope", [P, 2, S])
        m.qf, m.ra, m.rb = (sb(n, [P, S]) for n in ("qf", "ra", "rb"))
        m.vt = m.qf
        m.gw_raw = sb("gw_raw", [P, KD, E])
        m.gw = sb("gw", [P, KD, 2 * E], F32R)
        m.b1 = sb("b1", [P, NE, KH])
        m.bias = sb("bias", [P, KH])
        m.b2 = sb("b2", [BIAS_ROWS, D], F32R)
        m.b2_raw = m.ctok[0:BIAS_ROWS, 0, :]
        m.lt = m.ctok[0:2 * E, 1, :]
        m.gt = m.pt_hi[0:BIAS_ROWS, 0:S]
        m.packed = sb("packed", [P, NT, BIAS_ROWS], F32R)
        m.gates = sb("gates", [P, B * NT, NE])
        m.ramp, m.logits, m.pick1, m.pick2 = (sb(n, [P, NT, E]) for n in ("ramp", "logits", "pick1", "pick2"))
        m.top1, m.top2, m.rank, m.gap, m.gap_exp = (sb(n, [P, NT]) for n in ("top1", "top2", "rank", "gap", "gap_exp"))
        m.bank = [ctx.enter_context(nc.psum_tensor(f"bank{i}", [P, 512], F32)) for i in range(8)]

        m.const_set = ctx.enter_context(nc.semaphore("const_set"))
        x_loaded = [ctx.enter_context(nc.semaphore(f"x_loaded{b}")) for b in range(B)]
        x0_loaded = [ctx.enter_context(nc.semaphore(f"x0_loaded{t}")) for t in range(NT)]
        small_loaded, m.gw_split, m.b2_split, stored = (
            ctx.enter_context(nc.semaphore(n)) for n in ("small_loaded", "gw_split", "b2_split", "stored"))
        SMALL = 16 * 5
        n = NormSems(named("norm"))
        a1, a2 = AttendSems(named("attn"), False), AttendSems(named("mla"), True)
        lat = LatentSems(named("latent"))
        g = [GateSems(named(f"gate{i}")) for i in range(2)]
        f = [ExpertSems(named(f"expert{i}")) for i in range(2)]
        A_END, F_END = NT * B * H, NT * B * NE

        block = ctx.enter_context(nc.Block())

        @block.sync
        def _(sp):
            def load_x(b):
                sp.dma_start(m.x[:, b * NT:(b + 1) * NT, :],
                             x_in[b, :, :].rearrange("(t p) d -> p t d", p=P)).then_inc(x_loaded[b], 16)

            for t in range(NT):
                sp.dma_start(m.x[:, t, :], x_in[0, t * P:(t + 1) * P, :]).then_inc(x0_loaded[t], 16)
            load_head(sp, m, a1, wa, woa, 0)
            for b in range(1, B):
                load_x(b)
            sp.dma_start(m.gw_raw[:, :, :], gate).then_inc(small_loaded, 16)
            sp.dma_start(m.b1[:, :, :], b1).then_inc(small_loaded, 16)
            sp.dma_start(m.b2_raw, b2).then_inc(small_loaded, 16)
            sp.dma_start(m.rope[HALF:P, 0, :], rope[0, :, :]).then_inc(small_loaded, 16)
            sp.dma_start(m.rope[HALF:P, 1, :], rope[1, :, :]).then_inc(small_loaded, 16)
            attend_sync(nc, sp, m, a1, False, wa, woa)
            expert_sync(nc, sp, m, f[0], a1, w1, w2)
            sp.wait_ge(f[0].w1_lo, 2 * NE)
            sp.dma_start(m.w_raw[:, :], wqa).then_inc(lat.w_loaded, 16)
            sp.wait_ge(f[0].w2_lo, NE)
            sp.dma_start(m.wo_raw[:, 0:768], wkva).then_inc(lat.wkva_loaded, 16)
            sp.wait_ge(lat.w_lo, 2)
            load_head(sp, m, a2, wb, wob, 0)
            attend_sync(nc, sp, m, a2, True, wb, wob)
            expert_sync(nc, sp, m, f[1], a2, w1, w2)
            for b in range(B - 1):
                sp.wait_ge(f[1].y_added, F_END - NT * (B - 1 - b))
                sp.dma_start(out[b, :, :].rearrange("(t p) d -> p t d", p=P),
                             m.x[:, b * NT:(b + 1) * NT, :]).then_inc(stored, 16)
            for t in range(NT):
                sp.wait_ge(f[1].y_added, F_END - NT + t + 1)
                sp.dma_start(out[B - 1, t * P:(t + 1) * P, :], m.x[:, (B - 1) * NT + t, :]).then_inc(stored, 16)
            sp.wait_ge(stored, 16 * (B - 1 + NT))

        @block.gpsimd
        def _(pool):
            constants(nc, pool, m)
            attend_gpsimd(nc, pool, m, a1, False)
            pool.wait_ge(m.gw_split, 1)
            nc.gpsimd.tensor_tensor(m.gw[:, :, E:2 * E], m.gw_raw[:, :, :], m.gw[:, :, 0:E].bitcast(F32),
                                    ALU.subtract).then_inc(m.gw_split, 1)
            expert_gpsimd(nc, pool, m, f[0])
            latent_gpsimd(nc, pool, m, lat, a2, lambda: [rest_weights(nc, pool, m, a2, True, 0, part) for part in range(3)])
            attend_gpsimd(nc, pool, m, a2, True)
            pool.wait_ge(a2.q_lo, B * H)
            expert_gpsimd(nc, pool, m, f[1])


        places = {(1, i): (0, i) for i in range(NT)}
        places.update({(2, t): (1, t // 2) for t in range(NT)})
        places.update({(3, t): (1, 2 + t // 2) for t in range(NT)})
        later = dict(zip([(2, t) for t in range(NT)] + [(3, t) for t in range(NT)],
                         [(0, 3), (1, 0), (1, 1), (1, 2), (1, 3), (2, 0), (2, 1), (2, 2)]))

        def woven(r, stats, start, tile):
            def first(b, i):
                if r == 0:
                    if b == 0 and i == OPEN:
                        stats(1)
                        start(1)
                elif i == OPEN and b < 2:
                    stats(b + 2)
                    if b == 0:
                        start(2)
                for (batch, t), place in (later if r else places).items():
                    if place == (b, i):
                        tile(batch, t)
                        if t == NT - 1 and (batch == 2 or r == 0 and batch == 1):
                            start(batch + 1)
                if r == 0 and b == 0 and i >= 2:
                    stats(i)
            return first

        @block.scalar
        def _(act):
            def root(r):
                return lambda b: norm_root_scalar(nc, act, m, n, r, b)

            def tile(r):
                return lambda b, t: norm_tile_scalar(nc, act, m, n, r, b, t)

            def tiles(r):
                return lambda b: [tile(r)(b, t) for t in range(NT)]

            def behind_attention(r, a, e):
                def after(i):
                    if i == 0:
                        act.wait_ge(a.proj_done, a.projections * B * H)
                        split_w1(nc, act, m, e, 0)
                    tiles(r)(i)
                return after

            root(0)(0)
            tiles(0)(0)
            attend_scalar(nc, act, m, a1, False, nothing, woven(0, root(0), nothing, tile(0)), root(1), behind_attention(1, a1, f[0]))
            act.wait_ge(small_loaded, SMALL)
            nc.scalar.activation(m.gw[:, :, 0:E], m.gw_raw[:, :, :], ACT.Copy).then_inc(m.gw_split, 1)
            nc.scalar.activation(m.b2[:, :], m.b2_raw, ACT.Copy).then_inc(m.b2_split, 1)
            expert_scalar(nc, act, m, f[0], g[0], a1, woven(1, root(1), nothing, tile(1)), root(2), tiles(2))
            latent_scalar(nc, act, m, lat, f[0], woven(2, root(2), nothing, tile(2)),
                          lambda: [split_weights(nc, act, m, a2, True, 0, part, False) for part in range(3)])
            attend_scalar(nc, act, m, a2, True, lambda i: act.wait_ge(lat.done, (KQ + 2) * B), nothing, root(3),
                          behind_attention(3, a2, f[1]))
            expert_scalar(nc, act, m, f[1], g[1], a2, woven(3, root(3), nothing, tile(3)))

        @block.vector
        def _(dve):
            def stats(r):
                def measured(b):
                    if r == 0 and b:
                        dve.wait_ge(x_loaded[b], 16)
                    norm_stats_vector(nc, dve, m, n, r, b, x0_loaded if r == b == 0 else None)
                return measured

            def start(r):
                return lambda b: norm_start_vector(nc, dve, m, n, r, b)

            def both(r):
                def begun(b):
                    stats(r)(b)
                    start(r)(b)
                return begun

            def tile(r):
                return lambda b, t: norm_tile_vector(nc, dve, m, n, r, b, t)

            def tiles(r):
                def after(b):
                    for t in range(NT):
                        tile(r)(b, t)
                return after

            both(0)(0)
            tiles(0)(0)
            dve.wait_ge(m.const_set, CONSTS)
            attend_vector(nc, dve, m, a1, False, woven(0, stats(0), start(0), tile(0)), both(1), tiles(1))
            dve.wait_ge(m.b2_split, 1)
            second = slice(GROUP, GROUP + E + 1)
            nc.vector.tensor_tensor(m.b2[second, :], m.b2_raw[second, :], m.b2[second, :].bitcast(F32),
                                    ALU.subtract).then_inc(m.b2_split, 1)
            expert_vector(nc, dve, m, f[0], g[0], woven(1, stats(1), start(1), tile(1)), both(2), tiles(2))
            latent_vector(nc, dve, m, lat, woven(2, stats(2), start(2), tile(2)))
            dve.wait_ge(small_loaded, SMALL)
            dve.wait_ge(lat.rope_added, B)
            attend_vector(nc, dve, m, a2, True, nothing, both(3), tiles(3))
            expert_vector(nc, dve, m, f[1], g[1], woven(3, stats(3), start(3), tile(3)))

        @block.tensor
        def _(pe):
            def tile(r):
                return lambda b, t: norm_tile_tensor(nc, pe, m, n, r, b, t)

            def ready(r):
                return lambda b: pe.wait_ge(n.xt_lo, NT * (B * r + b + 1))

            def ready_and_banks(b):
                ready(0)(b if b < 2 else B - 1)

            def behind(r, bank_free):
                def after(i):
                    if i == 0:
                        bank_free()
                    for t in range(NT):
                        tile(r)(i, t)
                return after

            def latents_ready(b):
                last = b if b == 0 else B - 1
                pe.wait_ge(lat.lo, (KQ + 1) * (last + 1))
                pe.wait_ge(lat.rope_lo, last + 1)

            def a1_banks():
                pe.wait_ge(a1.vt_copied, B * H)
                pe.wait_ge(a1.v_lo, B * H)

            def a2_banks():
                pe.wait_ge(a2.nope_out, B * H)
                pe.wait_ge(a2.rope_out, B * H)
                pe.wait_ge(a2.k_lo, B * H)

            pe.wait_ge(m.const_set, CONSTS)
            for t in range(NT):
                tile(0)(0, t)
            attend_tensor(nc, pe, m, a1, False, ready_and_banks, woven(0, nothing, nothing, tile(0)), behind(1, a1_banks))
            expert_tensor(nc, pe, m, f[0], g[0], ready(1), woven(1, nothing, nothing, tile(1)),
                          behind(2, lambda: pe.wait_ge(g[0].gt_out, B)))
            latent_tensor(nc, pe, m, lat, f[0], ready(2), woven(2, nothing, nothing, tile(2)))
            attend_tensor(nc, pe, m, a2, True, latents_ready, nothing, behind(3, a2_banks))
            expert_tensor(nc, pe, m, f[1], g[1], ready(3), woven(3, nothing, nothing, tile(3)))


def kernel(**inputs):
    import concourse.bacc as bacc
    from concourse.bass_utils import run_bass_kernel_spmd

    def arr(name):
        return np.asarray(inputs[name])

    def tiles(w, cols):
        return w.reshape(-1, P, cols).transpose(1, 0, 2)

    c = np.ascontiguousarray
    w_in = arr("L0_attn_a_w_in").reshape(H, 3, DH, KD, P).transpose(0, 4, 1, 3, 2).reshape(H, P, 3 * KD * DH)
    wo_a = arr("L0_attn_a_w_out").T.reshape(H, DH, D)
    turned = np.concatenate([np.arange(0, HALF, 2), np.arange(1, HALF, 2)])
    order = np.concatenate([np.arange(HALF), HALF + turned])
    wqb = arr("L0_attn_b_Wqb").reshape(KQ, P, H, DH)[:, :, :, order].transpose(2, 1, 0, 3).reshape(H, P, KQ * DH)
    wkvb = arr("L0_attn_b_Wkvb").reshape(P, H, HALF + DH)
    wb = np.concatenate([wqb, wkvb[:, :, :HALF].transpose(1, 0, 2), wkvb[:, :, HALF:].transpose(1, 2, 0)], axis=2)
    wkva = arr("L0_attn_b_Wkva")[:, np.concatenate([np.arange(P), P + turned])]
    wob = arr("L0_attn_b_Wo").reshape(H, DH, D)
    sw1, sb1, sw2 = arr("L0_ffn_shared_w1"), arr("L0_ffn_shared_b1"), arr("L0_ffn_shared_w2")
    w1 = np.concatenate([sw1.reshape(D, 2, HF).transpose(1, 0, 2), arr("L0_ffn_w1")])
    w1 = w1.reshape(NE, KD, P, HF).transpose(0, 2, 1, 3).reshape(NE, P, KD * HF)
    b1 = np.concatenate([sb1.reshape(2, HF), arr("L0_ffn_b1")]).reshape(NE, KH, P).transpose(2, 0, 1)
    w2 = np.concatenate([sw2.reshape(2, HF, D), arr("L0_ffn_w2")])
    w2 = w2.reshape(NE, KH, P, D).transpose(0, 2, 1, 3).reshape(NE, P, KH * D)
    b2 = np.concatenate([arr("L0_ffn_shared_b2")[None], arr("L0_ffn_b2")])
    b2 = np.tile(np.concatenate([b2, np.zeros((GROUP - E - 1, D), np.float32)]), (3, 1))
    inv_freq = (1.0 / np.float32(10000.0) ** (np.arange(QUARTER, dtype=np.float32) * np.float32(2.0 / HALF))).astype(np.float32)
    freqs = inv_freq[:, None] * np.arange(S, dtype=np.float32)[None, :]
    rope = np.stack([np.concatenate([np.cos(freqs), np.cos(freqs)]), np.concatenate([np.sin(freqs), -np.sin(freqs)])]).astype(np.float32)
    arrays = {
        "x_in": c(arr("L0_attn_a_x")), "wa": c(w_in), "woa": c(wo_a),
        "wqa": c(tiles(arr("L0_attn_b_Wqa"), 384).reshape(P, -1)), "wkva": c(tiles(wkva, 192).reshape(P, -1)),
        "wb": c(wb), "wob": c(wob), "rope": c(rope), "gate": c(tiles(arr("L0_ffn_gate_w"), E)),
        "w1": c(w1), "b1": c(b1), "w2": c(w2), "b2": c(b2),
    }
    nc = bacc.Bacc("TRN2", target_bir_lowering=False, num_devices=1)
    args = [nc.dram_tensor("dram_" + k, v.shape, mybir.dt.from_np(v.dtype), kind="ExternalInput").ap() for k, v in arrays.items()]
    args.append(nc.dram_tensor("dram_out", (B, S, D), F32, kind="ExternalOutput").ap())
    program(nc, *args)
    r = run_bass_kernel_spmd(nc, [{"dram_" + k: v for k, v in arrays.items()}], core_ids=[0])
    return r.results[0]["dram_out"]
```

```python
from contextlib import ExitStack

import numpy as np
import concourse.bass as bass
from concourse import mybir

F32 = mybir.dt.float32
F32R = mybir.dt.float32r
ALU = mybir.AluOpType
ACT = mybir.ActivationFunctionType
AX = mybir.AxisListType

P = 128
D = 512
KD = D // P
B = 4
S = 512
NT = S // P
H = 16
DH = 128
HALF = 64
QUARTER = 32
KQ = 3
E = 8
NE = E + 2
HF = 256
KH = HF // P
SCALE = float(DH) ** -0.5
EPS = 1e-5
BIG = 1.0e30
FLT_MAX = 3.0e38
HI, LO = 0, 1

PT_MOV = [(0, 0, 512), (512, 128, 384), (1152, 256, 256), (896, 256, 256)]
PT_ZERO = 896
PT_COLS = 1408
S_AT = [0, 128, 384, 768]
S_COLS = 1280


def product(nc, out, hi, lo, mov_hi, mov_lo, first, last):
    nc.tensor.matmul(out, hi, mov_hi, start=first, stop=False)
    nc.tensor.matmul(out, hi, mov_lo, start=False, stop=False)
    return nc.tensor.matmul(out, lo, mov_hi, start=False, stop=last)



def constants(nc, pool, m):
    nc.gpsimd.memset(m.ident[:, :], 0.0).then_inc(m.const_set, 1)
    nc.gpsimd.memset(m.mask[:, :], 0.0).then_inc(m.const_set, 1)
    nc.gpsimd.memset(m.pt_hi[:, PT_ZERO:PT_ZERO + P].bitcast(F32), 0.0).then_inc(m.const_set, 1)
    nc.gpsimd.memset(m.pt_lo[:, PT_ZERO:PT_ZERO + P].bitcast(F32), 0.0).then_inc(m.const_set, 1)
    for e in range(E):
        nc.gpsimd.memset(m.ramp[:, :, e:e + 1], float(E - e)).then_inc(m.const_set, 1)
    nc.gpsimd.memset(m.gates[:, :, 0:2], 1.0).then_inc(m.const_set, 1)
    pool.wait_ge(m.const_set, 2)
    nc.gpsimd.affine_select(out=m.ident[:, :], in_=m.ident[:, :], compare_op=ALU.not_equal, fill=1.0,
                            base=0, pattern=[[-1, P]], channel_multiplier=1).then_inc(m.const_set, 1)
    tri = m.mask[:, S - P:S]
    nc.gpsimd.affine_select(out=tri, in_=tri, compare_op=ALU.is_ge, fill=-BIG,
                            base=0, pattern=[[-1, P]], channel_multiplier=1).then_inc(m.const_set, 1)


CONSTS = 4 + E + 1 + 2



def norm_bank(m, r, t):
    return m.bank[(6 if r == 0 else 3) + t % 2]


def norm_stats_vector(nc, dve, m, n, r, b, tile_loaded=None):
    c = B * r + b
    for t in range(NT):
        if tile_loaded:
            dve.wait_ge(tile_loaded[t], 16)
        nc.vector.bn_stats(m.stats[:, b, t, :], m.x[:, b * NT + t, :]).then_inc(n.stats_done, 1)
    for t in range(NT):
        dve.wait_ge(n.stats_done, c * NT + t + 1)
        nc.vector.bn_aggr(m.moments[:, b, t, :], m.stats[:, b, t, :]).then_inc(n.moments_done, 1)
    dve.wait_ge(n.moments_done, NT * (c + 1))
    nc.vector.tensor_scalar_add(m.var[:, b, :], m.moments[:, b, :, 1], EPS).then_inc(n.var_done, 1)

    square, product_, factor = (m.newt[:, b, i, :] for i in range(3))
    dve.wait_ge(n.root_done, c + 1)
    nc.vector.reciprocal(m.rstd0[:, b, :], m.root[:, b, :]).then_inc(n.newton, 1)
    dve.wait_ge(n.newton, 5 * c + 1)
    nc.vector.tensor_tensor(square, m.rstd0[:, b, :], m.rstd0[:, b, :], ALU.mult).then_inc(n.newton, 1)
    dve.wait_ge(n.newton, 5 * c + 2)
    nc.vector.tensor_tensor(product_, square, m.var[:, b, :], ALU.mult).then_inc(n.newton, 1)
    dve.wait_ge(n.newton, 5 * c + 3)
    nc.vector.tensor_scalar(factor, product_, -0.5, 1.5, ALU.mult, ALU.add).then_inc(n.newton, 1)
    dve.wait_ge(n.newton, 5 * c + 4)
    nc.vector.tensor_tensor(m.rstd[:, b, :], m.rstd0[:, b, :], factor, ALU.mult).then_inc(n.newton, 1)
    dve.wait_ge(n.newton, 5 * c + 5)


def normalise(nc, dve, m, n, r, b, t):
    done = NT * (B * r + b) + t
    if done >= 2:
        dve.wait_ge(n.turned, done - 1)
    nc.vector.tensor_scalar(m.xn[:, t % 2, :], m.x[:, b * NT + t, :], m.moments[:, b, t, 0:1],
                            m.rstd[:, b, t:t + 1], ALU.subtract, ALU.mult).then_inc(n.normed, 1)


def norm_start_vector(nc, dve, m, n, r, b):
    normalise(nc, dve, m, n, r, b, 0)
    normalise(nc, dve, m, n, r, b, 1)


def norm_tile_vector(nc, dve, m, n, r, b, t):
    if t + 2 < NT:
        normalise(nc, dve, m, n, r, b, t + 2)
    dve.wait_ge(n.xt_hi, NT * (B * r + b) + t + 1)
    at = (slice(None), b, slice(None), slice(t * P, t * P + P))
    nc.vector.tensor_tensor(m.xT[LO][at], norm_bank(m, r, t)[:, :].rearrange("p (k n) -> p k n", k=KD),
                            m.xT[HI][at].bitcast(F32), ALU.subtract).then_inc(n.xt_lo, 1)


def norm_root_scalar(nc, act, m, n, r, b):
    act.wait_ge(n.var_done, B * r + b + 1)
    nc.scalar.activation(m.root[:, b, :], m.var[:, b, :], ACT.Sqrt).then_inc(n.root_done, 1)


def norm_tile_scalar(nc, act, m, n, r, b, t):
    act.wait_ge(n.turned, NT * (B * r + b) + t + 1)
    nc.scalar.activation(m.xT[HI][:, b, :, t * P:t * P + P],
                         norm_bank(m, r, t)[:, :].rearrange("p (k n) -> p k n", k=KD),
                         ACT.Copy).then_inc(n.xt_hi, 1)


def norm_tile_tensor(nc, pe, m, n, r, b, t):
    done = NT * (B * r + b) + t
    pe.wait_ge(n.normed, done + 1)
    if done >= 2:
        pe.wait_ge(n.xt_lo, done - 1)
    for k in range(KD):
        last = nc.tensor.transpose(norm_bank(m, r, t)[:, k * P:k * P + P],
                                   m.xn[:, t % 2, k * P:k * P + P], m.ident[:, :])
    last.then_inc(n.turned, 1)


OPEN = -1


def nothing(*_):
    pass



def scores_of(m, t):
    n = max(256, (t + 1) * P)
    return m.bank[max(t - 1, 0)][:, (256 if t == 1 else 0):(256 if t == 1 else 0) + n], n


def over_heads(eng, mla, steps):
    steps(0, 0)
    if mla:
        with eng.Fori(1, H - 1) as h:
            steps(h, None)
        steps(H - 1, None)
        return
    steps(1, 1)
    with eng.Fori(1, H // 2 - 1) as pair:
        steps(2 * pair, 0)
        steps(2 * pair + 1, 1)
    steps(H - 2, 0)
    steps(H - 1, 1)


def slot_of(h, odd):
    return h % 2 if odd is None else odd


def before(h, odd):
    return h - 1, None if odd is None else 1 - odd


def values_of(m, odd, b):
    return (m.ckv[HI][:, b, :], m.ckv[LO][:, b, :]) if odd else (m.v[HI][:, :], m.v[LO][:, :])


def pair_values(h, odd, b):
    return 8 * (h - odd) + 4 * b + 4


def value_weights(m, part):
    if part == 0:
        return m.w[HI][:, 1024:1536], m.w[LO][:, 1024:1536]
    return m.vw2[HI][:, :], m.vw2[LO][:, :]


def values_bank(m, half, odd):
    return m.bank[3 + half][:, :].rearrange("p (t n) -> p t n", t=2)[:, :, odd * DH:odd * DH + DH]


def values_part(values, half):
    return values[:, half * 2 * DH:(half + 1) * 2 * DH].rearrange("p (t n) -> p t n", t=2)


def attend_tensor(nc, pe, m, a, mla, input_ready, first=nothing, after=nothing):
    parts = a.parts

    def keys(b):
        return (m.xT[HI][:, b, KQ, :], m.xT[LO][:, b, KQ, :]) if mla else (m.k[HI][:, :], m.k[LO][:, :])

    def scores(u, b):
        pe.wait_ge(a.q_lo, u + 1)
        pe.wait_ge(a.k_lo, u + 1)
        k_hi, k_lo = keys(b)
        for t in range(NT):
            out, n = scores_of(m, t)
            at = slice(t * P, t * P + P)
            product(nc, out, m.q[HI][:, at], m.q[LO][:, at], k_hi[:, 0:n], k_lo[:, 0:n],
                    True, True).then_inc(a.scores_done, 1)

    def turn(u):
        pe.wait_ge(a.probs_ready, NT * (u + 1))
        for group in ((0,), (1,), (3, 2)):
            col = 0
            for j in group:
                for t in range(j, NT):
                    last = nc.tensor.transpose(m.bank[min(j, 2)][:, col:col + P],
                                               m.s[:, S_AT[t] + j * P:S_AT[t] + j * P + P], m.ident[:, :])
                    col += P
            last.then_inc(a.pt_done, 1)

    def times_v(u, h, odd, b):
        pe.wait_ge(a.v_lo, u + 1 if mla else pair_values(h, odd, b))
        v_hi, v_lo = values_of(m, odd and not mla, b)
        for j in range(NT):
            if j < 3:
                pe.wait_ge(a.pt_lo, 3 * u + j + 1)
            src, q0, n = PT_MOV[j]
            at = slice(j * DH, j * DH + DH)
            last = product(nc, m.bank[5][:, q0:q0 + n], v_hi[:, at], v_lo[:, at],
                           m.pt_hi[:, src:src + n], m.pt_lo[:, src:src + n], j == 0, j == NT - 1)
        last.then_inc(a.av_done, 1)

    def output(v, slot, tiles):
        if tiles[0] == 0:
            pe.wait_ge(a.o_lo, v + 1)
        for t in tiles:
            ge(pe, a.y_added, NT * v + t - 1)
            at = slice(t * P, t * P + P)
            product(nc, m.bank[6 + t % 2][:, :], m.o[HI][:, at], m.o[LO][:, at],
                    m.wo[HI][:, slot, :], m.wo[LO][:, slot, :], True, True).then_inc(a.y_done, 1)

    def project_q(s, h, odd, b):
        if b == 0:
            pe.wait_ge(a.w_lo, parts * h + 1)
        if mla:
            ge(pe, a.nope_out, s)
            ge(pe, a.rope_out, s)
            if b == 1:
                pe.wait_ge(a.wo_lo, h + 1)
        elif odd and b == 0:
            pe.wait_ge(a.v_lo, pair_values(h, odd, B - 1) - 2)
        elif not odd and b:
            pe.wait_ge(a.v_lo, pair_values(h, odd, b - 1) - 2)
        kn = KQ if mla else KD
        for k in range(kn):
            at = slice(k * DH, k * DH + DH)
            last = product(nc, m.bank[3][:, :], m.w[HI][:, at], m.w[LO][:, at],
                           m.xT[HI][:, b, k, :], m.xT[LO][:, b, k, :], k == 0, k == kn - 1)
        last.then_inc(a.proj_done, 1)

    def project_k(s, h, odd, b):
        if b == 0:
            pe.wait_ge(a.w_lo, parts * h + 2)
        if mla:
            ge(pe, a.k_lo, s)
        elif odd and b == 0:
            pe.wait_ge(a.v_lo, pair_values(h, odd, B - 1))
        elif not odd and b:
            pe.wait_ge(a.v_lo, pair_values(h, odd, b - 1))
        if mla:
            last = product(nc, m.bank[4][0:HALF, :], m.w[HI][:, 512:512 + HALF], m.w[LO][:, 512:512 + HALF],
                           m.ckv[HI][:, b, :], m.ckv[LO][:, b, :], True, True)
        else:
            for k in range(KD):
                at = slice(512 + k * DH, 512 + k * DH + DH)
                last = product(nc, m.bank[4][:, :], m.w[HI][:, at], m.w[LO][:, at],
                               m.xT[HI][:, b, k, :], m.xT[LO][:, b, k, :], k == 0, k == KD - 1)
        last.then_inc(a.proj_done, 1)

    def project_v(s, h, b, half):
        pe.wait_ge(a.k_lo if half else a.q_lo, s + 1)
        for i in range(2):
            t = 2 * half + i
            for k in range(KD):
                if b == 0 and half == 0 and i == 0 and k % 2 == 0:
                    pe.wait_ge(a.vw_lo, h + 1 + k // 2)
                w_hi, w_lo = value_weights(m, k // 2)
                at = slice(k % 2 * 2 * DH, (k % 2 + 1) * 2 * DH)
                last = product(nc, m.bank[3 + half][:, i * 2 * DH:(i + 1) * 2 * DH],
                               m.xT[HI][:, b, k, t * P:t * P + P], m.xT[LO][:, b, k, t * P:t * P + P],
                               w_hi[:, at], w_lo[:, at], k == 0, k == KD - 1)
        last.then_inc(a.v_done, 1)

    def combine(s, h):
        pe.wait_ge(a.w_lo, parts * h + 3)
        pe.wait_ge(a.nope_out, s + 1)
        pe.wait_ge(a.rope_out, s + 1)
        product(nc, m.bank[3][:, :], m.w[HI][:, 576:576 + DH], m.w[LO][:, 576:576 + DH],
                m.w[HI][:, 1024:1536], m.w[LO][:, 1024:1536], True, True).then_inc(a.combined, 1)

    def step(h, odd, b, n1, n2, new=True, hook=nothing):
        s = 4 * h + b
        u, v = s - 1, s - 2
        bu, slot = (b - 1) % B, slot_of(*((h, odd) if b >= 2 else before(h, odd)))
        if mla and isinstance(h, int) and h == 0:
            input_ready(b)
        if n1:
            scores(u, bu)
        if not mla and isinstance(h, int) and h == 0:
            input_ready(b)
        if new and mla:
            project_q(s, h, odd, b)
        if n2:
            if b == 2:
                pe.wait_ge(a.wo_lo, h + 1)
            output(v, slot, (0, 1))
        if new and not mla:
            project_q(s, h, odd, b)
        hook(b, 0)
        if n1:
            turn(u)
        if new:
            project_k(s, h, odd, b)
            hook(b, 1)
            if not mla:
                if not odd:
                    project_v(s, h, b, 0)
                hook(b, 2)
            elif b == 0:
                combine(s, h)
        if n2 and mla:
            output(v, slot, (2, 3))
        if n1:
            times_v(u, *((h, odd) if b else before(h, odd)), bu)
        if n2 and not mla:
            output(v, slot, (2, 3))
        if new and not mla and not odd:
            project_v(s, h, b, 1)
        hook(b, 3)

    def steps(h, odd):
        begins = isinstance(h, int) and h == 0
        for b in range(B):
            step(h, odd, b, b >= 1 or not begins, b >= 2 or not begins, hook=first if begins else nothing)

    over_heads(pe, mla, steps)
    after(0)
    step(H, 0, 0, True, True, new=False)
    after(1)
    step(H, 0, 1, False, True, new=False)


def split_weights(nc, act, m, a, mla, h, part, again, free=nothing):
    parts, proj = weight_parts(mla), a.projections
    if part == 0:
        act.wait_ge(a.w_loaded, 16 * h + 16)
        if again:
            act.wait_ge(a.proj_done, proj * B * h - (1 if mla else 0))
        else:
            free(0)
    if mla and part == 1 and again:
        act.wait_ge(a.proj_done, proj * B * h)
    src, dst = parts[part]
    if mla and part == 2:
        act.wait_ge(a.wo_loaded, 16 * h + 16)
        if again:
            act.wait_ge(a.combined, h)
        nc.scalar.activation(m.w[HI][:, dst[0]:dst[1]], m.wo_raw[:, 0:D], ACT.Copy).then_inc(a.w_hi, 1)
    else:
        nc.scalar.activation(m.w[HI][:, dst[0]:dst[1]], m.w_raw[:, src[0]:src[1]], ACT.Copy).then_inc(a.w_hi, 1)


def attend_scalar(nc, act, m, a, mla, free, first=nothing, mid=nothing, after=nothing):
    proj = a.projections

    def split_w(h, part, again):
        split_weights(nc, act, m, a, mla, h, part, again, free)

    def split_wo(h, odd, again):
        act.wait_ge(a.wo_loaded, 16 * h + 16)
        if again:
            act.wait_ge(a.y_done, 16 * h - 8)
        else:
            free(1)
        nc.scalar.activation(m.wo[HI][:, one(odd), :], m.wo_raw[:, 0:D].rearrange("p (a n) -> p a n", a=1),
                             ACT.Copy).then_inc(a.wo_hi, 1)

    def split_vw(h, again):
        act.wait_ge(a.vw_loaded, 8 * h + 16)
        if again:
            act.wait_ge(a.v_done, 4 * h)
        for part in range(2):
            nc.scalar.activation(value_weights(m, part)[HI], m.vw_raw[:, part, :], ACT.Copy).then_inc(a.vw_hi, 1)

    def exps(u, b):
        for t in range(NT):
            act.wait_ge(a.masked, NT * u + t + 1)
            at = m.s[:, S_AT[t]:S_AT[t] + (t + 1) * P]
            nc.scalar.activation(at, at, ACT.Exp, bias=m.top[:, b, t:t + 1], scale=-1.0,
                                 accum_out=m.rowsum[:, b, t:t + 1]).then_inc(a.probs_ready, 1)

    def probs_hi(u):
        for g, (dst, n, src) in enumerate(((0, 512, 0), (512, 384, 1), (1024, 384, 2))):
            act.wait_ge(a.pt_done, 3 * u + g + 1)
            nc.scalar.activation(m.pt_hi[:, dst:dst + n], m.bank[src][:, 0:n], ACT.Copy).then_inc(a.pt_hi, 1)

    def step(h, odd, b, n1, new=True, mid=None, hook=nothing):
        s = 4 * h + b
        u, bu = s - 1, (b - 1) % B
        fresh = new and b == 0 and not mla
        ahead = mla and new and b == B - 1 and not last_head(h)
        if fresh:
            split_w(h, 0, n1)
        if mid:
            mid()
        if n1:
            exps(u, bu)
        if fresh:
            split_w(h, 1, n1)
            if not n1:
                split_vw(h, False)
            split_wo(h, odd, n1)
        hook(b, OPEN)
        if new:
            act.wait_ge(a.proj_done, proj * s + 1)
            if mla:
                nc.scalar.activation(m.qf[0:HALF, :], m.bank[3][0:HALF, :], ACT.Copy).then_inc(a.nope_out, 1)
                if ahead:
                    split_w(h + 1, 0, True)
            else:
                nc.scalar.activation(m.q[HI][:, :], m.bank[3][:, :], ACT.Copy).then_inc(a.q_hi, 1)
        hook(b, 0)
        if n1:
            probs_hi(u)
        if new:
            act.wait_ge(a.proj_done, proj * s + 2)
            if mla:
                nc.scalar.activation(m.xT[HI][0:HALF, b, KQ, :], m.bank[4][0:HALF, :], ACT.Copy).then_inc(a.k_hi, 1)
                if b == 0:
                    act.wait_ge(a.combined, h + 1)
                    if n1:
                        act.wait_ge(a.y_done, 16 * h - 8)
                    else:
                        free(1)
                act.wait_ge(a.nope_out, s + 1)
                act.wait_ge(a.rope_added, s + 1)
                nc.scalar.activation(m.q[HI][:, :], m.qf[:, :], ACT.Copy).then_inc(a.q_hi, 1)
                if b == 0:
                    nc.scalar.activation(m.wo[HI][:, one(h % 2), :], m.bank[3][:, :].rearrange("p (a n) -> p a n", a=1),
                                         ACT.Copy).then_inc(a.wo_hi, 1)
                if ahead:
                    split_w(h + 1, 1, True)
                    split_w(h + 1, 2, True)
            else:
                nc.scalar.activation(m.k[HI][:, :], m.bank[4][:, :], ACT.Copy).then_inc(a.k_hi, 1)
                if odd and b == 1 and not last_head(h):
                    split_vw(h + 1, True)
                hook(b, 1)
                hook(b, 2)
        if n1:
            act.wait_ge(a.av_done, u + 1)
            ge(act, a.y_done, 4 * u)
            nc.scalar.activation(m.o[HI][:, :], m.bank[5][:, :], ACT.Copy).then_inc(a.o_hi, 1)
        if new and mla:
            nc.scalar.activation(m.v[HI][:, :], m.ctok[:, b, :], ACT.Copy).then_inc(a.v_hi, 1)
        if new and not mla and not odd:
            for half in range(2):
                act.wait_ge(a.v_done, 4 * h + 2 * b + half + 1)
                for other in range(2):
                    nc.scalar.activation(values_part(values_of(m, other, b)[HI], half), values_bank(m, half, other),
                                         ACT.Copy).then_inc(a.v_hi, 1)
        hook(b, 3)

    def steps(h, odd):
        begins = isinstance(h, int) and h == 0
        for b in range(B):
            step(h, odd, b, b >= 1 or not begins, hook=first if begins else nothing,
                 mid=(lambda: mid(0)) if last_head(h) and b == B - 1 else None)

    over_heads(act, mla, steps)
    after(0)
    step(H, 0, 0, True, new=False, mid=lambda: mid(1))
    after(1)


def attend_vector(nc, dve, m, a, mla, first=nothing, mid=nothing, after=nothing):
    proj = a.projections

    def mask_and_max(u, b):
        for t in range(NT):
            out, _ = scores_of(m, t)
            n = (t + 1) * P
            nc.vector.tensor_tensor_reduce(
                out=m.s[:, S_AT[t]:S_AT[t] + n], in0=out[:, 0:n], in1=m.mask[:, S - n:S], scale=-SCALE,
                scalar=FLT_MAX, op0=ALU.add, op1=ALU.min, accum_out=m.top[:, b, t:t + 1]).then_inc(a.masked, 1)

    def add_output(v, b, tiles):
        for t in tiles:
            dve.wait_ge(a.y_done, NT * v + t + 1)
            xt = m.x[:, b * NT + t, :]
            nc.vector.scalar_tensor_tensor(out=xt, in0=m.bank[6 + t % 2][:, :], scalar=m.inv[:, b, t:t + 1],
                                           in1=xt, op0=ALU.mult, op1=ALU.add).then_inc(a.y_added, 1)

    def probs_lo(u):
        for g, (dst, n, src) in enumerate(((0, 512, 0), (512, 384, 1), (1024, 384, 2))):
            dve.wait_ge(a.pt_hi, 3 * u + g + 1)
            nc.vector.tensor_tensor(m.pt_lo[:, dst:dst + n], m.bank[src][:, 0:n],
                                    m.pt_hi[:, dst:dst + n].bitcast(F32), ALU.subtract).then_inc(a.pt_lo, 1)

    def rest(out, bank, hi, done):
        return nc.vector.tensor_tensor(out, bank, hi.bitcast(F32), ALU.subtract).then_inc(done, 1)

    def step(h, odd, b, n1, n2, new=True, mid=None, hook=nothing):
        s = 4 * h + b
        u, v, bu, bv = s - 1, s - 2, (b - 1) % B, (b - 2) % B
        if mid:
            dve.wait_ge(a.y_added, NT * (s - 2))
            mid()
        if n1:
            dve.wait_ge(a.scores_done, NT * (u + 1))
        if n2:
            nc.vector.reciprocal(m.inv[:, bv, :], m.rowsum[:, bv, :]).then_inc(a.inverted, 1)
        if n1:
            mask_and_max(u, bu)
        if new and mla:
            dve.wait_ge(a.proj_done, proj * s + 1)
            ge(dve, a.rope_added, s)
            rotate(nc, m, m.bank[3]).then_inc(a.rope_out, 1)
        if n2:
            dve.wait_ge(a.inverted, v + 1)
            add_output(v, bv, (0, 1))
        hook(b, OPEN)
        if new and not mla:
            dve.wait_ge(a.q_hi, s + 1)
            rest(m.q[LO][:, :], m.bank[3][:, :], m.q[HI][:, :], a.q_lo)
        hook(b, 0)
        if n1:
            probs_lo(u)
        if new:
            dve.wait_ge(a.k_hi, s + 1)
            if mla:
                rest(m.xT[LO][0:HALF, b, KQ, :], m.bank[4][0:HALF, :], m.xT[HI][0:HALF, b, KQ, :], a.k_lo)
                if b == 0:
                    dve.wait_ge(a.wo_hi, h + 1)
                    flat = m.bank[3][:, :].rearrange("p (a n) -> p a n", a=1)
                    rest(m.wo[LO][:, one(h % 2), :], flat, m.wo[HI][:, one(h % 2), :], a.wo_lo)
            else:
                rest(m.k[LO][:, :], m.bank[4][:, :], m.k[HI][:, :], a.k_lo)
            hook(b, 1)
            hook(b, 2)
        if n2:
            add_output(v, bv, (2, 3))
        if n1:
            dve.wait_ge(a.o_hi, u + 1)
            rest(m.o[LO][:, :], m.bank[5][:, :], m.o[HI][:, :], a.o_lo)
        if new and not mla and not odd:
            for half in range(2):
                dve.wait_ge(a.v_hi, pair_values(h, odd, b) - 2 + 2 * half)
                for other in range(2):
                    hi, lo = (values_part(part, half) for part in values_of(m, other, b))
                    rest(lo, values_bank(m, half, other), hi, a.v_lo)
        hook(b, 3)

    def steps(h, odd):
        begins = isinstance(h, int) and h == 0
        for b in range(B):
            step(h, odd, b, b >= 1 or not begins, b >= 2 or not begins, hook=first if begins else nothing,
                 mid=(lambda: mid(0)) if last_head(h) and b == B - 1 else None)

    over_heads(dve, mla, steps)
    after(0)
    step(H, 0, 0, True, True, new=False, mid=lambda: mid(1))
    after(1)
    step(H, 0, 1, False, True, new=False)


def weight_parts(mla):
    if mla:
        return ((0, 384), (0, 384)), ((384, 576), (512, 704)), ((0, 512), (1024, 1536))
    return tuple(((512 * i, 512 * i + 512),) * 2 for i in range(2))


def rest_weights(nc, pool, m, a, mla, h, part):
    pool.wait_ge(a.w_hi, a.parts * h + part + 1)
    src, dst = weight_parts(mla)[part]
    at = slice(dst[0], dst[1])
    raw = m.wo_raw if mla and part == 2 else m.w_raw
    nc.gpsimd.tensor_tensor(m.w[LO][:, at], raw[:, src[0]:src[1]], m.w[HI][:, at].bitcast(F32),
                            ALU.subtract).then_inc(a.w_lo, 1)


def attend_gpsimd(nc, pool, m, a, mla):
    def rest_w(h, part):
        rest_weights(nc, pool, m, a, mla, h, part)

    def rest_vw(h):
        for part in range(2):
            pool.wait_ge(a.vw_hi, h + part + 1)
            hi, lo = value_weights(m, part)
            nc.gpsimd.tensor_tensor(lo, m.vw_raw[:, part, :], hi.bitcast(F32), ALU.subtract).then_inc(a.vw_lo, 1)

    def rest_wo(h, odd):
        pool.wait_ge(a.wo_hi, h + 1)
        at = one(odd)
        nc.gpsimd.tensor_tensor(m.wo[LO][:, at, :], m.wo_raw[:, 0:D].rearrange("p (a n) -> p a n", a=1),
                                m.wo[HI][:, at, :].bitcast(F32), ALU.subtract).then_inc(a.wo_lo, 1)

    def head(h, odd):
        if not mla:
            for part in range(a.parts):
                rest_w(h, part)
            if isinstance(h, int) and h == 0:
                rest_vw(h)
            rest_wo(h, odd)
            if odd and not last_head(h):
                rest_vw(h + 1)
            return
        for b in range(B):
            s = 4 * h + b
            pool.wait_ge(a.rope_out, s + 1)
            ge(pool, a.q_lo, s)
            ge(pool, a.v_lo, s)
            if b == 0:
                pool.wait_ge(a.w_lo, 3 * (h + 1))
            nc.gpsimd.tensor_tensor(m.qf[HALF:P, :], m.ra[HALF:P, :], m.rb[HALF:P, :],
                                    ALU.add).then_inc(a.rope_added, 1)
            ahead = b == B - 1 and not last_head(h)
            if ahead:
                pool.wait_ge(a.rope_added, s + 1)
                rest_w(h + 1, 0)
            pool.wait_ge(a.q_hi, s + 1)
            nc.gpsimd.tensor_tensor(m.q[LO][:, :], m.qf[:, :], m.q[HI][:, :].bitcast(F32),
                                    ALU.subtract).then_inc(a.q_lo, 1)
            if ahead:
                rest_w(h + 1, 1)
                rest_w(h + 1, 2)
            pool.wait_ge(a.v_hi, s + 1)
            nc.gpsimd.tensor_tensor(m.v[LO][:, :], m.ctok[:, b, :], m.v[HI][:, :].bitcast(F32),
                                    ALU.subtract).then_inc(a.v_lo, 1)

    over_heads(pool, mla, head)


def load_head(sp, m, a, w_dram, wo_dram, h):
    sp.dma_start(m.w_raw[:, 0:w_dram.shape[2]], w_dram[one(h), :, :].rearrange("h p n -> p (h n)")).then_inc(a.w_loaded, 16)
    sp.dma_start(m.wo_raw[:, 0:D], wo_dram[one(h), :, :].rearrange("h p n -> p (h n)")).then_inc(a.wo_loaded, 16)


def load_values(sp, m, a, wv_dram, pair):
    sp.dma_start(m.vw_raw, wv_dram[one(pair), :, :].rearrange("h p (a n) -> p (h a) n", a=2)).then_inc(a.vw_loaded, 16)


def attend_sync(nc, sp, m, a, mla, w_dram, wo_dram, wv_dram=None):
    def head(h, odd):
        if not (isinstance(h, int) and h == 0):
            sp.wait_ge(a.w_lo, a.parts * h)
            if not mla:
                sp.wait_ge(a.wo_lo, h)
            load_head(sp, m, a, w_dram, wo_dram, h)

    if mla:
        over_heads(sp, mla, head)
        return
    head(1, 1)
    with sp.Fori(1, H // 2) as pair:
        sp.wait_ge(a.vw_lo, 2 * pair)
        load_values(sp, m, a, wv_dram, pair)
        head(2 * pair, 0)
        head(2 * pair + 1, 1)


def last_head(h):
    return isinstance(h, int) and h == H - 1


def one(i):
    return slice(i, i + 1) if isinstance(i, int) else bass.ds(i, 1)


def ge(eng, sem, value):
    if not isinstance(value, int) or value > 0:
        eng.wait_ge(sem, value)


def rotate(nc, m, bank):
    e, o = HALF, HALF + QUARTER
    nc.vector.tensor_tensor(m.ra[e:P, :], bank[e:P, :], m.rope[e:P, 0, :], ALU.mult)
    nc.vector.tensor_tensor(m.rb[e:o, :], bank[o:P, :], m.rope[o:P, 1, :], ALU.mult)
    return nc.vector.tensor_tensor(m.rb[o:P, :], bank[e:o, :], m.rope[e:o, 1, :], ALU.mult)



LATENT_BANK = [0, 1, 2, 5, 6]


def latent_tensor(nc, pe, m, l, f, input_ready, first):
    for b in range(B):
        input_ready(b)
        for c in range(KQ + 2):
            if b == 0 and c == 0:
                pe.wait_ge(l.w_lo, 1)
            if b == 0 and c == KQ - 1:
                pe.wait_ge(f.y_added, NT * B * NE)
            if b == 0 and c == KQ:
                pe.wait_ge(l.w_lo, 2)
            if b:
                if c <= KQ:
                    pe.wait_ge(l.lo, (KQ + 1) * (b - 1) + c + 1)
                else:
                    pe.wait_ge(l.rope_out, b)
            for k in range(KD):
                at = slice(k * 384 + c * P, k * 384 + c * P + P) if c < KQ else \
                    slice(k * 192 + HALF * (c - KQ), k * 192 + HALF * (c - KQ) + P)
                w = m.w if c < KQ else m.wo1
                last = product(nc, m.bank[LATENT_BANK[c]][:, :], w[HI][:, at], w[LO][:, at],
                               m.xT[HI][:, b, k, :], m.xT[LO][:, b, k, :], k == 0, k == KD - 1)
            last.then_inc(l.done, 1)
            if 0 < c <= KQ:
                first(b, c - 1)
        pe.wait_ge(l.ckv_out, b + 1)
        ge(pe, l.tok_out, b)
        for t in range(NT):
            last = nc.tensor.transpose(m.bank[7][:, t * P:t * P + P], m.ckv32[:, t * P:t * P + P], m.ident[:, :])
        last.then_inc(l.tok_done, 1)
        first(b, NT - 1)


def latent_scalar(nc, act, m, l, f, first, then):
    act.wait_ge(l.w_loaded, 16)
    act.wait_ge(f.up_done, KH * B * NE)
    nc.scalar.activation(m.w[HI][:, :], m.w_raw[:, :], ACT.Copy).then_inc(l.w_hi, 1)
    act.wait_ge(l.wkva_loaded, 16)
    act.wait_ge(f.y_done, NT * B * NE)
    nc.scalar.activation(m.wo1[HI][:, 0:768], m.wo_raw[:, 0:768], ACT.Copy).then_inc(l.w_hi, 1)
    for b in range(B):
        for i in range(OPEN, NT - 1):
            first(b, i)
        act.wait_ge(l.done, (KQ + 2) * b + KQ + 1)
        nc.scalar.activation(m.ckv32[:, :], m.bank[5][:, :], ACT.Copy).then_inc(l.ckv_out, 1)
        act.wait_ge(l.done, (KQ + 2) * (b + 1))
        if b == B - 1:
            then()
        for c in range(KQ + 1):
            out = m.xT[HI][:, b, c, :] if c < KQ else m.ckv[HI][:, b, :]
            nc.scalar.activation(out, m.bank[LATENT_BANK[c]][:, :], ACT.Copy).then_inc(l.hi, 1)
        act.wait_ge(l.tok_done, b + 1)
        nc.scalar.activation(m.ctok[:, b, :], m.bank[7][:, :], ACT.Copy).then_inc(l.tok_out, 1)
        act.wait_ge(l.rope_added, b + 1)
        nc.scalar.activation(m.xT[HI][HALF:P, b, KQ, :], m.qf[HALF:P, :], ACT.Copy).then_inc(l.rope_hi, 1)
        first(b, NT - 1)


def latent_vector(nc, dve, m, l, first):
    def rotary(b):
        dve.wait_ge(l.done, (KQ + 2) * (b + 1))
        ge(dve, l.rope_added, b)
        rotate(nc, m, m.bank[6]).then_inc(l.rope_out, 1)

    for b in range(B):
        for i in range(OPEN, NT - 1):
            first(b, i)
        if b == B - 1:
            rotary(b)
        for c in range(KQ + 1):
            dve.wait_ge(l.hi, (KQ + 1) * b + c + 1)
            lo, hi = (m.xT[LO][:, b, c, :], m.xT[HI][:, b, c, :]) if c < KQ else (m.ckv[LO][:, b, :], m.ckv[HI][:, b, :])
            nc.vector.tensor_tensor(lo, m.bank[LATENT_BANK[c]][:, :], hi.bitcast(F32), ALU.subtract).then_inc(l.lo, 1)
        if b < B - 1:
            rotary(b)
        first(b, NT - 1)


def latent_gpsimd(nc, pool, m, l, a, then):
    for p, (lo, hi, raw, n) in enumerate(((m.w[LO], m.w[HI], m.w_raw, 1536), (m.wo1[LO], m.wo1[HI], m.wo_raw, 768))):
        pool.wait_ge(l.w_hi, p + 1)
        nc.gpsimd.tensor_tensor(lo[:, 0:n], raw[:, 0:n], hi[:, 0:n].bitcast(F32), ALU.subtract).then_inc(l.w_lo, 1)
    for b in range(B):
        if b == B - 1:
            pool.wait_ge(l.rope_lo, b)
            then()
        pool.wait_ge(l.rope_out, b + 1)
        if b:
            pool.wait_ge(l.rope_lo, b)
        else:
            pool.wait_ge(l.w_lo, 2)
        if b == B - 1:
            pool.wait_ge(a.w_lo, 3)
        nc.gpsimd.tensor_tensor(m.qf[HALF:P, :], m.ra[HALF:P, :], m.rb[HALF:P, :], ALU.add).then_inc(l.rope_added, 1)
        pool.wait_ge(l.rope_hi, b + 1)
        nc.gpsimd.tensor_tensor(m.xT[LO][HALF:P, b, KQ, :], m.qf[HALF:P, :],
                                m.xT[HI][HALF:P, b, KQ, :].bitcast(F32), ALU.subtract).then_inc(l.rope_lo, 1)
    pool.wait_ge(l.rope_lo, B)



CHAIN = 23
GAP = 14
GROUP = 32
BIAS_ROWS = 3 * GROUP


def gate_vector(nc, dve, m, g, b):
    count = [CHAIN * b]

    def then(op):
        count[0] += 1
        op.then_inc(g.chain, 1)
        dve.wait_ge(g.chain, count[0])

    def wide(x):
        return x[:, :].rearrange("p (n a) -> p n a", a=1).to_broadcast([P, NT, E])

    def first_of_largest(top, pick):
        then(nc.vector.tensor_reduce(top[:, :], m.logits[:, :, :], axis=AX.X, op=ALU.max))
        then(nc.vector.tensor_tensor(pick[:, :, :], m.logits[:, :, :], wide(top), ALU.is_equal))
        then(nc.vector.tensor_tensor(pick[:, :, :], pick[:, :, :], m.ramp[:, :, :], ALU.mult))
        then(nc.vector.tensor_reduce(m.rank[:, :], pick[:, :, :], axis=AX.X, op=ALU.max))
        then(nc.vector.tensor_tensor(pick[:, :, :], pick[:, :, :], wide(m.rank), ALU.is_equal))

    dve.wait_ge(g.logits_done, b + 1)
    halves = m.bank[4][:, 0:NT * 2 * E].rearrange("p (n e) -> p n e", e=2 * E)
    then(nc.vector.tensor_copy(m.pick1[:, :, :], halves[:, :, 0:E]))
    then(nc.vector.tensor_tensor(m.logits[:, :, :], m.pick1[:, :, :], halves[:, :, E:2 * E], ALU.add))
    first_of_largest(m.top1, m.pick1)
    then(nc.vector.scalar_tensor_tensor(out=m.logits[:, :, :], in0=m.pick1[:, :, :], scalar=-FLT_MAX,
                                        in1=m.logits[:, :, :], op0=ALU.mult, op1=ALU.add))
    first_of_largest(m.top2, m.pick2)
    then(nc.vector.tensor_tensor(m.gap[:, :], m.top2[:, :], m.top1[:, :], ALU.subtract))
    dve.wait_ge(g.exp_done, b + 1)
    then(nc.vector.tensor_scalar_add(m.gap[:, :], m.gap_exp[:, :], 1.0))
    then(nc.vector.reciprocal(m.top1[:, :], m.gap[:, :]))
    then(nc.vector.tensor_tensor(m.top2[:, :], m.top1[:, :], m.gap_exp[:, :], ALU.mult))
    then(nc.vector.tensor_tensor(m.pick1[:, :, :], m.pick1[:, :, :], wide(m.top1), ALU.mult))
    then(nc.vector.tensor_tensor(m.pick2[:, :, :], m.pick2[:, :, :], wide(m.top2), ALU.mult))
    then(nc.vector.tensor_tensor(m.gates[:, b * NT:(b + 1) * NT, 2:NE], m.pick1[:, :, :], m.pick2[:, :, :], ALU.add))
    gates = m.gates[:, b * NT:(b + 1) * NT, 1:NE]
    hi, again, lo = (m.packed[:, :, i * GROUP:i * GROUP + E + 1] for i in range(3))
    ge(dve, g.gt_done, b)
    if b == 0:
        dve.wait_ge(m.packed_zeroed, 1)
    nc.vector.tensor_copy(again, gates).then_inc(g.chain, 1)
    count[0] += 1
    then(nc.vector.tensor_copy(hi, gates))
    then(nc.vector.tensor_tensor(lo, gates, hi.bitcast(F32), ALU.subtract))
    assert count[0] == CHAIN * (b + 1)



Y_BANK = [2, 5, 6, 7]
W1_PARTS = [slice(0, KD * HF // 2), slice(KD * HF // 2, KD * HF)]


def expert_tensor(nc, pe, m, f, g, input_ready, first=nothing, after=nothing):
    def up(s, e, b, hook=nothing):
        for j in range(KH):
            ge(pe, f.gelu_done, KH * s - KH + j + 1)
            for k in range(KD):
                if b == 0 and j == 0 and k % (KD // 2) == 0:
                    pe.wait_ge(f.w1_lo, 2 * e + 1 + k // (KD // 2))
                at = slice(k * HF + j * P, k * HF + j * P + P)
                last = product(nc, m.bank[j][:, :], m.w[HI][:, at], m.w[LO][:, at],
                               m.xT[HI][:, b, k, :], m.xT[LO][:, b, k, :], k == 0, k == KD - 1)
            last.then_inc(f.up_done, 1)
            hook(j)

    def down(u, half, hook=nothing, biases=None):
        pe.wait_ge(f.h_lo, KH * (u + 1))
        if biases is not None:
            pe.wait_ge(g.gt_out, biases + 1)
        for t in range(NT):
            ge(pe, f.y_added, NT * u - NT + t + 1)
            for k in range(KH):
                at = slice(t * P, t * P + P)
                last = product(nc, m.bank[Y_BANK[t]][:, :], m.hq[HI][:, half, k, at], m.hq[LO][:, half, k, at],
                               m.wo[HI][:, k, :], m.wo[LO][:, k, :], k == 0, k == KH - 1 and biases is None)
            if biases is not None:
                last = nc.tensor.matmul(m.bank[Y_BANK[t]][:, :], m.gt[:, t * P:t * P + P], m.b2[:, :],
                                        start=False, stop=True)
            last.then_inc(f.y_done, 1)
            hook(t)

    def logits(b):
        if b == 0:
            pe.wait_ge(m.gw_split, 2)
            pe.wait_ge(m.b2_split, 2)
        ge(pe, g.lt_out, b)
        for k in range(KD):
            for part in (HI, LO):
                last = nc.tensor.matmul(m.bank[3][0:2 * E, :], m.gw[:, k, :], m.xT[part][:, b, k, :],
                                        start=k == 0 and part == HI, stop=k == KD - 1 and part == LO)
        last.then_inc(g.lt_done, 1)

    def turn_logits(b):
        pe.wait_ge(g.lt_out, b + 1)
        ge(pe, g.gt_out, b)
        for t in range(NT):
            last = nc.tensor.transpose(m.bank[4][:, t * 2 * E:t * 2 * E + 2 * E], m.lt[:, t * P:t * P + P],
                                       m.ident[0:2 * E, 0:2 * E])
        last.then_inc(g.logits_done, 1)

    def turn_gates(b):
        pe.wait_ge(g.chain, CHAIN * (b + 1))
        for t in range(NT):
            last = nc.tensor.transpose(m.bank[4][0:BIAS_ROWS, t * P:t * P + P], m.packed[:, t, :].bitcast(F32),
                                       m.ident[:, :])
        last.then_inc(g.gt_done, 1)

    def step(e, b, biases=None):
        s = B * e + b
        up(s, e, b, hook=lambda j: turn_gates(biases) if biases is not None and j == 0 else None)
        if b == 1:
            pe.wait_ge(f.w2_lo, e + 1)
        down(s - 1, (b - 1) % 2, biases=biases)

    for b in range(B):
        input_ready(b)
        up(b, 0, b, hook=lambda j: first(b, j))
        if b:
            if b == 1:
                pe.wait_ge(f.w2_lo, 1)
            down(b - 1, (b - 1) % 2, hook=lambda t: first(b, 2 + t // 2) if t % 2 else None)
        else:
            first(b, 2)
            first(b, 3)
    for b in range(B):
        s = B + b
        logits(b)
        up(s, 1, b, hook=lambda j: turn_gates(b - 1) if b and j == 0 else None)
        turn_logits(b)
        if b == 1:
            pe.wait_ge(f.w2_lo, 2)
        down(s - 1, (b - 1) % 2, biases=b - 1 if b else None)
    for b in range(B):
        step(2, b, biases=None if b else B - 1)
    with pe.Fori(3, NE - 1) as e:
        for b in range(B):
            step(e, b)
    for b in range(B):
        step(NE - 1, b)
        if b >= 2:
            after(b - 2)
    down(B * NE - 1, 1)


def split_w1(nc, act, m, f, e):
    act.wait_ge(f.w1_loaded, 16 * e + 16)
    for at in W1_PARTS:
        nc.scalar.activation(m.w[HI][:, at], m.w_raw[:, at], ACT.Copy).then_inc(f.w1_hi, 1)
    nc.scalar.activation(m.bias[:, :], m.b1[:, one(e), :], ACT.Copy).then_inc(f.bias_set, 1)


def expert_scalar(nc, act, m, f, g, a, first=nothing, mid=nothing, after=nothing):
    def step(e, b, n1, logits=False, gates=None, hook=nothing):
        s = B * e + b
        hook(b, OPEN)
        if b == 0 and n1:
            act.wait_ge(f.up_done, KH * s)
            split_w1(nc, act, m, f, e)
        if logits:
            act.wait_ge(g.lt_done, b + 1)
            nc.scalar.activation(m.lt[:, :], m.bank[3][0:2 * E, :], ACT.Copy).then_inc(g.lt_out, 1)
        act.wait_ge(f.bias_set, e + 1)
        for j in range(KH):
            act.wait_ge(f.up_done, KH * s + j + 1)
            ge(act, f.h_lo, KH * s - KH + j + 1)
            nc.scalar.activation(m.hid[:, j, :], m.bank[j][:, :], ACT.Gelu,
                                 bias=m.bias[:, j:j + 1]).then_inc(f.gelu_done, 1)
            act.wait_ge(f.gelu_done, KH * s + j + 1)
            if j == 0 and not (isinstance(e, int) and s < 2):
                act.wait_ge(f.y_done, NT * (s - 1))
            nc.scalar.activation(m.hq[HI][:, b % 2, j, :], m.hid[:, j, :], ACT.Copy).then_inc(f.h_hi, 1)
            if j == 0 and gates is not None:
                act.wait_ge(g.gt_done, gates + 1)
                nc.scalar.activation(m.gt[:, :], m.bank[4][0:BIAS_ROWS, :], ACT.Copy).then_inc(g.gt_out, 1)
            hook(b, j)
        hook(b, 2)
        hook(b, 3)
        if b == 0:
            act.wait_ge(f.w2_loaded, 16 * e + 16)
            if n1:
                act.wait_ge(f.y_done, NT * s)
            else:
                act.wait_ge(a.y_done, NT * B * H)
            nc.scalar.activation(m.wo[HI][:, :, :], m.wo_raw[:, :].rearrange("p (k n) -> p k n", k=KH), ACT.Copy).then_inc(f.w2_hi, 1)
        if logits:
            act.wait_ge(g.chain, CHAIN * b + GAP)
            nc.scalar.activation(m.gap_exp[:, :], m.gap[:, :], ACT.Exp).then_inc(g.exp_done, 1)

    for b in range(B):
        step(0, b, False, hook=first)
    for b in range(B):
        step(1, b, True, logits=True, gates=b - 1 if b else None)
    for b in range(B):
        step(2, b, True, gates=None if b else B - 1)
    with act.Fori(3, NE - 1) as e:
        for b in range(B):
            step(e, b, True)
    for b in range(B):
        step(NE - 1, b, True, hook=lambda b, i: mid(b - 2) if b >= 2 and i == OPEN else None)
        if b >= 2:
            after(b - 2)


def expert_vector(nc, dve, m, f, g, first=nothing, mid=nothing, after=nothing):
    def add(u, b, e, tiles=range(NT)):
        for t in tiles:
            dve.wait_ge(f.y_done, NT * u + t + 1)
            xt = m.x[:, b * NT + t, :]
            nc.vector.scalar_tensor_tensor(out=xt, in0=m.bank[Y_BANK[t]][:, :], scalar=m.gates[:, b * NT + t, one(e)],
                                           in1=xt, op0=ALU.mult, op1=ALU.add).then_inc(f.y_added, 1)

    def step(e, b, n1, gates=False, hook=nothing):
        s = B * e + b
        hook(b, OPEN)
        for j in range(KH):
            dve.wait_ge(f.h_hi, KH * s + j + 1)
            nc.vector.tensor_tensor(m.hq[LO][:, b % 2, j, :], m.hid[:, j, :], m.hq[HI][:, b % 2, j, :].bitcast(F32),
                                    ALU.subtract).then_inc(f.h_lo, 1)
            hook(b, j)
        if gates:
            gate_vector(nc, dve, m, g, b)
        if n1:
            add(s - 1, (b - 1) % B, e if b else e - 1, (0, 1))
        hook(b, 2)
        if n1:
            add(s - 1, (b - 1) % B, e if b else e - 1, (2, 3))
        hook(b, 3)

    for b in range(B):
        step(0, b, b >= 1, hook=first)
    for b in range(B):
        step(1, b, True, gates=True)
    with dve.Fori(2, NE - 1) as e:
        for b in range(B):
            step(e, b, True)
    def last_hook(b, i):
        if b >= 2 and i == OPEN:
            dve.wait_ge(f.y_added, NT * (B * (NE - 1) + b - 1))
            mid(b - 2)

    for b in range(B):
        step(NE - 1, b, True, hook=last_hook)
        if b >= 2:
            after(b - 2)
    add(B * NE - 1, B - 1, NE - 1)


def expert_gpsimd(nc, pool, m, f):
    def expert(e):
        for part, at in enumerate(W1_PARTS):
            pool.wait_ge(f.w1_hi, 2 * e + part + 1)
            nc.gpsimd.tensor_tensor(m.w[LO][:, at], m.w_raw[:, at], m.w[HI][:, at].bitcast(F32),
                                    ALU.subtract).then_inc(f.w1_lo, 1)
        pool.wait_ge(f.w2_hi, e + 1)
        nc.gpsimd.tensor_tensor(m.wo[LO][:, :, :], m.wo_raw[:, :].rearrange("p (k n) -> p k n", k=KH),
                                m.wo[HI][:, :, :].bitcast(F32), ALU.subtract).then_inc(f.w2_lo, 1)

    expert(0)
    with pool.Fori(1, NE) as e:
        expert(e)


def expert_sync(nc, sp, m, f, a, w1, w2):
    def expert(e, first):
        if first:
            sp.wait_ge(a.w_lo, a.parts * H)
            sp.wait_ge(a.wo_lo, H)
        else:
            sp.wait_ge(f.w1_lo, 2 * e)
        sp.dma_start(m.w_raw[:, 0:KD * HF], w1[one(e), :, :].rearrange("e p n -> p (e n)")).then_inc(f.w1_loaded, 16)
        if not first:
            sp.wait_ge(f.w2_lo, e)
        sp.dma_start(m.wo_raw[:, :], w2[one(e), :, :].rearrange("e p n -> p (e n)")).then_inc(f.w2_loaded, 16)

    expert(0, True)
    with sp.Fori(1, NE) as e:
        expert(e, False)




class NormSems:
    def __init__(self, sem):
        self.stats_done = sem("stats_done")
        self.moments_done = sem("moments_done")
        self.var_done = sem("var_done")
        self.root_done = sem("root_done")
        self.newton = sem("newton")
        self.normed = sem("normed")
        self.turned = sem("turned")
        self.xt_hi = sem("xt_hi")
        self.xt_lo = sem("xt_lo")


class AttendSems:
    def __init__(self, sem, mla):
        self.w_loaded = sem("w_loaded")
        self.wo_loaded = sem("wo_loaded")
        self.w_hi = sem("w_hi")
        self.w_lo = sem("w_lo")
        self.wo_hi = sem("wo_hi")
        self.wo_lo = sem("wo_lo")
        self.proj_done = sem("proj_done")
        self.q_hi = sem("q_hi")
        self.q_lo = sem("q_lo")
        self.k_hi = sem("k_hi")
        self.k_lo = sem("k_lo")
        self.v_hi = sem("v_hi")
        self.v_lo = sem("v_lo")
        self.scores_done = sem("scores_done")
        self.masked = sem("masked")
        self.probs_ready = sem("probs_ready")
        self.inverted = sem("inverted")
        self.pt_done = sem("pt_done")
        self.pt_hi = sem("pt_hi")
        self.pt_lo = sem("pt_lo")
        self.av_done = sem("av_done")
        self.o_hi = sem("o_hi")
        self.o_lo = sem("o_lo")
        self.y_done = sem("y_done")
        self.y_added = sem("y_added")
        self.projections = 2
        self.parts = 3 if mla else 2
        if mla:
            self.combined = sem("combined")
            self.nope_out = sem("nope_out")
            self.rope_out = sem("rope_out")
            self.rope_added = sem("rope_added")
        else:
            self.v_done = sem("v_done")
            self.vw_loaded = sem("vw_loaded")
            self.vw_hi = sem("vw_hi")
            self.vw_lo = sem("vw_lo")


class LatentSems:
    def __init__(self, sem):
        self.w_loaded = sem("w_loaded")
        self.w_hi = sem("w_hi")
        self.w_lo = sem("w_lo")
        self.done = sem("done")
        self.hi = sem("hi")
        self.lo = sem("lo")
        self.wkva_loaded = sem("wkva_loaded")
        self.ckv_out = sem("ckv_out")
        self.tok_done = sem("tok_done")
        self.tok_out = sem("tok_out")
        self.rope_out = sem("rope_out")
        self.rope_added = sem("rope_added")
        self.rope_hi = sem("rope_hi")
        self.rope_lo = sem("rope_lo")


class GateSems:
    def __init__(self, sem):
        self.lt_done = sem("lt_done")
        self.lt_out = sem("lt_out")
        self.logits_done = sem("logits_done")
        self.chain = sem("chain")
        self.exp_done = sem("exp_done")
        self.gt_done = sem("gt_done")
        self.gt_out = sem("gt_out")


class ExpertSems:
    def __init__(self, sem):
        self.w1_loaded = sem("w1_loaded")
        self.w2_loaded = sem("w2_loaded")
        self.w1_hi = sem("w1_hi")
        self.w1_lo = sem("w1_lo")
        self.w2_hi = sem("w2_hi")
        self.w2_lo = sem("w2_lo")
        self.bias_set = sem("bias_set")
        self.up_done = sem("up_done")
        self.gelu_done = sem("gelu_done")
        self.h_hi = sem("h_hi")
        self.h_lo = sem("h_lo")
        self.y_done = sem("y_done")
        self.y_added = sem("y_added")


class Buffers:
    pass


def program(nc, x_in, wa, wva, woa, wqa, wkva, wb, wob, rope, gate, w1, b1, w2, b2, out):
    with ExitStack() as ctx:
        def sb(name, shape, dt=F32):
            return ctx.enter_context(nc.sbuf_tensor(name, shape, dt))

        def pair(name, shape):
            return [sb(name + "_hi", shape, F32R), sb(name + "_lo", shape, F32R)]

        def named(prefix):
            return lambda name: ctx.enter_context(nc.semaphore(f"{prefix}_{name}"))

        m = Buffers()
        m.x = sb("x", [P, B * NT, D])
        m.xT = pair("xT", [P, B, KD, S])
        m.ident = sb("ident", [P, P])
        m.mask = sb("mask", [P, S])
        m.w_raw = sb("w_raw", [P, 1536])
        m.w = pair("w", [P, 1536])
        m.wo_raw = sb("wo_raw", [P, 2 * D])
        m.wo = pair("wo", [P, 2, D])
        m.wo1 = [w[:, :, :].rearrange("p a n -> p (a n)") for w in m.wo]
        m.hq = pair("hq", [P, 2, KH, S])
        m.q = [t[:, 0, 0, :] for t in m.hq]
        m.k = [t[:, 0, 1, :] for t in m.hq]
        m.v = [t[:, 1, 0, :] for t in m.hq]
        m.o = [t[:, 1, 1, :] for t in m.hq]
        m.s = sb("s", [P, S_COLS])
        m.hid = m.s[:, 0:KH * S].rearrange("p (k n) -> p k n", k=KH)
        m.xn = sb("xn", [P, 2, D])
        m.pt_hi = sb("pt_hi", [P, PT_COLS], F32R)
        m.pt_lo = sb("pt_lo", [P, PT_COLS], F32R)
        m.top = sb("top", [P, B, NT])
        m.rowsum = sb("rowsum", [P, B, NT])
        m.inv = sb("inv", [P, B, NT])
        m.stats = sb("stats", [P, B, NT, 6])
        m.moments = sb("moments", [P, B, NT, 2])
        m.var, m.root, m.rstd0, m.rstd = (sb(n, [P, B, NT]) for n in ("var", "root", "rstd0", "rstd"))
        m.newt = sb("newt", [P, B, 3, NT])
        m.ckv = pair("ckv", [P, B, S])
        m.ckv32 = m.s[:, 0:S]
        m.ctok = sb("ctok", [P, B, S])
        m.rope = sb("rope", [P, 2, S])
        m.qf, m.ra, m.rb = (sb(n, [P, S]) for n in ("qf", "ra", "rb"))
        m.gw_raw = sb("gw_raw", [P, KD, E])
        m.gw = sb("gw", [P, KD, 2 * E], F32R)
        m.b1 = sb("b1", [P, NE, KH])
        m.bias = sb("bias", [P, KH])
        m.b2 = sb("b2", [BIAS_ROWS, D], F32R)
        m.vw_raw = m.ctok[:, 2:4, :]
        m.vw2 = pair("vw2", [P, D])
        m.b2_raw = m.ctok[0:BIAS_ROWS, 0, :]
        m.lt = m.ctok[0:2 * E, 1, :]
        m.gt = m.pt_hi[0:BIAS_ROWS, 0:S]
        m.packed = m.vw2[HI][:, 0:NT * BIAS_ROWS].rearrange("p (t n) -> p t n", t=NT)
        m.gates = sb("gates", [P, B * NT, NE])
        m.ramp, m.logits, m.pick1, m.pick2 = (sb(n, [P, NT, E]) for n in ("ramp", "logits", "pick1", "pick2"))
        m.top1, m.top2, m.rank, m.gap, m.gap_exp = (sb(n, [P, NT]) for n in ("top1", "top2", "rank", "gap", "gap_exp"))
        m.bank = [ctx.enter_context(nc.psum_tensor(f"bank{i}", [P, 512], F32)) for i in range(8)]

        m.const_set = ctx.enter_context(nc.semaphore("const_set"))
        x_loaded = [ctx.enter_context(nc.semaphore(f"x_loaded{b}")) for b in range(B)]
        x0_loaded = [ctx.enter_context(nc.semaphore(f"x0_loaded{t}")) for t in range(NT)]
        small_loaded, m.packed_zeroed, m.gw_split, m.b2_split, stored = (
            ctx.enter_context(nc.semaphore(n)) for n in ("small_loaded", "packed_zeroed", "gw_split", "b2_split", "stored"))
        SMALL = 16 * 5
        n = NormSems(named("norm"))
        a1, a2 = AttendSems(named("attn"), False), AttendSems(named("mla"), True)
        lat = LatentSems(named("latent"))
        g = [GateSems(named(f"gate{i}")) for i in range(2)]
        f = [ExpertSems(named(f"expert{i}")) for i in range(2)]
        A_END, F_END = NT * B * H, NT * B * NE

        block = ctx.enter_context(nc.Block())

        @block.sync
        def _(sp):
            def load_x(b):
                sp.dma_start(m.x[:, b * NT:(b + 1) * NT, :],
                             x_in[b, :, :].rearrange("(t p) d -> p t d", p=P)).then_inc(x_loaded[b], 16)

            for t in range(NT):
                sp.dma_start(m.x[:, t, :], x_in[0, t * P:(t + 1) * P, :]).then_inc(x0_loaded[t], 16)
            load_head(sp, m, a1, wa, woa, 0)
            load_values(sp, m, a1, wva, 0)
            for b in range(1, B):
                load_x(b)
            sp.dma_start(m.gw_raw[:, :, :], gate).then_inc(small_loaded, 16)
            sp.dma_start(m.b1[:, :, :], b1).then_inc(small_loaded, 16)
            sp.dma_start(m.b2_raw, b2).then_inc(small_loaded, 16)
            sp.dma_start(m.rope[HALF:P, 0, :], rope[0, :, :]).then_inc(small_loaded, 16)
            sp.dma_start(m.rope[HALF:P, 1, :], rope[1, :, :]).then_inc(small_loaded, 16)
            attend_sync(nc, sp, m, a1, False, wa, woa, wva)
            expert_sync(nc, sp, m, f[0], a1, w1, w2)
            sp.wait_ge(f[0].w1_lo, 2 * NE)
            sp.dma_start(m.w_raw[:, :], wqa).then_inc(lat.w_loaded, 16)
            sp.wait_ge(f[0].w2_lo, NE)
            sp.dma_start(m.wo_raw[:, 0:768], wkva).then_inc(lat.wkva_loaded, 16)
            sp.wait_ge(lat.w_lo, 2)
            load_head(sp, m, a2, wb, wob, 0)
            attend_sync(nc, sp, m, a2, True, wb, wob)
            expert_sync(nc, sp, m, f[1], a2, w1, w2)
            for b in range(B - 1):
                sp.wait_ge(f[1].y_added, F_END - NT * (B - 1 - b))
                sp.dma_start(out[b, :, :].rearrange("(t p) d -> p t d", p=P),
                             m.x[:, b * NT:(b + 1) * NT, :]).then_inc(stored, 16)
            for t in range(NT):
                sp.wait_ge(f[1].y_added, F_END - NT + t + 1)
                sp.dma_start(out[B - 1, t * P:(t + 1) * P, :], m.x[:, (B - 1) * NT + t, :]).then_inc(stored, 16)
            sp.wait_ge(stored, 16 * (B - 1 + NT))

        @block.gpsimd
        def _(pool):
            constants(nc, pool, m)
            attend_gpsimd(nc, pool, m, a1, False)
            pool.wait_ge(a1.v_done, B * H)
            nc.gpsimd.memset(m.packed.bitcast(F32), 0.0).then_inc(m.packed_zeroed, 1)
            pool.wait_ge(m.gw_split, 1)
            nc.gpsimd.tensor_tensor(m.gw[:, :, E:2 * E], m.gw_raw[:, :, :], m.gw[:, :, 0:E].bitcast(F32),
                                    ALU.subtract).then_inc(m.gw_split, 1)
            expert_gpsimd(nc, pool, m, f[0])
            latent_gpsimd(nc, pool, m, lat, a2, lambda: [rest_weights(nc, pool, m, a2, True, 0, part) for part in range(3)])
            attend_gpsimd(nc, pool, m, a2, True)
            pool.wait_ge(a2.q_lo, B * H)
            expert_gpsimd(nc, pool, m, f[1])


        places = {(1, i): (0, i) for i in range(NT)}
        places.update({(2, t): (1, t // 2) for t in range(NT)})
        places.update({(3, t): (1, 2 + t // 2) for t in range(NT)})
        later = dict(zip([(2, t) for t in range(NT)] + [(3, t) for t in range(NT)],
                         [(0, 3), (1, 0), (1, 1), (1, 2), (1, 3), (2, 0), (2, 1), (2, 2)]))

        def woven(r, stats, start, tile):
            def first(b, i):
                if r == 0:
                    if b == 0 and i == OPEN:
                        stats(1)
                        start(1)
                elif i == OPEN and b < 2:
                    stats(b + 2)
                    if b == 0:
                        start(2)
                for (batch, t), place in (later if r else places).items():
                    if place == (b, i):
                        tile(batch, t)
                        if t == NT - 1 and (batch == 2 or r == 0 and batch == 1):
                            start(batch + 1)
                if r == 0 and (b, i) in ((0, 2), (1, OPEN)):
                    stats(b + 2)
            return first

        @block.scalar
        def _(act):
            def root(r):
                return lambda b: norm_root_scalar(nc, act, m, n, r, b)

            def tile(r):
                return lambda b, t: norm_tile_scalar(nc, act, m, n, r, b, t)

            def tiles(r):
                return lambda b: [tile(r)(b, t) for t in range(NT)]

            def behind_attention(r, a, e):
                def after(i):
                    if i == 0:
                        act.wait_ge(a.proj_done, a.projections * B * H)
                        split_w1(nc, act, m, e, 0)
                    tiles(r)(i)
                return after

            root(0)(0)
            tiles(0)(0)
            attend_scalar(nc, act, m, a1, False, nothing, woven(0, root(0), nothing, tile(0)), root(1), behind_attention(1, a1, f[0]))
            act.wait_ge(small_loaded, SMALL)
            nc.scalar.activation(m.gw[:, :, 0:E], m.gw_raw[:, :, :], ACT.Copy).then_inc(m.gw_split, 1)
            nc.scalar.activation(m.b2[:, :], m.b2_raw, ACT.Copy).then_inc(m.b2_split, 1)
            expert_scalar(nc, act, m, f[0], g[0], a1, woven(1, root(1), nothing, tile(1)), root(2), tiles(2))
            latent_scalar(nc, act, m, lat, f[0], woven(2, root(2), nothing, tile(2)),
                          lambda: [split_weights(nc, act, m, a2, True, 0, part, False) for part in range(3)])
            attend_scalar(nc, act, m, a2, True, lambda i: act.wait_ge(lat.done, (KQ + 2) * B), nothing, root(3),
                          behind_attention(3, a2, f[1]))
            expert_scalar(nc, act, m, f[1], g[1], a2, woven(3, root(3), nothing, tile(3)))

        @block.vector
        def _(dve):
            def stats(r):
                def measured(b):
                    if r == 0 and b:
                        dve.wait_ge(x_loaded[b], 16)
                    norm_stats_vector(nc, dve, m, n, r, b, x0_loaded if r == b == 0 else None)
                return measured

            def start(r):
                return lambda b: norm_start_vector(nc, dve, m, n, r, b)

            def both(r):
                def begun(b):
                    stats(r)(b)
                    start(r)(b)
                return begun

            def tile(r):
                return lambda b, t: norm_tile_vector(nc, dve, m, n, r, b, t)

            def tiles(r):
                def after(b):
                    for t in range(NT):
                        tile(r)(b, t)
                return after

            both(0)(0)
            tiles(0)(0)
            dve.wait_ge(m.const_set, CONSTS)
            attend_vector(nc, dve, m, a1, False, woven(0, stats(0), start(0), tile(0)), both(1), tiles(1))
            dve.wait_ge(m.b2_split, 1)
            second = slice(GROUP, GROUP + E + 1)
            nc.vector.tensor_tensor(m.b2[second, :], m.b2_raw[second, :], m.b2[second, :].bitcast(F32),
                                    ALU.subtract).then_inc(m.b2_split, 1)
            expert_vector(nc, dve, m, f[0], g[0], woven(1, stats(1), start(1), tile(1)), both(2), tiles(2))
            latent_vector(nc, dve, m, lat, woven(2, stats(2), start(2), tile(2)))
            dve.wait_ge(small_loaded, SMALL)
            dve.wait_ge(lat.rope_added, B)
            attend_vector(nc, dve, m, a2, True, nothing, both(3), tiles(3))
            expert_vector(nc, dve, m, f[1], g[1], woven(3, stats(3), start(3), tile(3)))

        @block.tensor
        def _(pe):
            def tile(r):
                return lambda b, t: norm_tile_tensor(nc, pe, m, n, r, b, t)

            def ready(r):
                return lambda b: pe.wait_ge(n.xt_lo, NT * (B * r + b + 1))

            def ready_and_banks(b):
                ready(0)(b if b < 2 else B - 1)

            def behind(r, bank_free):
                def after(i):
                    if i == 0:
                        bank_free()
                    for t in range(NT):
                        tile(r)(i, t)
                return after

            def latents_ready(b):
                last = b if b == 0 else B - 1
                pe.wait_ge(lat.lo, (KQ + 1) * (last + 1))
                pe.wait_ge(lat.rope_lo, last + 1)

            def a1_banks():
                pe.wait_ge(a1.q_lo, B * H)
                pe.wait_ge(a1.k_lo, B * H)

            def a2_banks():
                pe.wait_ge(a2.nope_out, B * H)
                pe.wait_ge(a2.rope_out, B * H)
                pe.wait_ge(a2.k_lo, B * H)

            pe.wait_ge(m.const_set, CONSTS)
            for t in range(NT):
                tile(0)(0, t)
            attend_tensor(nc, pe, m, a1, False, ready_and_banks, woven(0, nothing, nothing, tile(0)), behind(1, a1_banks))
            expert_tensor(nc, pe, m, f[0], g[0], ready(1), woven(1, nothing, nothing, tile(1)),
                          behind(2, lambda: pe.wait_ge(g[0].gt_out, B)))
            latent_tensor(nc, pe, m, lat, f[0], ready(2), woven(2, nothing, nothing, tile(2)))
            attend_tensor(nc, pe, m, a2, True, latents_ready, nothing, behind(3, a2_banks))
            expert_tensor(nc, pe, m, f[1], g[1], ready(3), woven(3, nothing, nothing, tile(3)))


def kernel(**inputs):
    import concourse.bacc as bacc
    from concourse.bass_utils import run_bass_kernel_spmd

    def arr(name):
        return np.asarray(inputs[name])

    def tiles(w, cols):
        return w.reshape(-1, P, cols).transpose(1, 0, 2)

    c = np.ascontiguousarray
    w_in = arr("L0_attn_a_w_in").reshape(H, 3, DH, KD, P)
    wqk = w_in[:, 0:2].transpose(0, 4, 1, 3, 2).reshape(H, P, 2 * KD * DH)
    wv = w_in[:, 2].reshape(H // 2, 2, DH, KD, P).transpose(0, 4, 3, 1, 2).reshape(H // 2, P, 2 * KD * DH)
    wo_a = arr("L0_attn_a_w_out").T.reshape(H, DH, D)
    turned = np.concatenate([np.arange(0, HALF, 2), np.arange(1, HALF, 2)])
    order = np.concatenate([np.arange(HALF), HALF + turned])
    wqb = arr("L0_attn_b_Wqb").reshape(KQ, P, H, DH)[:, :, :, order].transpose(2, 1, 0, 3).reshape(H, P, KQ * DH)
    wkvb = arr("L0_attn_b_Wkvb").reshape(P, H, HALF + DH)
    wb = np.concatenate([wqb, wkvb[:, :, :HALF].transpose(1, 0, 2), wkvb[:, :, HALF:].transpose(1, 2, 0)], axis=2)
    wkva = arr("L0_attn_b_Wkva")[:, np.concatenate([np.arange(P), P + turned])]
    wob = arr("L0_attn_b_Wo").reshape(H, DH, D)
    sw1, sb1, sw2 = arr("L0_ffn_shared_w1"), arr("L0_ffn_shared_b1"), arr("L0_ffn_shared_w2")
    w1 = np.concatenate([sw1.reshape(D, 2, HF).transpose(1, 0, 2), arr("L0_ffn_w1")])
    w1 = w1.reshape(NE, KD, P, HF).transpose(0, 2, 1, 3).reshape(NE, P, KD * HF)
    b1 = np.concatenate([sb1.reshape(2, HF), arr("L0_ffn_b1")]).reshape(NE, KH, P).transpose(2, 0, 1)
    w2 = np.concatenate([sw2.reshape(2, HF, D), arr("L0_ffn_w2")])
    w2 = w2.reshape(NE, KH, P, D).transpose(0, 2, 1, 3).reshape(NE, P, KH * D)
    b2 = np.concatenate([arr("L0_ffn_shared_b2")[None], arr("L0_ffn_b2")])
    b2 = np.tile(np.concatenate([b2, np.zeros((GROUP - E - 1, D), np.float32)]), (3, 1))
    inv_freq = (1.0 / np.float32(10000.0) ** (np.arange(QUARTER, dtype=np.float32) * np.float32(2.0 / HALF))).astype(np.float32)
    freqs = inv_freq[:, None] * np.arange(S, dtype=np.float32)[None, :]
    rope = np.stack([np.concatenate([np.cos(freqs), np.cos(freqs)]), np.concatenate([np.sin(freqs), -np.sin(freqs)])]).astype(np.float32)
    arrays = {
        "x_in": c(arr("L0_attn_a_x")), "wa": c(wqk), "wva": c(wv), "woa": c(wo_a),
        "wqa": c(tiles(arr("L0_attn_b_Wqa"), 384).reshape(P, -1)), "wkva": c(tiles(wkva, 192).reshape(P, -1)),
        "wb": c(wb), "wob": c(wob), "rope": c(rope), "gate": c(tiles(arr("L0_ffn_gate_w"), E)),
        "w1": c(w1), "b1": c(b1), "w2": c(w2), "b2": c(b2),
    }
    nc = bacc.Bacc("TRN2", target_bir_lowering=False, num_devices=1)
    args = [nc.dram_tensor("dram_" + k, v.shape, mybir.dt.from_np(v.dtype), kind="ExternalInput").ap() for k, v in arrays.items()]
    args.append(nc.dram_tensor("dram_out", (B, S, D), F32, kind="ExternalOutput").ap())
    program(nc, *args)
    r = run_bass_kernel_spmd(nc, [{"dram_" + k: v for k, v in arrays.items()}], core_ids=[0])
    return r.results[0]["dram_out"]
```
